# Optimizing a Trainium2 kernel written in Bass

```python
import numpy as np
import jax
import jax.numpy as jnp

def _softmax(x, axis=-1):
    return jax.nn.softmax(x, axis=axis)

def _gelu(x):
    return jax.nn.gelu(x, approximate=True)

def _silu(x):
    return jax.nn.silu(x)

def _sigmoid(x):
    return jax.nn.sigmoid(x)

def _layernorm(x, axis=-1, eps=1e-05):
    m = jnp.mean(x, axis=axis, keepdims=True)
    v = jnp.var(x, axis=axis, keepdims=True)
    return (x - m) / jnp.sqrt(v + eps)

def _scatter_add(tgt, idx, src, axis=0):
    return tgt.at[idx].add(src)

def _segment_sum(src, seg, n):
    return jax.ops.segment_sum(src, seg, n)
kernel_name = 'mk_xattn_ffn_d2_seqx_r4_321b9f'

def setup_inputs(seed: int=0):
    np.random.seed(seed)
    _w = jnp.asarray

    def _rec_inputs():
        import jax
        import jax.numpy as jnp
        _rk = jax.random.key(seed)
        x = 7.22e-05 + 1 * jax.random.normal(jax.random.fold_in(_rk, 1), (4, 512, 512), jnp.float32)
        _lenS = 512 - jax.random.randint(jax.random.fold_in(_rk, 7), (4,), 0, max(1, 512 // 4) + 1, jnp.int32)
        _lenS2 = 64 - jax.random.randint(jax.random.fold_in(_rk, 8), (4,), 0, max(1, 64 // 4) + 1, jnp.int32)
        _ctx_2048P = jax.random.normal(jax.random.fold_in(_rk, 11), (4, 16, 512), jnp.float32)
        _ctx_2048c = jax.random.dirichlet(jax.random.fold_in(_rk, 511), 0.3 * jnp.ones((16,), jnp.float32), (4, 64))
        _ctx_2048t = jnp.einsum('bsk,bkd->bsd', _ctx_2048c, _ctx_2048P)
        _ctx_2048t = _ctx_2048t * jax.lax.rsqrt(jnp.mean(jnp.square(_ctx_2048t)) + 1e-12) * 0.953939
        ctx_2048 = 4.13588e-05 + 0.999923 * (_ctx_2048t + 0.3 * jax.random.normal(jax.random.fold_in(_rk, 611), (4, 64, 512), jnp.float32))
        _validS = jnp.arange(512)[None, :] < _lenS[:, None]
        _validS2 = jnp.arange(64)[None, :] < _lenS2[:, None]
        _causal = jnp.tril(jnp.ones((512, 512), dtype=bool))
        mask_BxS2_bk0 = jnp.logical_not(jnp.broadcast_to(_validS2[:, :], (4, 64)))
        return (x, ctx_2048, mask_BxS2_bk0)
    x, ctx_2048, mask_BxS2_bk0 = _rec_inputs()

    def _L0_xattn_setup():
        import math
        import jax, jax.numpy as jnp
        import numpy as np
        HEADS = 16
        MASKED_BIAS = -10000.0

        def _mha(q, k, v):
            B, Sq, D = q.shape
            Sk = k.shape[-2]
            hd = D // HEADS
            qh = q.reshape(B, Sq, HEADS, hd).transpose(0, 2, 1, 3)
            kh = k.reshape(B, Sk, HEADS, hd).transpose(0, 2, 1, 3)
            vh = v.reshape(B, Sk, HEADS, hd).transpose(0, 2, 1, 3)
            scores = jnp.einsum('bhqd,bhkd->bhqk', qh, kh) / math.sqrt(hd)
            qi = jnp.arange(Sq)[:, None] + (Sk - Sq)
            ki = jnp.arange(Sk)[None, :]
            causal = ki <= qi
            scores = jnp.where(causal[None, None], scores, jnp.asarray(MASKED_BIAS, scores.dtype))
            attn = jax.nn.softmax(scores, axis=-1)
            out = jnp.einsum('bhqk,bhkd->bhqd', attn, vh)
            return out.transpose(0, 2, 1, 3).reshape(B, Sq, D)
        key = jax.random.key(seed)
        kq, kk, kv = jax.random.split(key, 3)
        B, S, D = (4, 256, 512)
        q = jax.random.normal(kq, (B, S, D), dtype=jnp.float32)
        k = jax.random.normal(kk, (B, S, D), dtype=jnp.float32)
        v = jax.random.normal(kv, (B, S, D), dtype=jnp.float32)
        return {'q': q, 'k': k, 'v': v}
    _L0_xattn_all = _L0_xattn_setup()
    _L0_xattn_in = {k: v for k, v in _L0_xattn_all.items() if k in ()}
    del _L0_xattn_all

    def _L0_ffn_setup():
        import jax, jax.numpy as jnp
        import numpy as np
        B, S, H = (4, 256, 512)
        NH = 16
        HD = H // NH
        RD = HD // 2
        LAT = H // 4
        I = 256
        NE = 8
        NSH = 1
        NR = NE - NSH
        TOPK = 2
        EPS = 1e-05
        SCALING = 8.0

        def _w(key, shape, fan_in):
            return jax.random.normal(key, shape, dtype=jnp.float32) / np.sqrt(fan_in)

        def rmsnorm(x, w):
            rms = jax.lax.rsqrt(jnp.mean(x * x, axis=-1, keepdims=True) + EPS)
            return w * rms * x

        def rope_cos_sin(seq_len):
            inv_freq = 1.0 / 10000.0 ** (jnp.arange(0, RD, 2, dtype=jnp.float32) / RD)
            t = jnp.arange(seq_len, dtype=jnp.float32)
            ang = jnp.outer(t, inv_freq)
            emb = jnp.concatenate([ang, ang], axis=-1)
            return (jnp.cos(emb), jnp.sin(emb))

        def apply_rope(x, cos, sin):
            c = cos[None, :, None, :]
            s = sin[None, :, None, :]
            x1, x2 = jnp.split(x, 2, axis=-1)
            rot = jnp.concatenate([-x2, x1], axis=-1)
            return x * c + rot * s

        def expert_ffn(x, wg, wu, wd):
            h = jax.nn.silu(x @ wg) * (x @ wu) / SCALING
            return h @ wd

        def attention(x, kv_d_w, q_d_w, k_u_w, v_u_w, q_u_w, rope_k_w, rope_q_w, o_w):
            b, s, _ = x.shape
            kv_d = x @ kv_d_w
            q_d = x @ q_d_w
            k_p = (kv_d @ k_u_w).reshape(b, s, NH, RD)
            q_p = (q_d @ q_u_w).reshape(b, s, NH, RD)
            v = (kv_d @ v_u_w).reshape(b, s, NH, HD)
            k_r = (x @ rope_k_w).reshape(b, s, NH, RD)
            q_r = (q_d @ rope_q_w).reshape(b, s, NH, RD)
            cos, sin = rope_cos_sin(s)
            k_r = apply_rope(k_r, cos, sin)
            q_r = apply_rope(q_r, cos, sin)
            k = jnp.concatenate([k_p, k_r], axis=-1)
            q = jnp.concatenate([q_p, q_r], axis=-1)
            scale = 1.0 / np.sqrt(HD)
            scores = jnp.einsum('bqhd,bkhd->bhqk', q, k) * scale
            causal = jnp.tril(jnp.ones((s, s), dtype=bool))
            scores = jnp.where(causal[None, None], scores, jnp.finfo(scores.dtype).min)
            probs = jax.nn.softmax(scores, axis=-1)
            out = jnp.einsum('bhqk,bkhd->bqhd', probs, v).reshape(b, s, H)
            return out @ o_w

        def moe(x, sh_gate, sh_up, sh_down, r_gate, r_up, r_down, router_w, router_b):
            shared = expert_ffn(x, sh_gate, sh_up, sh_down)
            logits = x @ router_w + router_b
            probs = jax.nn.sigmoid(logits)
            scores, idx = jax.lax.top_k(probs, TOPK)
            scores = scores / jnp.sum(scores, axis=-1, keepdims=True)
            w = jnp.sum(jax.nn.one_hot(idx, NR, dtype=x.dtype) * scores[..., None], axis=-2)
            combined = jnp.zeros_like(x)
            for e in range(NR):
                combined = combined + w[..., e:e + 1] * expert_ffn(x, r_gate[e], r_up[e], r_down[e])
            return shared + combined
        key = jax.random.key(seed)
        ks = jax.random.split(key, 24)
        return {'x': jax.random.normal(ks[0], (B, S, H), dtype=jnp.float32), 'ln1_w': jnp.ones((H,), jnp.float32), 'ln2_w': jnp.ones((H,), jnp.float32), 'kv_d_w': _w(ks[1], (H, LAT), H), 'q_d_w': _w(ks[2], (H, LAT), H), 'k_u_w': _w(ks[3], (LAT, H // 2), LAT), 'v_u_w': _w(ks[4], (LAT, H), LAT), 'q_u_w': _w(ks[5], (LAT, H // 2), LAT), 'rope_k_w': _w(ks[6], (H, H // 2), H), 'rope_q_w': _w(ks[7], (LAT, H // 2), LAT), 'o_w': _w(ks[8], (H, H), H), 'sh_gate': _w(ks[9], (H, I), H), 'sh_up': _w(ks[10], (H, I), H), 'sh_down': _w(ks[11], (I, H), I), 'r_gate': _w(ks[12], (NR, H, I), H), 'r_up': _w(ks[13], (NR, H, I), H), 'r_down': _w(ks[14], (NR, I, H), I), 'router_w': _w(ks[15], (H, NR), H), 'router_b': jnp.zeros((NR,), jnp.float32)}
    _L0_ffn_all = _L0_ffn_setup()
    _L0_ffn_in = {k: v for k, v in _L0_ffn_all.items() if k in ('ln1_w', 'ln2_w', 'kv_d_w', 'q_d_w', 'k_u_w', 'v_u_w', 'q_u_w', 'rope_k_w', 'rope_q_w', 'o_w', 'sh_gate', 'sh_up', 'sh_down', 'r_gate', 'r_up', 'r_down', 'router_w', 'router_b')}
    del _L0_ffn_all

    def _L1_xattn_setup():
        import jax, jax.numpy as jnp
        import numpy as np
        key = jax.random.key(seed)
        k1, k2, k3 = jax.random.split(key, 3)
        B, S, D, M = (8, 512, 512, 128)
        hidden_states = jax.random.normal(k1, (B, S, D), dtype=jnp.float32)
        memory_tokens = jax.random.normal(k2, (B, M, D), dtype=jnp.float32)
        memory_mask = jax.random.randint(k3, (B, M), 0, 2).astype(jnp.bool_)
        return {'hidden_states': hidden_states, 'memory_tokens': memory_tokens, 'memory_mask': memory_mask}
    _L1_xattn_all = _L1_xattn_setup()
    _L1_xattn_in = {k: v for k, v in _L1_xattn_all.items() if k in ()}
    del _L1_xattn_all

    def _L1_ffn_setup():
        import jax, jax.numpy as jnp
        import numpy as np
        B, S, H, E, K, I = (2, 256, 512, 32, 8, 192)
        key = jax.random.key(seed)
        ks = jax.random.split(key, 5)
        scaled = lambda k, shp, fan: jax.random.normal(k, shp, jnp.float32) * fan ** (-0.5)
        return {'hidden_states': jax.random.normal(ks[0], (B, S, H), jnp.float32), 'router_w': scaled(ks[1], (E, H), H), 'w_gate': scaled(ks[2], (E, H, I), H), 'w_up': scaled(ks[3], (E, H, I), H), 'w_down': scaled(ks[4], (E, I, H), I)}
    _L1_ffn_all = _L1_ffn_setup()
    _L1_ffn_in = {k: v for k, v in _L1_ffn_all.items() if k in ('router_w', 'w_gate', 'w_up', 'w_down')}
    del _L1_ffn_all
    return {'x': x, 'ctx_2048': ctx_2048, 'mask_BxS2_bk0': mask_BxS2_bk0, 'L0_ffn_ln1_w': _L0_ffn_in['ln1_w'], 'L0_ffn_ln2_w': _L0_ffn_in['ln2_w'], 'L0_ffn_kv_d_w': _L0_ffn_in['kv_d_w'], 'L0_ffn_q_d_w': _L0_ffn_in['q_d_w'], 'L0_ffn_k_u_w': _L0_ffn_in['k_u_w'], 'L0_ffn_v_u_w': _L0_ffn_in['v_u_w'], 'L0_ffn_q_u_w': _L0_ffn_in['q_u_w'], 'L0_ffn_rope_k_w': _L0_ffn_in['rope_k_w'], 'L0_ffn_rope_q_w': _L0_ffn_in['rope_q_w'], 'L0_ffn_o_w': _L0_ffn_in['o_w'], 'L0_ffn_sh_gate': _L0_ffn_in['sh_gate'], 'L0_ffn_sh_up': _L0_ffn_in['sh_up'], 'L0_ffn_sh_down': _L0_ffn_in['sh_down'], 'L0_ffn_r_gate': _L0_ffn_in['r_gate'], 'L0_ffn_r_up': _L0_ffn_in['r_up'], 'L0_ffn_r_down': _L0_ffn_in['r_down'], 'L0_ffn_router_w': _L0_ffn_in['router_w'], 'L0_ffn_router_b': _L0_ffn_in['router_b'], 'L1_ffn_router_w': _L1_ffn_in['router_w'], 'L1_ffn_w_gate': _L1_ffn_in['w_gate'], 'L1_ffn_w_up': _L1_ffn_in['w_up'], 'L1_ffn_w_down': _L1_ffn_in['w_down']}

def reference(x, ctx_2048, mask_BxS2_bk0, L0_ffn_ln1_w, L0_ffn_ln2_w, L0_ffn_kv_d_w, L0_ffn_q_d_w, L0_ffn_k_u_w, L0_ffn_v_u_w, L0_ffn_q_u_w, L0_ffn_rope_k_w, L0_ffn_rope_q_w, L0_ffn_o_w, L0_ffn_sh_gate, L0_ffn_sh_up, L0_ffn_sh_down, L0_ffn_r_gate, L0_ffn_r_up, L0_ffn_r_down, L0_ffn_router_w, L0_ffn_router_b, L1_ffn_router_w, L1_ffn_w_gate, L1_ffn_w_up, L1_ffn_w_down):
    import jax
    import jax.numpy as jnp

    def _L0_xattn_ref(q, k, v):
        import math
        import jax, jax.numpy as jnp
        import numpy as np
        HEADS = 16
        MASKED_BIAS = -10000.0

        def _mha(q, k, v):
            B, Sq, D = q.shape
            Sk = k.shape[-2]
            hd = D // HEADS
            qh = q.reshape(B, Sq, HEADS, hd).transpose(0, 2, 1, 3)
            kh = k.reshape(B, Sk, HEADS, hd).transpose(0, 2, 1, 3)
            vh = v.reshape(B, Sk, HEADS, hd).transpose(0, 2, 1, 3)
            scores = jnp.einsum('bhqd,bhkd->bhqk', qh, kh) / math.sqrt(hd)
            qi = jnp.arange(Sq)[:, None] + (Sk - Sq)
            ki = jnp.arange(Sk)[None, :]
            causal = ki <= qi
            scores = jnp.where(causal[None, None], scores, jnp.asarray(MASKED_BIAS, scores.dtype))
            attn = jax.nn.softmax(scores, axis=-1)
            out = jnp.einsum('bhqk,bhkd->bhqd', attn, vh)
            return out.transpose(0, 2, 1, 3).reshape(B, Sq, D)
        return _mha(q, k, v)

    def _L0_ffn_ref(x, ln1_w, ln2_w, kv_d_w, q_d_w, k_u_w, v_u_w, q_u_w, rope_k_w, rope_q_w, o_w, sh_gate, sh_up, sh_down, r_gate, r_up, r_down, router_w, router_b):
        import jax, jax.numpy as jnp
        import numpy as np
        B, S, H = (4, 256, 512)
        NH = 16
        HD = H // NH
        RD = HD // 2
        LAT = H // 4
        I = 256
        NE = 8
        NSH = 1
        NR = NE - NSH
        TOPK = 2
        EPS = 1e-05
        SCALING = 8.0

        def _w(key, shape, fan_in):
            return jax.random.normal(key, shape, dtype=jnp.float32) / np.sqrt(fan_in)

        def rmsnorm(x, w):
            rms = jax.lax.rsqrt(jnp.mean(x * x, axis=-1, keepdims=True) + EPS)
            return w * rms * x

        def rope_cos_sin(seq_len):
            inv_freq = 1.0 / 10000.0 ** (jnp.arange(0, RD, 2, dtype=jnp.float32) / RD)
            t = jnp.arange(seq_len, dtype=jnp.float32)
            ang = jnp.outer(t, inv_freq)
            emb = jnp.concatenate([ang, ang], axis=-1)
            return (jnp.cos(emb), jnp.sin(emb))

        def apply_rope(x, cos, sin):
            c = cos[None, :, None, :]
            s = sin[None, :, None, :]
            x1, x2 = jnp.split(x, 2, axis=-1)
            rot = jnp.concatenate([-x2, x1], axis=-1)
            return x * c + rot * s

        def expert_ffn(x, wg, wu, wd):
            h = jax.nn.silu(x @ wg) * (x @ wu) / SCALING
            return h @ wd

        def attention(x, kv_d_w, q_d_w, k_u_w, v_u_w, q_u_w, rope_k_w, rope_q_w, o_w):
            b, s, _ = x.shape
            kv_d = x @ kv_d_w
            q_d = x @ q_d_w
            k_p = (kv_d @ k_u_w).reshape(b, s, NH, RD)
            q_p = (q_d @ q_u_w).reshape(b, s, NH, RD)
            v = (kv_d @ v_u_w).reshape(b, s, NH, HD)
            k_r = (x @ rope_k_w).reshape(b, s, NH, RD)
            q_r = (q_d @ rope_q_w).reshape(b, s, NH, RD)
            cos, sin = rope_cos_sin(s)
            k_r = apply_rope(k_r, cos, sin)
            q_r = apply_rope(q_r, cos, sin)
            k = jnp.concatenate([k_p, k_r], axis=-1)
            q = jnp.concatenate([q_p, q_r], axis=-1)
            scale = 1.0 / np.sqrt(HD)
            scores = jnp.einsum('bqhd,bkhd->bhqk', q, k) * scale
            causal = jnp.tril(jnp.ones((s, s), dtype=bool))
            scores = jnp.where(causal[None, None], scores, jnp.finfo(scores.dtype).min)
            probs = jax.nn.softmax(scores, axis=-1)
            out = jnp.einsum('bhqk,bkhd->bqhd', probs, v).reshape(b, s, H)
            return out @ o_w

        def moe(x, sh_gate, sh_up, sh_down, r_gate, r_up, r_down, router_w, router_b):
            shared = expert_ffn(x, sh_gate, sh_up, sh_down)
            logits = x @ router_w + router_b
            probs = jax.nn.sigmoid(logits)
            scores, idx = jax.lax.top_k(probs, TOPK)
            scores = scores / jnp.sum(scores, axis=-1, keepdims=True)
            w = jnp.sum(jax.nn.one_hot(idx, NR, dtype=x.dtype) * scores[..., None], axis=-2)
            combined = jnp.zeros_like(x)
            for e in range(NR):
                combined = combined + w[..., e:e + 1] * expert_ffn(x, r_gate[e], r_up[e], r_down[e])
            return shared + combined
        h = x + attention(rmsnorm(x, ln1_w), kv_d_w, q_d_w, k_u_w, v_u_w, q_u_w, rope_k_w, rope_q_w, o_w)
        out = h + moe(rmsnorm(h, ln2_w), sh_gate, sh_up, sh_down, r_gate, r_up, r_down, router_w, router_b)
        return out

    def _L1_xattn_ref(hidden_states, memory_tokens, memory_mask):
        import jax, jax.numpy as jnp
        import numpy as np
        B, S, D = hidden_states.shape
        scale = 1.0 / jnp.sqrt(jnp.asarray(D, hidden_states.dtype))
        scores = jnp.einsum('bsd,bmd->bsm', hidden_states, memory_tokens) * scale
        neg_inf = jnp.asarray(-1e+30, scores.dtype)
        scores = jnp.where(memory_mask[:, None, :], scores, neg_inf)
        attn = jax.nn.softmax(scores, axis=-1)
        readout = jnp.einsum('bsm,bmd->bsd', attn, memory_tokens)
        valid_b = jnp.any(memory_mask, axis=-1)
        out = jnp.where(valid_b[:, None, None], readout, jnp.zeros_like(readout))
        return out

    def _L1_ffn_ref(hidden_states, router_w, w_gate, w_up, w_down):
        import jax, jax.numpy as jnp
        import numpy as np
        B, S, H, E, K, I = (2, 256, 512, 32, 8, 192)
        Bq, Sq, Hd = hidden_states.shape
        x = hidden_states.reshape(-1, Hd)
        logits = x @ router_w.T
        probs = jax.nn.softmax(logits.astype(jnp.float32), axis=-1)
        rw, sel = jax.lax.top_k(probs, K)
        rw = rw / jnp.sum(rw, axis=-1, keepdims=True)
        rw = rw.astype(x.dtype)

        def body(acc, operand):
            e, wg, wu, wd = operand
            w_e = jnp.sum(jnp.where(sel == e, rw, jnp.zeros_like(rw)), axis=-1)
            h = jax.nn.silu(x @ wg) * (x @ wu)
            return (acc + h @ wd * w_e[:, None], None)
        acc0 = jnp.zeros_like(x)
        acc, _ = jax.lax.scan(body, acc0, (jnp.arange(E), w_gate, w_up, w_down))
        return acc.reshape(Bq, Sq, Hd)
    x = x + _L0_xattn_ref(_layernorm(x, axis=-1), ctx_2048, ctx_2048)
    x = x + _L0_ffn_ref(_layernorm(x, axis=-1), L0_ffn_ln1_w, L0_ffn_ln2_w, L0_ffn_kv_d_w, L0_ffn_q_d_w, L0_ffn_k_u_w, L0_ffn_v_u_w, L0_ffn_q_u_w, L0_ffn_rope_k_w, L0_ffn_rope_q_w, L0_ffn_o_w, L0_ffn_sh_gate, L0_ffn_sh_up, L0_ffn_sh_down, L0_ffn_r_gate, L0_ffn_r_up, L0_ffn_r_down, L0_ffn_router_w, L0_ffn_router_b)
    x = x + _L1_xattn_ref(_layernorm(x, axis=-1), ctx_2048, mask_BxS2_bk0)
    x = x + _L1_ffn_ref(_layernorm(x, axis=-1), L1_ffn_router_w, L1_ffn_w_gate, L1_ffn_w_up, L1_ffn_w_down)
    return x

_drawn_inputs = setup_inputs


def setup_inputs(seed=0):
    import zlib

    import numpy as np

    out = dict(_drawn_inputs(seed))
    spreads = {'L0_ffn_ln1_w': (1.0, 0.2), 'L0_ffn_ln2_w': (1.0, 0.6), 'L0_ffn_router_b': (0.0, 0.8)}
    factors = {'L0_ffn_router_w': 2.821}
    for name, (base, spread) in spreads.items():
        noise = np.random.default_rng([zlib.crc32(name.encode()), seed]).standard_normal(out[name].shape)
        drawn = base * np.exp(spread * noise) if base else spread * noise
        out[name] = jnp.asarray(drawn.astype(out[name].dtype))
    for name, factor in factors.items():
        out[name] = (out[name] * factor).astype(out[name].dtype)
    return out
```

```python
from contextlib import ExitStack

import concourse.bass as bass
from concourse import mybir

F32, I32, U32, U8 = mybir.dt.float32, mybir.dt.int32, mybir.dt.uint32, mybir.dt.uint8
ALU, ACT, AX = mybir.AluOpType, mybir.ActivationFunctionType, mybir.AxisListType

P = 128
BATCH, SEQ, D = 4, 512, 512
TOKENS = BATCH * SEQ
TILES = TOKENS // P
TPB = SEQ // P
DC = D // P
KEYS = 64
HEADS, HD = 16, 32
ROT = HD // 2
LAT = 128
EPS = 1e-5
SPARE = P
BLOCKS = TOKENS // P
RING = 4
GROUP = 8
RESULTS = 4
AHEAD = 4

CONST = {}
_at = 0
for _name, _n in [("ident", P), ("earlier", P), ("future", P), ("allowed", KEYS), ("barred", KEYS),
                  ("cos", TPB * ROT), ("sin", TPB * ROT // 2), ("expert", 32), ("offset0", 8),
                  ("offset1", 32), ("token", TILES), ("tile", 2)]:
    CONST[_name] = (_at, _at + _n)
    _at += _n
CONST_COLS = _at


class Moe:

    def __init__(self, name, experts, routed, top, inner, scaling):
        self.name, self.experts, self.routed, self.top = name, experts, routed, top
        self.first = experts - routed
        self.inner, self.scaling = inner, scaling
        self.blocks = experts * BLOCKS + 1
        most = self.first * BLOCKS + (TOKENS * top) // P + routed
        self.tiles = -(-most // GROUP) * GROUP
        self.groups = -(-self.tiles // P)
        self.fc = [(f, min(P, inner - f)) for f in range(0, inner, P)]
        self.loads = 16 * (2 + len(self.fc))
        self.up = 2 * inner
        self.cols = DC * self.up + len(self.fc) * D


MOE0 = Moe("moe0", 8, 7, 2, 256, 8.0)
MOE1 = Moe("moe1", 32, 32, 8, 192, 1.0)


class Steps:

    def __init__(self, eng, sem, base=0, passed=None):
        self.eng, self.sem, self.base, self.passed, self.n = eng, sem, base, passed, 0

    def did(self, ins):
        ins.then_inc(self.sem, 1)
        self.n += 1

    def wait(self):
        self.eng.wait_ge(self.sem, self.base + self.n)

    def hold(self):
        hold(self.eng, self.sem, self.base + self.n, self.passed)

    def run(self, ins):
        self.did(ins)
        self.wait()


def hold(eng, sem, count, passed):
    eng.wait_ge(sem, count)
    eng.sem_inc(passed, 1)


def since(eng, sem, count):
    if not isinstance(count, int) or count > 0:
        eng.wait_ge(sem, count)


def tile_at(a, i):
    return a[:, bass.ds(i, 1), :].rearrange("p a n -> p (a n)")


def build(nc, a, out, stop=None, debug=None):
    ctx = ExitStack()

    def sb(name, shape, dt=F32):
        return ctx.enter_context(nc.sbuf_tensor(name, shape, dt))

    def sem(name):
        return ctx.enter_context(nc.semaphore(name))

    with ctx:
        m = {
            "x": sb("x_sb", [P, TILES, D]), "const": sb("const_sb", [P, CONST_COLS]),
            "ones": sb("ones", [P, P]), "mean_w": sb("mean_w", [KEYS, P]), "power": sb("power", [P, TPB]), "eps": sb("eps", [P, TPB]),
            "ctx": sb("ctx_sb", [P, BATCH, D]), "ctx_t": sb("ctx_t", [P, BATCH, DC, KEYS]),
            "psum": ctx.enter_context(nc.psum_tensor("psum", [P, 8, 512], F32)),
            "before0": sb("before0", [P, TPB + 1, MOE0.routed]),
            "before1": sb("before1", [P, TPB + 1, MOE1.routed]),
        }
        c = {k: m["const"][:, u:v] for k, (u, v) in CONST.items()}
        dram = {}
        for moe in (MOE0, MOE1):
            n = moe.name
            dram[n] = {
                "rows": nc.dram_tensor(f"{n}_rows", (TOKENS + SPARE, D), F32, kind="Internal").ap(),
                "sum": nc.dram_tensor(f"{n}_sum", (TOKENS + SPARE, D), F32, kind="Internal").ap(),
                "slots": nc.dram_tensor(f"{n}_slots", (moe.blocks * P, 2), F32, kind="Internal").ap(),
            }
        s_init = sem("tables_set")
        m["loaded"] = [sem(f"loaded{u}") for u in range(RING)]
        m["gathered"] = [sem(f"gathered{u}") for u in range(GROUP)]
        m["passed"] = {e: sem(f"passed_{e}") for e in ("dve", "pool", "pe", "sp")}
        front(nc, a, m, c, dram, s_init)
        if stop == "front":
            dump(nc, debug, dram["moe0"], m["before0"], MOE0)
            return
        mixture(nc, a, m, c, dram["moe0"], MOE0, m["before0"], None)
        if stop == "moe0":
            dump(nc, debug, dram["moe0"], m["before0"], MOE0)
            return
        middle(nc, a, m, c, dram)
        if stop == "middle":
            dump(nc, debug, dram["moe1"], m["before1"], MOE1)
            return
        mixture(nc, a, m, c, dram["moe1"], MOE1, m["before1"], out)


def dump(nc, debug, d, before, moe):
    with nc.semaphore("dumped") as s, nc.Block() as block:
        @block.sync
        def _(sp):
            sp.dma_start(debug[0], d["rows"]).then_inc(s, 16)
            sp.dma_start(debug[1], d["sum"]).then_inc(s, 16)
            sp.dma_start(debug[2], d["slots"]).then_inc(s, 16)
            sp.dma_start(debug[3], before[:, TPB, :]).then_inc(s, 16)
            sp.wait_ge(s, 64)




def route_memory(sb, moe):
    n, k = moe.routed, moe.top
    return {
        "prob": sb(f"{moe.name}_prob", [P, TPB, max(n, 8)]), "logit": sb(f"{moe.name}_logit", [P, TPB, n]),
        "value": sb(f"{moe.name}_value", [P, TPB, 8]), "index": sb(f"{moe.name}_index", [P, TPB, 8], U32),
        "chosen": sb(f"{moe.name}_chosen", [P, TPB, k]), "total": sb(f"{moe.name}_total", [P, TPB, 1]),
        "hot": sb(f"{moe.name}_hot", [P, TPB * k, n]), "picked": sb(f"{moe.name}_picked", [P, TPB * k, n]),
        "mask": sb(f"{moe.name}_mask", [P, TPB, n]), "place": sb(f"{moe.name}_place", [P, TPB, n]),
        "slot_f": sb(f"{moe.name}_slot_f", [P, TPB * k]), "slot": sb(f"{moe.name}_slot", [P, TPB * k], I32),
        "entry": sb(f"{moe.name}_entry", [P, TPB * k, 2]),
    }


def choose(nc, steps, r, moe, c, token, before, masked):
    v, n, k = nc.vector, moe.routed, moe.top
    steps.hold()
    for t in range(TPB):
        steps.did(v.max(r["value"][:, t, :], r["prob"][:, t, :]))
    steps.hold()
    for t in range(TPB):
        steps.did(v.max_index(r["index"][:, t, :], r["value"][:, t, :], r["prob"][:, t, :]))
    steps.did(v.tensor_reduce(r["total"][:, :, 0], r["value"][:, :, 0:k], AX.X, ALU.add))
    entry = r["entry"][:, :, :].rearrange("p (t k) e -> p t k e", k=k)
    steps.did(v.tensor_copy(entry[:, :, :, 0], token.unsqueeze(2).to_broadcast([P, TPB, k])))
    steps.wait()
    steps.did(v.tensor_copy(r["chosen"][:, :, :], r["index"][:, :, 0:k]))
    steps.did(v.reciprocal(r["total"][:, :, :], r["total"][:, :, :]))
    steps.wait()
    steps.did(v.tensor_tensor(entry[:, :, :, 1], r["value"][:, :, 0:k],
                              r["total"][:, :, :].to_broadcast([P, TPB, k]), ALU.mult))
    chosen = r["chosen"][:, :, :].rearrange("p t k -> p (t k)")
    steps.run(v.tensor_tensor(r["hot"][:, :, :], c["expert"][:, 0:n].unsqueeze(1).to_broadcast([P, TPB * k, n]),
                              chosen.unsqueeze(2).to_broadcast([P, TPB * k, n]), ALU.is_equal))
    steps.run(v.tensor_reduce(r["mask"][:, :, :], r["hot"][:, :, :].rearrange("p (t k) e -> p t e k", k=k),
                              AX.X, ALU.add))
    for t in range(TPB):
        ins = v.tensor_tensor(before[:, t + 1, :], before[:, t, :], r["mask"][:, t, :], ALU.add)
        if t < TPB - 1:
            steps.run(ins)
    ins.then_inc(masked, 1)


def places(nc, r, moe, c, m, before, bank):
    n = moe.routed
    for t in range(TPB):
        o = m["psum"][:, bank, t * n:(t + 1) * n]
        nc.tensor.matmul(o, c["earlier"], r["mask"][:, t, :], start=True, stop=False)
        last = nc.tensor.matmul(o, m["ones"][:, :], before[:, t, :], start=False, stop=True)
    return last


def slots(nc, steps, r, moe, c, m, before, bank, offset):
    v, n, k = nc.vector, moe.routed, moe.top
    rank = m["psum"][:, bank, 0:TPB * n].rearrange("p (t e) -> p t e", e=n)
    steps.did(v.tensor_tensor(r["place"][:, :, :], rank, offset.unsqueeze(1).to_broadcast([P, TPB, n]), ALU.add))
    steps.did(v.tensor_copy(before[:, 0, :], before[:, TPB, :]))
    steps.wait()
    hot = r["hot"][:, :, :].rearrange("p (t k) e -> p t k e", k=k)
    picked = r["picked"][:, :, :].rearrange("p (t k) e -> p t k e", k=k)
    for t in range(TPB):
        steps.did(v.tensor_tensor(picked[:, t], hot[:, t], r["place"][:, t, :].unsqueeze(1).to_broadcast([P, k, n]), ALU.mult))
    steps.wait()
    steps.run(v.tensor_reduce(r["slot_f"][:, :], r["picked"][:, :, :], AX.X, ALU.add))
    return v.tensor_copy(r["slot"][:, :], r["slot_f"][:, :])


def scatter(pool, r, moe, table, written):
    for j in range(TPB * moe.top):
        pool.indirect_dma_start(table, bass.IndirectOffsetOnAxis(r["slot"][:, j:j + 1], 0),
                                r["entry"][:, j, :], None).then_inc(written, 16)




def front(nc, a, m, c, dram, s_init):
    ctx = ExitStack()
    with ctx:
        def sb(name, shape, dt=F32):
            return ctx.enter_context(nc.sbuf_tensor(name, shape, dt))

        def sem(name):
            return ctx.enter_context(nc.semaphore(name))

        ps, x, ctx_sb = m["psum"], m["x"], m["ctx"]
        GH = P // HD
        w_kvd, w_qd = sb("w_kvd", [P, DC, LAT]), sb("w_qd", [P, DC, LAT])
        w_kr = sb("w_kr", [P, DC, D // 2])
        w_q = sb("w_q", [LAT, D])
        w_ku, w_vu = sb("w_ku", [LAT, D // 2]), sb("w_vu", [LAT, D])
        w_o = sb("w_o", [P, DC, D])
        w_rt = sb("w_rt", [P, DC, MOE0.routed])
        bias_rt = sb("bias_rt", [P, MOE0.routed])
        ln1, ln2 = sb("ln1", [P, D]), sb("ln2", [P, D])
        ctx_heads = sb("ctx_heads", [P, BATCH, DC, GH * KEYS])
        ctx_pairs = sb("ctx_pairs", [P, BATCH, HEADS // 2, 2 * HD])
        stats, mv, rstd = sb("stats", [P, TPB, 6]), sb("mv", [P, TPB, 2]), sb("rstd", [P, TPB])
        rms, var_e = sb("rms", [P, TPB]), sb("var_e", [P, TPB])
        xn, xn_t = sb("xn", [P, D]), sb("xn_t", [P, DC, P])
        att0 = sb("att0", [P, HEADS, KEYS])
        top0, sum0 = sb("top0", [P, HEADS]), sb("sum0", [P, HEADS])
        att0_t = sb("att0_t", [P, HEADS // 2, P])
        y, z = sb("y", [P, TPB, D]), sb("z", [P, TPB, D])
        z_t = sb("z_t", [P, DC, SEQ])
        kv_d, q_d = sb("kv_d", [LAT, SEQ]), sb("q_d", [LAT, SEQ])
        v_sb = sb("v_sb", [P, TPB, D])
        qk = sb("qk", [P, 2, 2 * HEADS, HD])
        rot_a, rot_b = sb("rot_a", [P, 2 * HEADS, ROT]), sb("rot_b", [P, 2 * HEADS, ROT])
        q_t, k_t = sb("q_t", [P, DC, SEQ]), sb("k_t", [P, DC, SEQ])
        neg_top = sb("neg_top", [P, 2, 2])
        prob = sb("prob", [P, 2, 2, SEQ])
        prob_t = sb("prob_t", [P, 2, 2 * TPB, P])
        den = sb("den", [P, TPB, HEADS])
        att, att_t = sb("att", [P, TPB, D]), sb("att_t", [P, 2, DC, P])
        h, acc, hn = v_sb, y, z
        hn_t = sb("hn_t", [P, 2, DC, P])
        r = route_memory(sb, MOE0)

        names = ("const x weights ones_set eps0 rstd0 xn0 xn0_t xn0_ts s0 mean0 shift0 e0 p0 p0_t p0_ts o0 var1 "
                 "rstd1 z zt zts kvd qd kvds qds pp pr pv_ qkp qkr vs qkt qts kts st ntop pexp pt pta ptb pv "
                 "attd hres at ats oproj var2 rms2 hn hnt hnts logit lgs lge masked ranked slotted scattered rows_out "
                 "dve pool ctxt ctxts acts blocks_set").split()
        S = {n: sem("f_" + n) for n in names}
        r0 = dram["moe0"]

        block = ctx.enter_context(nc.Block())

        @block.sync
        def _(sp):
            sp.dma_start(m["const"][:, :], a["const"]).then_inc(S["const"], 16)
            for half in range(2):
                sp.dma_start(ctx_sb[half * KEYS:(half + 1) * KEYS, :, :],
                             a["ctx_2048"].rearrange("b k d -> k b d")).then_inc(S["const"], 16)
            sp.dma_start(x[:, :, :], a["x"].rearrange("b (t p) d -> p (b t) d", p=P)).then_inc(S["x"], 16)
            chunks = "(c p) n -> p c n"
            for dst, src in [(w_kvd[:, :, :], a["L0_ffn_kv_d_w"].rearrange(chunks, p=P)),
                             (w_qd[:, :, :], a["L0_ffn_q_d_w"].rearrange(chunks, p=P)),
                             (w_kr[:, :, :], a["L0_ffn_rope_k_w"].rearrange(chunks, p=P)),
                             (w_q[:, 0:D // 2], a["L0_ffn_q_u_w"]), (w_q[:, D // 2:D], a["L0_ffn_rope_q_w"]),
                             (w_ku[:, :], a["L0_ffn_k_u_w"]), (w_vu[:, :], a["L0_ffn_v_u_w"]),
                             (w_o[:, :, :], a["L0_ffn_o_w"].rearrange(chunks, p=P)),
                             (w_rt[:, :, :], a["L0_ffn_router_w"].rearrange(chunks, p=P)),
                             (bias_rt[:, :], a["L0_ffn_router_b"].partition_broadcast(P)),
                             (ln1[:, :], a["L0_ffn_ln1_w"].partition_broadcast(P)),
                             (ln2[:, :], a["L0_ffn_ln2_w"].partition_broadcast(P))]:
                sp.dma_start(dst, src).then_inc(S["weights"], 16)
            for moe in (MOE0, MOE1):
                d = dram[moe.name]
                sp.dma_start(d["slots"].rearrange("(b p) e -> b (p e)", p=P), a[moe.name + "_empty"]).then_inc(s_init, 16)
                for n in ("rows", "sum"):
                    sp.dma_start(d[n][TOKENS:TOKENS + SPARE, :], a["zero_rows"]).then_inc(s_init, 16)
            with sp.Fori(0, BATCH) as b:
                sp.wait_ge(S["hn"], TPB * (b + 1))
                sp.dma_start(r0["sum"][bass.ds(b * SEQ, SEQ), :].rearrange("(t p) d -> p t d", p=P), acc[:, :, :]).then_inc(S["rows_out"], 16)
                sp.dma_start(r0["rows"][bass.ds(b * SEQ, SEQ), :].rearrange("(t p) d -> p t d", p=P), hn[:, :, :]).then_inc(S["rows_out"], 16)
                hold(sp, S["rows_out"], 32 * (b + 1), m["passed"]["sp"])

        @block.gpsimd
        def _(pool):
            g = nc.gpsimd
            g.memset(m["ones"][:, :], 1.0)
            g.memset(m["mean_w"][:, :], 1.0 / KEYS)
            g.memset(m["power"][:, :], -0.5)
            g.memset(m["eps"][:, :], EPS)
            g.memset(m["before0"][:, 0, :], 0.0)
            g.memset(m["before1"][:, 0, :], 0.0)
            g.memset(r["prob"][:, :, :], -1.0).then_inc(S["ones_set"], 1)
            pool.wait_ge(S["ones_set"], 1)
            pool.wait_ge(s_init, 96)
            with pool.Fori(0, BATCH) as b:
                own = Steps(pool, S["pool"], b * 4)
                pool.wait_ge(S["eps0"], b + 1)
                g.tensor_tensor(rstd[:, 0:1], var_e[:, 0:1], m["power"][:, 0:1], ALU.pow).then_inc(S["rstd0"], 1)
                pool.wait_ge(S["var1"], b + 1)
                own.run(g.tensor_tensor(rstd[:, :], var_e[:, :], m["power"][:, 0:TPB], ALU.pow))
                own.run(g.tensor_tensor(rms[:, :], rstd[:, :], rstd[:, :], ALU.mult))
                own.run(g.tensor_tensor(rms[:, :], rms[:, :], mv[:, :, 1], ALU.mult))
                own.run(g.tensor_tensor(rms[:, :], rms[:, :], m["eps"][:, :], ALU.add))
                g.tensor_tensor(rms[:, :], rms[:, :], m["power"][:, 0:TPB], ALU.pow).then_inc(S["rstd1"], 1)
                assert own.n == 4
                pool.wait_ge(S["var2"], b + 1)
                g.tensor_tensor(rms[:, :], var_e[:, :], m["power"][:, 0:TPB], ALU.pow).then_inc(S["rms2"], 1)
                hold(pool, S["slotted"], b + 1, m["passed"]["pool"])
                scatter(pool, r, MOE0, r0["slots"], S["scattered"])
                pool.wait_ge(S["scattered"], 16 * TPB * MOE0.top * (b + 1))

        def prob_t_second(act, sc, b, s, ns):
            act.wait_ge(S["pt"], b * ns + s + 1)
            act.wait_ge(S["pv"], b * ns + s - 1)
            w = (s // (HEADS // 2) + 1) * 2 * P - 512
            sc.activation(prob_t[:, s % 2, 4:4 + w // P, :].rearrange("p c q -> p (c q)"), ps[:, 5, 0:w], ACT.Copy).then_inc(S["ptb"], 1)

        @block.scalar
        def _(act):
            sc = nc.scalar
            with act.Fori(0, BATCH) as b:
                act.wait_ge(S["xn0_t"], b + 1)
                sc.activation(xn_t[:, :, :].rearrange("p c q -> p (c q)"), ps[:, 0, :], ACT.Copy).then_inc(S["xn0_ts"], 1)
                act.wait_ge(S["shift0"], b + 1)
                sc.activation(att0[:, :, :], att0[:, :, :], ACT.Exp).then_inc(S["e0"], 1)
                act.wait_ge(S["p0_t"], b + 1)
                for j in range(2):
                    sc.activation(att0_t[:, 4 * j:4 * j + 4, :].rearrange("p c q -> p (c q)"), ps[:, 4 + j, :], ACT.Copy).then_inc(S["p0_ts"], 1)
                for t in range(TPB):
                    act.wait_ge(S["zt"], b * TPB + t + 1)
                    sc.activation(z_t[:, :, t * P:(t + 1) * P], ps[:, t, :].rearrange("p (c q) -> p c q", q=P), ACT.Copy).then_inc(S["zts"], 1)
                act.wait_ge(S["kvd"], b + 1)
                sc.activation(kv_d[:, :], ps[:, 4, :], ACT.Copy).then_inc(S["kvds"], 1)
                for t in range(TPB):
                    i = t % 2
                    act.wait_ge(S["pp"], b * TPB + t + 1)
                    if t >= 2:
                        act.wait_ge(S["qkt"], b * TPB + t - 1)
                    sc.activation(qk[:, i, :, 0:ROT], ps[:, 2 * i, :].rearrange("p (h e) -> p h e", e=ROT), ACT.Copy).then_inc(S["qkp"], 1)
                    act.wait_ge(S["pv_"], b * TPB + t + 1)
                    sc.activation(v_sb[:, t, :], ps[:, 6 + i, :], ACT.Copy).then_inc(S["vs"], 1)
                    act.wait_ge(S["qkt"], b * TPB + t + 1)
                    sc.activation(q_t[:, :, t * P:(t + 1) * P], ps[:, 4, :].rearrange("p (c q) -> p c q", q=P), ACT.Copy).then_inc(S["qts"], 1)
                NS = TPB * HEADS // 2
                for s in range(NS):
                    i, hp = s // (HEADS // 2), s % (HEADS // 2)
                    n, u = (i + 1) * P, s % 2
                    act.wait_ge(S["ntop"], b * NS + s + 1)
                    if s >= 2:
                        act.wait_ge(S["pt"], b * NS + s - 1)
                    for e in range(2):
                        ins = sc.activation(prob[:, u, e, 0:n], ps[:, 2 * u + e, 0:n], ACT.Exp, bias=neg_top[:, u, e:e + 1],
                                            scale=HD ** -0.5, accum_out=den[:, i, 2 * hp + e:2 * hp + e + 1])
                    ins.then_inc(S["pexp"], 1)
                    if s >= 1 and (s - 1) // (HEADS // 2) >= 2:
                        prob_t_second(act, sc, b, s - 1, NS)
                prob_t_second(act, sc, b, NS - 1, NS)
                for t in range(TPB):
                    act.wait_ge(S["at"], b * TPB + t + 1)
                    if t >= 2:
                        act.wait_ge(S["oproj"], b * TPB + t - 1)
                    sc.activation(att_t[:, t % 2, :, :].rearrange("p c q -> p (c q)"), ps[:, t % 2, :], ACT.Copy).then_inc(S["ats"], 1)
                for t in range(TPB):
                    act.wait_ge(S["hnt"], b * TPB + t + 1)
                    if t >= 2:
                        act.wait_ge(S["logit"], b * TPB + t - 1)
                    sc.activation(hn_t[:, t % 2, :, :].rearrange("p c q -> p (c q)"), ps[:, 4 + t % 2, :], ACT.Copy).then_inc(S["hnts"], 1)
                act.wait_ge(S["lgs"], b + 1)
                sc.activation(r["logit"][:, :, :], r["logit"][:, :, :], ACT.Exp, scale=-1.0).then_inc(S["lge"], 1)

        DVE_STEPS = 115

        @block.vector
        def _(dve):
            v = nc.vector
            dve.wait_ge(S["const"], 48)
            pre = Steps(dve, S["acts"])
            pre.did(v.memset(ctx_heads[:, :, :, :], 0.0))
            pre.did(v.memset(ctx_pairs[:, :, :, :], 0.0))
            pre.wait()
            pairs = ctx_sb[:, :, :].rearrange("p b (j two e) -> p b j two e", two=2, e=HD)
            for half in range(2):
                rows = slice(half * KEYS, (half + 1) * KEYS)
                for b in range(BATCH):
                    last = v.tensor_copy(ctx_pairs[rows, b, :, half * HD:(half + 1) * HD], pairs[rows, b, :, half, :])
            for b in range(BATCH):
                dve.wait_ge(S["ctxt"], b + 1)
                for g in range(GH):
                    rows = slice(g * HD, (g + 1) * HD)
                    v.tensor_copy(ctx_heads[rows, b, :, g * KEYS:(g + 1) * KEYS],
                                  ps[rows, b, 0:DC * KEYS].rearrange("p (c k) -> p c k", k=KEYS))
                v.tensor_copy(m["ctx_t"][:, b, :, :], ps[:, b, 0:DC * KEYS].rearrange("p (c k) -> p c k", k=KEYS)).then_inc(S["ctxts"], 1)
            dve.wait_ge(S["x"], 16)
            dve.wait_ge(S["ones_set"], 1)
            dve.wait_ge(S["weights"], 16 * 12)

            with dve.Fori(0, BATCH) as b:
                own = Steps(dve, S["dve"], b * DVE_STEPS, m["passed"]["dve"])

                def stats_of(src, t):
                    own.did(v.bn_stats(stats[:, t, :], src))
                    own.hold()
                    own.did(v.bn_aggr(mv[:, t, :], stats[:, t, :]))

                xq = tile_at(x, b * TPB + TPB - 1)
                stats_of(xq, 0)
                own.wait()
                v.tensor_scalar(var_e[:, 0:1], mv[:, 0, 1:2], EPS, None, ALU.add).then_inc(S["eps0"], 1)
                dve.wait_ge(S["rstd0"], b + 1)
                v.tensor_scalar(xn[:, :], xq, mv[:, 0, 0:1], rstd[:, 0:1], ALU.subtract, ALU.mult).then_inc(S["xn0"], 1)
                dve.wait_ge(S["mean0"], b + 1)
                for t in range(TPB - 1):
                    xt = tile_at(x, b * TPB + t)
                    own.did(v.tensor_tensor(xt, xt, ps[:, 3, :], ALU.add))
                dve.wait_ge(S["s0"], b + 1)
                s2 = ps[:, 1:3, :].rearrange("p a (h k) -> p (a h) k", k=KEYS)
                own.run(v.scalar_tensor_tensor(att0[:, :, :], s2, HD ** -0.5, c["allowed"].unsqueeze(1).to_broadcast([P, HEADS, KEYS]), ALU.mult, ALU.mult))
                own.run(v.tensor_tensor(att0[:, :, :], att0[:, :, :], c["barred"].unsqueeze(1).to_broadcast([P, HEADS, KEYS]), ALU.add))
                own.run(v.tensor_reduce(top0[:, :], att0[:, :, :], AX.X, ALU.max))
                v.tensor_tensor(att0[:, :, :], att0[:, :, :], top0[:, :].unsqueeze(2).to_broadcast([P, HEADS, KEYS]), ALU.subtract).then_inc(S["shift0"], 1)
                dve.wait_ge(S["e0"], b + 1)
                own.run(v.tensor_reduce(sum0[:, :], att0[:, :, :], AX.X, ALU.add))
                own.run(v.reciprocal(sum0[:, :], sum0[:, :]))
                v.tensor_tensor(att0[:, :, :], att0[:, :, :], sum0[:, :].unsqueeze(2).to_broadcast([P, HEADS, KEYS]), ALU.mult).then_inc(S["p0"], 1)
                dve.wait_ge(S["o0"], b + 1)
                own.did(v.tensor_tensor(xq, xq, ps[:, 6, :], ALU.add))

                own.hold()
                for t in range(TPB):
                    stats_of(tile_at(x, b * TPB + t), t)
                own.wait()
                v.tensor_scalar(var_e[:, :], mv[:, :, 1], EPS, None, ALU.add).then_inc(S["var1"], 1)
                dve.wait_ge(S["rstd1"], b + 1)
                for t in range(TPB):
                    own.run(v.tensor_scalar(y[:, t, :], tile_at(x, b * TPB + t), mv[:, t, 0:1], rstd[:, t:t + 1], ALU.subtract, ALU.mult))
                    v.scalar_tensor_tensor(z[:, t, :], y[:, t, :], rms[:, t:t + 1], ln1[:, :], ALU.mult, ALU.mult).then_inc(S["z"], 1)
                dve.wait_ge(S["qd"], b + 1)
                v.tensor_copy(q_d[:, :], ps[:, 5, :]).then_inc(S["qds"], 1)

                for t in range(TPB):
                    i = t % 2
                    dve.wait_ge(S["pr"], b * TPB + t + 1)
                    src = ps[:, 2 * i + 1, :].rearrange("p (h e) -> p h e", e=ROT)
                    cos = c["cos"][:, t * ROT:(t + 1) * ROT].unsqueeze(1).to_broadcast([P, 2 * HEADS, ROT])
                    sin = c["sin"][:, t * ROT // 2:(t + 1) * ROT // 2].unsqueeze(1).to_broadcast([P, 2 * HEADS, ROT // 2])
                    own.did(v.tensor_tensor(rot_a[:, :, :], src, cos, ALU.mult))
                    own.did(v.tensor_tensor(rot_b[:, :, 0:ROT // 2], src[:, :, ROT // 2:ROT], sin, ALU.mult))
                    own.did(v.tensor_tensor(rot_b[:, :, ROT // 2:ROT], src[:, :, 0:ROT // 2], sin, ALU.mult))
                    own.wait()
                    if t >= 2:
                        dve.wait_ge(S["qkt"], b * TPB + t - 1)
                    own.did(v.tensor_tensor(qk[:, i, :, ROT:ROT + ROT // 2], rot_a[:, :, 0:ROT // 2], rot_b[:, :, 0:ROT // 2], ALU.subtract))
                    v.tensor_tensor(qk[:, i, :, ROT + ROT // 2:HD], rot_a[:, :, ROT // 2:ROT], rot_b[:, :, ROT // 2:ROT], ALU.add).then_inc(S["qkr"], 1)
                    dve.wait_ge(S["qkt"], b * TPB + t + 1)
                    dve.wait_ge(S["qkr"], b * TPB + t + 1)
                    v.tensor_copy(k_t[:, :, t * P:(t + 1) * P], ps[:, 5, :].rearrange("p (c q) -> p c q", q=P)).then_inc(S["kts"], 1)

                NS = TPB * HEADS // 2
                for s in range(NS + 1):
                    if s < NS:
                        i, u = s // (HEADS // 2), s % 2
                        n = (i + 1) * P
                        dve.wait_ge(S["st"], b * NS + s + 1)
                        if s >= 2:
                            dve.wait_ge(S["pexp"], b * NS + s - 1)
                        own.run(v.tensor_reduce(neg_top[:, u, :], ps[:, 2 * u:2 * u + 2, 0:n], AX.X, ALU.max))
                        v.tensor_scalar(neg_top[:, u, :], neg_top[:, u, :], -(HD ** -0.5), None, ALU.mult).then_inc(S["ntop"], 1)
                    if s >= 1:
                        q = s - 1
                        w = min(512, (q // (HEADS // 2) + 1) * 2 * P)
                        dve.wait_ge(S["pt"], b * NS + q + 1)
                        if q >= 2:
                            dve.wait_ge(S["pv"], b * NS + q - 1)
                        v.tensor_copy(prob_t[:, q % 2, 0:w // P, :].rearrange("p c q -> p (c q)"), ps[:, 4, 0:w]).then_inc(S["pta"], 1)
                        if (q + 1) % (HEADS // 2) == 0:
                            i = q // (HEADS // 2)
                            dve.wait_ge(S["pexp"], b * NS + q + 1)
                            own.run(v.reciprocal(den[:, i, :], den[:, i, :]))
                            dve.wait_ge(S["pv"], b * NS + q + 1)
                            v.tensor_tensor(att[:, i, :].rearrange("p (h e) -> p h e", e=HD), ps[:, 6 + i % 2, :].rearrange("p (h e) -> p h e", e=HD),
                                            den[:, i, :].unsqueeze(2).to_broadcast([P, HEADS, HD]), ALU.mult).then_inc(S["attd"], 1)

                for t in range(TPB):
                    dve.wait_ge(S["oproj"], b * TPB + t + 1)
                    v.tensor_tensor(h[:, t, :], y[:, t, :], ps[:, 2 + t % 2, :], ALU.add).then_inc(S["hres"], 1)
                    dve.wait_ge(S["hres"], b * TPB + t + 1)
                    own.did(v.tensor_tensor(acc[:, t, :], tile_at(x, b * TPB + t), h[:, t, :], ALU.add))
                    stats_of(h[:, t, :], t)
                own.wait()
                own.run(v.tensor_tensor(var_e[:, :], mv[:, :, 0], mv[:, :, 0], ALU.mult))
                v.scalar_tensor_tensor(var_e[:, :], var_e[:, :], EPS, mv[:, :, 1], ALU.add, ALU.add).then_inc(S["var2"], 1)
                dve.wait_ge(S["rms2"], b + 1)
                for t in range(TPB):
                    v.scalar_tensor_tensor(hn[:, t, :], h[:, t, :], rms[:, t:t + 1], ln2[:, :], ALU.mult, ALU.mult).then_inc(S["hn"], 1)

                dve.wait_ge(S["logit"], b * TPB + TPB)
                n = MOE0.routed
                v.tensor_tensor(r["logit"][:, :, :], ps[:, 6, 0:TPB * 8].rearrange("p (t e) -> p t e", e=8)[:, :, 0:n],
                                bias_rt[:, :].unsqueeze(1).to_broadcast([P, TPB, n]), ALU.add).then_inc(S["lgs"], 1)
                dve.wait_ge(S["lge"], b + 1)
                own.run(v.tensor_scalar(r["logit"][:, :, :], r["logit"][:, :, :], 1.0, None, ALU.add))
                own.run(v.reciprocal(r["prob"][:, :, 0:n], r["logit"][:, :, :]))
                token = c["token"][:, bass.ds(b * TPB, TPB)]
                choose(nc, own, r, MOE0, c, token, m["before0"], S["masked"])
                dve.wait_ge(S["ranked"], b + 1)
                slots(nc, own, r, MOE0, c, m, m["before0"], 7, c["offset0"][:, 0:n]).then_inc(S["slotted"], 1)
                dve.wait_ge(S["scattered"], 16 * TPB * MOE0.top * (b + 1))
                dve.wait_ge(S["rows_out"], 32 * (b + 1))
                assert own.n == DVE_STEPS, own.n

        @block.tensor
        def _(pe):
            mm, tr = nc.tensor.matmul, nc.tensor.transpose
            ident = c["ident"]
            pe.wait_ge(S["const"], 48)
            for b in range(BATCH):
                for k in range(DC):
                    last = tr(ps[:, b, k * KEYS:(k + 1) * KEYS], ctx_sb[0:KEYS, b, k * P:(k + 1) * P], ident[0:KEYS, 0:KEYS])
                last.then_inc(S["ctxt"], 1)
            pe.wait_ge(S["ctxts"], BATCH)
            pe.wait_ge(S["ones_set"], 1)
            pe.wait_ge(S["weights"], 16 * 12)
            with pe.Fori(0, BATCH) as b:
                def four(bank, src):
                    for k in range(DC):
                        last = tr(ps[:, bank, k * P:(k + 1) * P], src[:, k * P:(k + 1) * P], ident)
                    return last

                mm(ps[:, 3, :], m["mean_w"][:, :], tile_at(ctx_sb, b)[0:KEYS, :], start=True, stop=True).then_inc(S["mean0"], 1)
                pe.wait_ge(S["xn0"], b + 1)
                four(0, xn[:, :]).then_inc(S["xn0_t"], 1)
                pe.wait_ge(S["xn0_ts"], b + 1)
                for k in range(DC):
                    last = mm(ps[:, 1 + k // 2, (k % 2) * 256:(k % 2) * 256 + 256], xn_t[:, k, :],
                              ctx_heads[:, bass.ds(b, 1), k, :].rearrange("p a n -> p (a n)"), start=True, stop=True)
                last.then_inc(S["s0"], 1)
                pe.wait_ge(S["p0"], b + 1)
                flat = att0[:, :, :].rearrange("p h k -> p (h k)")
                for j in range(HEADS // 2):
                    last = tr(ps[:, 4 + j // 4, (j % 4) * P:(j % 4 + 1) * P], flat[:, j * P:(j + 1) * P], ident)
                last.then_inc(S["p0_t"], 1)
                pe.wait_ge(S["p0_ts"], 2 * (b + 1))
                for j in range(HEADS // 2):
                    last = mm(ps[:, 6, j * 2 * HD:(j + 1) * 2 * HD], att0_t[:, j, :],
                              ctx_pairs[:, bass.ds(b, 1), j, :].rearrange("p a n -> p (a n)"), start=True, stop=True)
                last.then_inc(S["o0"], 1)

                for t in range(TPB):
                    pe.wait_ge(S["z"], b * TPB + t + 1)
                    four(t, z[:, t, :]).then_inc(S["zt"], 1)
                pe.wait_ge(S["zts"], TPB * (b + 1))
                for bank, w, done in ((4, w_kvd, "kvd"), (5, w_qd, "qd")):
                    for k in range(DC):
                        last = mm(ps[:, bank, :], w[:, k, :], z_t[:, k, :], start=(k == 0), stop=(k == DC - 1))
                    last.then_inc(S[done], 1)
                pe.wait_ge(S["kvds"], b + 1)
                pe.wait_ge(S["qds"], b + 1)

                def project(t):
                    i, q = t % 2, slice(t * P, (t + 1) * P)
                    if t >= 2:
                        pe.wait_ge(S["vs"], b * TPB + t - 1)
                    mm(ps[:, 2 * i, 0:256], q_d[:, q], w_q[:, 0:256], start=True, stop=True)
                    mm(ps[:, 2 * i, 256:512], kv_d[:, q], w_ku[:, :], start=True, stop=True).then_inc(S["pp"], 1)
                    mm(ps[:, 2 * i + 1, 0:256], q_d[:, q], w_q[:, 256:512], start=True, stop=True)
                    for k in range(DC):
                        last = mm(ps[:, 2 * i + 1, 256:512], z_t[:, k, q], w_kr[:, k, :], start=(k == 0), stop=(k == DC - 1))
                    last.then_inc(S["pr"], 1)
                    mm(ps[:, 6 + i, :], kv_d[:, q], w_vu[:, :], start=True, stop=True).then_inc(S["pv_"], 1)

                project(0)
                for t in range(TPB):
                    if t + 1 < TPB:
                        project(t + 1)
                    pe.wait_ge(S["qkp"], b * TPB + t + 1)
                    pe.wait_ge(S["qkr"], b * TPB + t + 1)
                    if t >= 1:
                        pe.wait_ge(S["qts"], b * TPB + t)
                        pe.wait_ge(S["kts"], b * TPB + t)
                    flat = qk[:, t % 2, :, :].rearrange("p h e -> p (h e)")
                    four(4, flat[:, 0:D])
                    four(5, flat[:, D:2 * D]).then_inc(S["qkt"], 1)
                pe.wait_ge(S["qts"], TPB * (b + 1))
                pe.wait_ge(S["kts"], TPB * (b + 1))
                pe.wait_ge(S["vs"], TPB * (b + 1))

                NS = TPB * HEADS // 2

                def scores(s):
                    i, hp, u = s // (HEADS // 2), s % (HEADS // 2), s % 2
                    n = (i + 1) * P
                    if s >= 2:
                        pe.wait_ge(S["pexp"], b * NS + s - 1)
                    for e in range(2):
                        k, g = (2 * hp + e) // GH, (2 * hp + e) % GH
                        rows = slice(g * HD, (g + 1) * HD)
                        mm(ps[:, 2 * u + e, 0:n], q_t[rows, k, i * P:(i + 1) * P], k_t[rows, k, 0:n], start=True, stop=False)
                        last = mm(ps[:, 2 * u + e, n - P:n], ident, c["future"], start=False, stop=True)
                    last.then_inc(S["st"], 1)

                scores(0)
                for s in range(NS):
                    i, hp, u = s // (HEADS // 2), s % (HEADS // 2), s % 2
                    if s + 1 < NS:
                        scores(s + 1)
                    pe.wait_ge(S["pexp"], b * NS + s + 1)
                    if s >= 1:
                        pe.wait_ge(S["pta"], b * NS + s)
                        if (s - 1) // (HEADS // 2) >= 2:
                            pe.wait_ge(S["ptb"], b * (NS // 2) + s - NS // 2)
                    for j in range(i + 1):
                        for e in range(2):
                            q = 2 * j + e
                            last = tr(ps[:, 4 + q // 4, (q % 4) * P:(q % 4 + 1) * P], prob[:, u, e, j * P:(j + 1) * P], ident)
                    last.then_inc(S["pt"], 1)
                    pe.wait_ge(S["pta"], b * NS + s + 1)
                    if i >= 2:
                        pe.wait_ge(S["ptb"], b * (NS // 2) + s + 1 - NS // 2)
                        if hp == 0:
                            pe.wait_ge(S["attd"], b * TPB + i - 1)
                    for e in range(2):
                        cols = slice((2 * hp + e) * HD, (2 * hp + e + 1) * HD)
                        for j in range(i + 1):
                            last = mm(ps[:, 6 + i % 2, cols], prob_t[:, u, 2 * j + e, :], v_sb[:, j, cols], start=(j == 0), stop=(j == i))
                    last.then_inc(S["pv"], 1)

                for t in range(TPB):
                    pe.wait_ge(S["attd"], b * TPB + t + 1)
                    if t >= 2:
                        pe.wait_ge(S["oproj"], b * TPB + t - 1)
                    four(t % 2, att[:, t, :]).then_inc(S["at"], 1)
                    pe.wait_ge(S["ats"], b * TPB + t + 1)
                    if t >= 2:
                        pe.wait_ge(S["hres"], b * TPB + t - 1)
                    for k in range(DC):
                        last = mm(ps[:, 2 + t % 2, :], att_t[:, t % 2, k, :], w_o[:, k, :], start=(k == 0), stop=(k == DC - 1))
                    last.then_inc(S["oproj"], 1)
                for t in range(TPB):
                    pe.wait_ge(S["hn"], b * TPB + t + 1)
                    if t >= 2:
                        pe.wait_ge(S["hnts"], b * TPB + t - 1)
                    four(4 + t % 2, hn[:, t, :]).then_inc(S["hnt"], 1)
                    pe.wait_ge(S["hnts"], b * TPB + t + 1)
                    for k in range(DC):
                        last = mm(ps[:, 6, t * 8:t * 8 + MOE0.routed], hn_t[:, t % 2, k, :], w_rt[:, k, :], start=(k == 0), stop=(k == DC - 1))
                    last.then_inc(S["logit"], 1)
                pe.wait_ge(S["masked"], b + 1)
                places(nc, r, MOE0, c, m, m["before0"], 7).then_inc(S["ranked"], 1)
                pe.wait_ge(S["scattered"], 16 * TPB * MOE0.top * (b + 1))




def mixture(nc, a, m, c, d, moe, before, out):
    ctx = ExitStack()
    with ctx:
        def sb(name, shape, dt=F32):
            return ctx.enter_context(nc.sbuf_tensor(f"{moe.name}_{name}", shape, dt))

        def sem(name):
            return ctx.enter_context(nc.semaphore(f"{moe.name}_{name}"))

        ps = m["psum"]
        E, N, G, I = moe.experts, moe.tiles, moe.groups, moe.inner
        full, n_fc = E * BLOCKS, len(moe.fc)
        ident = c["ident"]
        w_up = sb("w_up", [P, RING * DC, moe.up])
        w_down = sb("w_down", [P, RING * n_fc, D])
        count_i, tiles_of = sb("count_i", [P, E], I32), sb("tiles_of", [P, E])
        ends, starts = sb("ends", [P, E]), sb("starts", [P, E])
        starts_i = sb("starts_i", [1, E], I32)
        at_or_before, begun = sb("at_or_before", [P, G, E]), sb("begun", [P, G])
        first, valid = sb("first", [P, G]), sb("valid", [P, G])
        block_f, block = sb("block_f", [P, G]), sb("block", [P, G], I32)
        pair_i, pair = sb("pair_i", [P, G], I32), sb("pair", [P, G, 2])
        of_tile = sb("of_tile", [1, 2, G * P], I32)
        table = sb("table", [P, G, 2 * P])
        ids, weight = sb("ids", [P, G * P], I32), sb("weight", [P, G * P])
        idx = [sb(f"idx{u}", [P, 1], I32) for u in range(GROUP)]
        rows = [sb(f"rows{u}", [P, D]) for u in range(GROUP)]
        rows_t = [sb(f"rows_t{u}", [P, DC, P]) for u in range(2)]
        gate, hid = [sb(f"gate{u}", [P, I]) for u in range(2)], [sb(f"hid{u}", [P, I]) for u in range(2)]
        hid_t = [sb(f"hid_t{u}", [P, n_fc, P]) for u in range(2)]
        res = [sb(f"res{u}", [P, D]) for u in range(RESULTS)]
        loaded, gathered = m["loaded"], m["gathered"]
        loaded_0 = 0 if moe is MOE0 else MOE0.loads * (MOE0.experts // RING)
        gathered_0 = 0 if moe is MOE0 else 16 * (MOE0.tiles // GROUP)
        S = {n: sem(n) for n in ("counted chain tiled blocks flipped tables listed ready copied rt rts up silu "
                                 "hidden ht hts down res added stored").split()}

        def groups(eng, body):
            n = N // GROUP
            body(0, False)
            with eng.Fori(1, n - 1) as g:
                body(g, False)
            body(n - 1, True)

        block_ = ctx.enter_context(nc.Block())

        @block_.sync
        def _(sp):
            def load(e, u):
                up = w_up[:, u * DC:(u + 1) * DC, :]
                if isinstance(e, int) and e < moe.first:
                    gate_w, up_w, down_w = a["L0_ffn_sh_gate"], a["L0_ffn_sh_up"], a["L0_ffn_sh_down"]
                else:
                    pick = (lambda w: w[e - moe.first]) if isinstance(e, int) else \
                        (lambda w: w[bass.ds(e - moe.first, 1), :, :].rearrange("a d n -> (a d) n"))
                    names = ("L0_ffn_r_gate", "L0_ffn_r_up", "L0_ffn_r_down") if moe is MOE0 else \
                        ("L1_ffn_w_gate", "L1_ffn_w_up", "L1_ffn_w_down")
                    gate_w, up_w, down_w = (pick(a[n]) for n in names)
                sp.dma_start(up[:, :, 0:I], gate_w.rearrange("(c p) n -> p c n", p=P)).then_inc(loaded[u], 16)
                sp.dma_start(up[:, :, I:2 * I], up_w.rearrange("(c p) n -> p c n", p=P)).then_inc(loaded[u], 16)
                for j, (f, w) in enumerate(moe.fc):
                    sp.dma_start(w_down[0:w, u * n_fc + j, :], down_w[f:f + w, :]).then_inc(loaded[u], 16)

            for u in range(RING):
                load(u, u)
            for u in range(RING):
                sp.wait_ge(loaded[u], loaded_0 + moe.loads)
                sp.sem_inc(S["ready"], 1)
            sp.wait_ge(S["tiled"], 1)
            with sp.Fori(1, E // RING) as g:
                for u in range(RING):
                    free = sp.value_load(starts_i[0:1, bass.ds(g * RING + u - RING + 1, 1)], min_val=1, max_val=N)
                    hold(sp, S["down"], free, m["passed"]["sp"])
                    load(g * RING + u, u)
                    sp.wait_ge(loaded[u], loaded_0 + moe.loads * (g + 1))
                    sp.sem_inc(S["ready"], 1)
            if out is not None:
                sp.wait_ge(S["added"], 16 * N)
                sp.dma_start(out.rearrange("b s d -> (b s) d"), d["sum"][0:TOKENS, :]).then_inc(S["stored"], 16)
                sp.wait_ge(S["stored"], 16)

        @block_.gpsimd
        def _(pool):
            g = nc.gpsimd
            pool.wait_ge(S["blocks"], 1)
            table_rows = d["slots"].rearrange("(b p) e -> b (p e)", p=P)
            for j in range(G):
                pool.indirect_dma_start(table[:, j, :], None, table_rows, bass.IndirectOffsetOnAxis(block[:, j:j + 1], 0)).then_inc(S["tables"], 16)
            pool.wait_ge(S["listed"], 1)

            def gather(t, u):
                since(pool, S["added"], 16 * (t - GROUP + 1))
                g.tensor_copy(idx[u][:, :], ids[:, bass.ds(t, 1)]).then_inc(S["copied"], 1)
                pool.wait_ge(S["copied"], t + 1)
                since(pool, S["rt"], t - GROUP + 1)
                pool.sem_inc(m["passed"]["pool"], 1)
                pool.indirect_dma_start(rows[u][:, :], None, d["rows"], bass.IndirectOffsetOnAxis(idx[u][:, :], 0)).then_inc(gathered[u], 16)

            def tiles(g, last):
                for u in range(GROUP):
                    t = g * GROUP + u
                    if not last or u < GROUP - AHEAD:
                        gather(t + AHEAD, (u + AHEAD) % GROUP)
                    pool.wait_ge(S["res"], t + 1)
                    since(pool, S["added"], 16 * t)
                    pool.sem_inc(m["passed"]["pool"], 1)
                    pool.indirect_dma_start(d["sum"], bass.IndirectOffsetOnAxis(idx[u][:, :], 0), res[u % RESULTS][:, :], None,
                                            compute_op=ALU.add).then_inc(S["added"], 16)

            for t in range(AHEAD):
                gather(t, t)
            groups(pool, tiles)
            pool.wait_ge(S["added"], 16 * N)

        @block_.scalar
        def _(act):
            sc = nc.scalar

            def flip(t, u):
                i = u % 2
                act.wait_ge(S["rt"], t + 1)
                since(act, S["up"], t - 1)
                sc.activation(rows_t[i][:, :, :].rearrange("p c q -> p (c q)"), ps[:, i, :], ACT.Copy).then_inc(S["rts"], 1)

            def silu(t, u):
                i = u % 2
                act.wait_ge(S["up"], t + 1)
                since(act, S["hidden"], t - 1)
                sc.activation(gate[i][:, :], ps[:, 2 + i, 0:I], ACT.Silu).then_inc(S["silu"], 1)

            def tiles(g, last):
                for u in range(GROUP):
                    i, t = u % 2, g * GROUP + u
                    if not last or u < GROUP - 2:
                        flip(t + 2, u)
                    if not last or u < GROUP - 1:
                        silu(t + 1, u + 1)
                    act.wait_ge(S["down"], t + 1)
                    since(act, S["added"], 16 * (t - RESULTS + 1))
                    sc.activation(res[u % RESULTS][:, :], ps[:, 5 + i, :], ACT.Copy, scale=weight[:, bass.ds(t, 1)]).then_inc(S["res"], 1)

            act.wait_ge(S["listed"], 1)
            flip(0, 0)
            flip(1, 1)
            silu(0, 0)
            groups(act, tiles)

        @block_.vector
        def _(dve):
            v = nc.vector
            own = Steps(dve, S["chain"])
            dve.wait_ge(S["counted"], 1)
            if moe.first:
                own.did(v.memset(tiles_of[:, 0:moe.first], float(BLOCKS)))
            own.run(v.tensor_scalar(count_i[:, 0:moe.routed], ps[:, 0, 0:moe.routed], float(P - 1), None, ALU.add))
            own.run(v.tensor_scalar(count_i[:, 0:moe.routed], count_i[:, 0:moe.routed], P.bit_length() - 1, None, ALU.logical_shift_right))
            own.run(v.tensor_scalar(tiles_of[:, moe.first:E], count_i[:, 0:moe.routed], 1.0, None, ALU.max))
            own.run(v.tensor_tensor_scan(ends[:, :], m["ones"][:, 0:E], tiles_of[:, :], 0.0, ALU.mult, ALU.add))
            own.run(v.tensor_tensor(starts[:, :], ends[:, :], tiles_of[:, :], ALU.subtract))
            v.tensor_copy(starts_i[:, :], starts[0:1, :]).then_inc(S["tiled"], 1)
            for j in range(G):
                t = c["tile"][:, j:j + 1]
                own.run(v.tensor_scalar(at_or_before[:, j, :], starts[:, :], t, None, ALU.is_le, ALU.add, accum_out=begun[:, j:j + 1]))
                own.run(v.tensor_tensor(at_or_before[:, j, :], at_or_before[:, j, :], starts[:, :], ALU.mult))
                own.run(v.tensor_reduce(first[:, j:j + 1], at_or_before[:, j, :], AX.X, ALU.max))
                own.did(v.tensor_tensor(valid[:, j:j + 1], t, ends[:, E - 1:E], ALU.is_lt))
                own.run(v.tensor_tensor(first[:, j:j + 1], t, first[:, j:j + 1], ALU.subtract))
                own.run(v.scalar_tensor_tensor(block_f[:, j:j + 1], begun[:, j:j + 1], float(BLOCKS), first[:, j:j + 1], ALU.mult, ALU.add))
                own.run(v.scalar_tensor_tensor(block_f[:, j:j + 1], block_f[:, j:j + 1], -float(BLOCKS + full), valid[:, j:j + 1], ALU.add, ALU.mult))
            own.did(v.tensor_scalar(pair_i[:, :], begun[:, :], -1.0, None, ALU.add))
            v.tensor_scalar(block[:, :], block_f[:, :], float(full), None, ALU.add).then_inc(S["blocks"], 1)
            own.wait()
            own.run(v.tensor_scalar(pair_i[:, :], pair_i[:, :], RING - 1, None, ALU.bitwise_and))
            own.did(v.tensor_copy(pair[:, :, 0], pair_i[:, :]))
            v.tensor_copy(pair[:, :, 1], begun[:, :]).then_inc(S["tiled"], 1)
            dve.wait_ge(S["flipped"], 1)
            for j in range(G):
                own.did(v.tensor_copy(ids[:, j * P:(j + 1) * P], ps[:, 1 + 2 * j, 0:P]))
                own.did(v.tensor_scalar(weight[:, j * P:(j + 1) * P], ps[:, 2 + 2 * j, 0:P], 1.0 / moe.scaling, None, ALU.mult))
            own.wait()
            v.tensor_copy(of_tile[:, :, :].rearrange("p a t -> p (a t)"), ps[0:1, 5, 0:2 * G * P]).then_inc(S["listed"], 1)

            def flip(t, u):
                i = u % 2
                dve.wait_ge(S["ht"], t + 1)
                since(dve, S["down"], t - 1)
                if I % P == 0:
                    last = v.tensor_copy(hid_t[i][:, :, :].rearrange("p c q -> p (c q)"), ps[:, 4, 0:n_fc * P])
                else:
                    for j, (f, w) in enumerate(moe.fc):
                        last = v.tensor_copy(hid_t[i][0:w, j, :], ps[0:w, 4, j * P:(j + 1) * P])
                last.then_inc(S["hts"], 1)

            def tiles(g, last):
                for u in range(GROUP):
                    i, t = u % 2, g * GROUP + u
                    dve.wait_ge(S["silu"], t + 1)
                    since(dve, S["ht"], t - 1)
                    v.tensor_tensor(hid[i][:, :], gate[i][:, :], ps[:, 2 + i, I:2 * I], ALU.mult).then_inc(S["hidden"], 1)
                    flip(t, u)

            groups(dve, tiles)

        @block_.tensor
        def _(pe):
            mm, tr = nc.tensor.matmul, nc.tensor.transpose
            mm(ps[:, 0, 0:moe.routed], m["ones"][:, :], before[:, TPB, :], start=True, stop=True).then_inc(S["counted"], 1)
            pe.wait_ge(S["tiled"], 2)
            pe.wait_ge(S["tables"], 16 * G)
            for j in range(G):
                for e in range(2):
                    tr(ps[:, 1 + 2 * j + e, 0:P], table[:, j, :].rearrange("p (s e) -> p e s", e=2)[:, e, :], ident)
            for e in range(2):
                for j in range(G):
                    last = mm(ps[0:1, 5, (e * G + j) * P:(e * G + j + 1) * P], pair[:, j, e:e + 1], ident, start=True, stop=True)
            last.then_inc(S["flipped"], 1)
            pe.wait_ge(S["listed"], 1)

            def flip(g, u):
                i, t = u % 2, g * GROUP + u
                pe.wait_ge(gathered[u], gathered_0 + 16 * (g + 1))
                since(pe, S["rts"], t - 1)
                for k in range(DC):
                    last = tr(ps[:, i, k * P:(k + 1) * P], rows[u][:, k * P:(k + 1) * P], ident)
                last.then_inc(S["rt"], 1)

            def load(what, t, least, most):
                return pe.value_load(of_tile[0:1, what, bass.ds(t, 1)], min_val=least, max_val=most)

            def up(g, u, at, needed):
                i, t = u % 2, g * GROUP + u
                pe.wait_ge(S["ready"], needed)
                pe.wait_ge(S["rts"], t + 1)
                since(pe, S["hidden"], t - 1)
                for k in range(DC):
                    last = mm(ps[:, 2 + i, 0:2 * I], rows_t[i][:, k, :], w_up[:, bass.ds(at * DC + k, 1), :].rearrange("p a n -> p (a n)"),
                              start=(k == 0), stop=(k == DC - 1))
                last.then_inc(S["up"], 1)

            def tiles(g, last):
                at = load(0, g * GROUP, 0, RING - 1)
                for u in range(GROUP):
                    i, t = u % 2, g * GROUP + u
                    more, over = divmod(u + 1, GROUP)
                    if not last or u < GROUP - 1:
                        at_next, needed = load(0, t + 1, 0, RING - 1), load(1, t + 1, 1, E)
                    pe.wait_ge(S["hidden"], t + 1)
                    since(pe, S["hts"], t)
                    for j, (f, w) in enumerate(moe.fc):
                        done = tr(ps[0:w, 4, j * P:(j + 1) * P], hid[i][:, f:f + w], ident)
                    done.then_inc(S["ht"], 1)
                    if not last or u < GROUP - 2:
                        flip(g + (u + 2) // GROUP, (u + 2) % GROUP)
                    if not last or u < GROUP - 1:
                        up(g + more, over, at_next, needed)
                    pe.wait_ge(S["hts"], t + 1)
                    since(pe, S["res"], t - 1)
                    for j, (f, w) in enumerate(moe.fc):
                        done = mm(ps[:, 5 + i, :], hid_t[i][0:w, j, :], w_down[0:w, bass.ds(at * n_fc + j, 1), :].rearrange("p a n -> p (a n)"),
                                  start=(j == 0), stop=(j == n_fc - 1))
                    done.then_inc(S["down"], 1)
                    at = at_next

            flip(0, 0)
            flip(0, 1)
            up(0, 0, load(0, 0, 0, RING - 1), load(1, 0, 1, E))
            groups(pe, tiles)




def middle(nc, a, m, c, dram):
    ctx = ExitStack()
    with ctx:
        def sb(name, shape, dt=F32):
            return ctx.enter_context(nc.sbuf_tensor("m_" + name, shape, dt))

        def sem(name):
            return ctx.enter_context(nc.semaphore("m_" + name))

        ps, x, ctx_sb = m["psum"], m["x"], m["ctx"]
        N = MOE1.routed
        w_rt = sb("w_rt", [P, DC, N])
        mask_u8, mask, barred = sb("mask_u8", [P, BATCH, KEYS], U8), sb("mask", [P, BATCH, KEYS]), sb("barred", [P, BATCH, KEYS])
        any_key = sb("any_key", [P, BATCH])
        stats, mv, rstd, var_e = sb("stats", [P, TPB, 6]), sb("mv", [P, TPB, 2]), sb("rstd", [P, TPB]), sb("var_e", [P, TPB])
        xn, xn_t = sb("xn", [P, TPB, D]), sb("xn_t", [P, DC, SEQ])
        att, top, den = sb("att", [P, TPB, KEYS]), sb("top", [P, TPB]), sb("den", [P, TPB])
        att_t = sb("att_t", [KEYS, TPB, P])
        x3, hn, hn_t = sb("x3", [P, TPB, D]), sb("hn", [P, TPB, D]), sb("hn_t", [P, 2, DC, P])
        top_l, sum_l = sb("top_l", [P, TPB]), sb("sum_l", [P, TPB])
        r = route_memory(sb, MOE1)
        names = ("w mask x_in var rstd xn xt xts s shift e p pt pts o x3 var2 rstd2 hn hnt hnts logit lsh le masked ranked "
                 "slotted scattered rows_out dve").split()
        S = {n: sem(n) for n in names}
        r0, r1 = dram["moe0"], dram["moe1"]
        block = ctx.enter_context(nc.Block())

        @block.sync
        def _(sp):
            sp.dma_start(mask_u8[:, :, :].rearrange("p b k -> p (b k)"), a["mask_BxS2_bk0"].rearrange("b k -> (b k)").partition_broadcast(P)).then_inc(S["mask"], 16)
            for b in range(BATCH):
                sp.dma_start(x[:, b * TPB:(b + 1) * TPB, :], r0["sum"][b * SEQ:(b + 1) * SEQ, :].rearrange("(t p) d -> p t d", p=P)).then_inc(S["x_in"], 16)
            sp.dma_start(w_rt[:, :, :], a["L1_router_t"].rearrange("(c p) n -> p c n", p=P)).then_inc(S["w"], 16)
            with sp.Fori(0, BATCH) as b:
                sp.wait_ge(S["x3"], TPB * (b + 1))
                sp.dma_start(r1["sum"][bass.ds(b * SEQ, SEQ), :].rearrange("(t p) d -> p t d", p=P), x3[:, :, :]).then_inc(S["rows_out"], 16)
                sp.wait_ge(S["hn"], TPB * (b + 1))
                sp.dma_start(r1["rows"][bass.ds(b * SEQ, SEQ), :].rearrange("(t p) d -> p t d", p=P), hn[:, :, :]).then_inc(S["rows_out"], 16)
                hold(sp, S["rows_out"], 32 * (b + 1), m["passed"]["sp"])

        @block.gpsimd
        def _(pool):
            g = nc.gpsimd
            with pool.Fori(0, BATCH) as b:
                pool.wait_ge(S["var"], b + 1)
                g.tensor_tensor(rstd[:, :], var_e[:, :], m["power"][:, 0:TPB], ALU.pow).then_inc(S["rstd"], 1)
                pool.wait_ge(S["var2"], b + 1)
                g.tensor_tensor(rstd[:, :], var_e[:, :], m["power"][:, 0:TPB], ALU.pow).then_inc(S["rstd2"], 1)
                hold(pool, S["slotted"], b + 1, m["passed"]["pool"])
                scatter(pool, r, MOE1, r1["slots"], S["scattered"])
                pool.wait_ge(S["scattered"], 16 * TPB * MOE1.top * (b + 1))

        @block.scalar
        def _(act):
            sc = nc.scalar
            with act.Fori(0, BATCH) as b:
                for t in range(TPB):
                    act.wait_ge(S["xt"], b * TPB + t + 1)
                    sc.activation(xn_t[:, :, t * P:(t + 1) * P], ps[:, t, :].rearrange("p (c q) -> p c q", q=P), ACT.Copy).then_inc(S["xts"], 1)
                act.wait_ge(S["shift"], b + 1)
                sc.activation(att[:, :, :], att[:, :, :], ACT.Exp).then_inc(S["e"], 1)
                act.wait_ge(S["pt"], b + 1)
                sc.activation(att_t[:, :, :].rearrange("p t q -> p (t q)"), ps[0:KEYS, 5, :], ACT.Copy).then_inc(S["pts"], 1)
                for t in range(TPB):
                    act.wait_ge(S["hnt"], b * TPB + t + 1)
                    if t >= 2:
                        act.wait_ge(S["logit"], b * TPB + t - 1)
                    sc.activation(hn_t[:, t % 2, :, :].rearrange("p c q -> p (c q)"), ps[:, t % 2, :], ACT.Copy).then_inc(S["hnts"], 1)
                act.wait_ge(S["lsh"], b + 1)
                sc.activation(r["logit"][:, :, :], r["logit"][:, :, :], ACT.Exp).then_inc(S["le"], 1)

        DVE_STEPS = 51

        @block.vector
        def _(dve):
            v = nc.vector
            pre = Steps(dve, S["masked"])
            dve.wait_ge(S["mask"], 16)
            pre.run(v.tensor_copy(mask[:, :, :], mask_u8[:, :, :]))
            pre.did(v.tensor_scalar(barred[:, :, :], mask[:, :, :], 1.0, 1e30, ALU.subtract, ALU.mult))
            pre.did(v.tensor_reduce(any_key[:, :], mask[:, :, :], AX.X, ALU.max))
            pre.wait()
            dve.wait_ge(S["x_in"], 16 * BATCH)
            with dve.Fori(0, BATCH) as b:
                own = Steps(dve, S["dve"], b * DVE_STEPS, m["passed"]["dve"])

                def stats_of(src, t):
                    own.did(v.bn_stats(stats[:, t, :], src))
                    own.hold()
                    own.did(v.bn_aggr(mv[:, t, :], stats[:, t, :]))

                for t in range(TPB):
                    stats_of(tile_at(x, b * TPB + t), t)
                own.wait()
                v.tensor_scalar(var_e[:, :], mv[:, :, 1], EPS, None, ALU.add).then_inc(S["var"], 1)
                dve.wait_ge(S["rstd"], b + 1)
                for t in range(TPB):
                    v.tensor_scalar(xn[:, t, :], tile_at(x, b * TPB + t), mv[:, t, 0:1], rstd[:, t:t + 1], ALU.subtract, ALU.mult).then_inc(S["xn"], 1)
                dve.wait_ge(S["s"], b + 1)
                s2 = ps[:, 4, 0:TPB * KEYS].rearrange("p (t k) -> p t k", k=KEYS)
                own.run(v.scalar_tensor_tensor(att[:, :, :], s2, D ** -0.5, mask[:, bass.ds(b, 1), :].to_broadcast([P, TPB, KEYS]), ALU.mult, ALU.mult))
                own.run(v.tensor_tensor(att[:, :, :], att[:, :, :], barred[:, bass.ds(b, 1), :].to_broadcast([P, TPB, KEYS]), ALU.add))
                own.run(v.tensor_reduce(top[:, :], att[:, :, :], AX.X, ALU.max))
                v.tensor_tensor(att[:, :, :], att[:, :, :], top[:, :].unsqueeze(2).to_broadcast([P, TPB, KEYS]), ALU.subtract).then_inc(S["shift"], 1)
                dve.wait_ge(S["e"], b + 1)
                own.run(v.tensor_reduce(den[:, :], att[:, :, :], AX.X, ALU.add))
                own.run(v.reciprocal(den[:, :], den[:, :]))
                own.run(v.tensor_scalar(den[:, :], den[:, :], any_key[:, bass.ds(b, 1)], None, ALU.mult))
                v.tensor_tensor(att[:, :, :], att[:, :, :], den[:, :].unsqueeze(2).to_broadcast([P, TPB, KEYS]), ALU.mult).then_inc(S["p"], 1)
                for t in range(TPB):
                    dve.wait_ge(S["o"], b * TPB + t + 1)
                    v.tensor_tensor(x3[:, t, :], tile_at(x, b * TPB + t), ps[:, 6 + t % 2, :], ALU.add).then_inc(S["x3"], 1)
                    hold(dve, S["x3"], b * TPB + t + 1, m["passed"]["dve"])
                    stats_of(x3[:, t, :], t)
                own.wait()
                v.tensor_scalar(var_e[:, :], mv[:, :, 1], EPS, None, ALU.add).then_inc(S["var2"], 1)
                dve.wait_ge(S["rstd2"], b + 1)
                for t in range(TPB):
                    v.tensor_scalar(hn[:, t, :], x3[:, t, :], mv[:, t, 0:1], rstd[:, t:t + 1], ALU.subtract, ALU.mult).then_inc(S["hn"], 1)
                dve.wait_ge(S["logit"], TPB * (b + 1))
                lg = ps[:, 2, 0:TPB * N].rearrange("p (t e) -> p t e", e=N)
                own.run(v.tensor_reduce(top_l[:, :], lg, AX.X, ALU.max))
                v.tensor_tensor(r["logit"][:, :, :], lg, top_l[:, :].unsqueeze(2).to_broadcast([P, TPB, N]), ALU.subtract).then_inc(S["lsh"], 1)
                dve.wait_ge(S["le"], b + 1)
                own.run(v.tensor_reduce(sum_l[:, :], r["logit"][:, :, :], AX.X, ALU.add))
                own.run(v.reciprocal(sum_l[:, :], sum_l[:, :]))
                own.run(v.tensor_tensor(r["prob"][:, :, :], r["logit"][:, :, :], sum_l[:, :].unsqueeze(2).to_broadcast([P, TPB, N]), ALU.mult))
                token = c["token"][:, bass.ds(b * TPB, TPB)]
                choose(nc, own, r, MOE1, c, token, m["before1"], S["masked"])
                dve.wait_ge(S["ranked"], b + 1)
                slots(nc, own, r, MOE1, c, m, m["before1"], 3, c["offset1"]).then_inc(S["slotted"], 1)
                dve.wait_ge(S["scattered"], 16 * TPB * MOE1.top * (b + 1))
                dve.wait_ge(S["rows_out"], 32 * (b + 1))
                assert own.n == DVE_STEPS, own.n

        @block.tensor
        def _(pe):
            mm, tr = nc.tensor.matmul, nc.tensor.transpose
            ident = c["ident"]
            pe.wait_ge(S["w"], 16)
            with pe.Fori(0, BATCH) as b:
                def four(bank, src):
                    for k in range(DC):
                        last = tr(ps[:, bank, k * P:(k + 1) * P], src[:, k * P:(k + 1) * P], ident)
                    return last

                for t in range(TPB):
                    pe.wait_ge(S["xn"], b * TPB + t + 1)
                    four(t, xn[:, t, :]).then_inc(S["xt"], 1)
                for t in range(TPB):
                    pe.wait_ge(S["xts"], b * TPB + t + 1)
                    for k in range(DC):
                        last = mm(ps[:, 4, t * KEYS:(t + 1) * KEYS], xn_t[:, k, t * P:(t + 1) * P],
                                  m["ctx_t"][:, bass.ds(b, 1), k, :].rearrange("p a n -> p (a n)"), start=(k == 0), stop=(k == DC - 1))
                last.then_inc(S["s"], 1)
                hold(pe, S["p"], b + 1, m["passed"]["pe"])
                for t in range(TPB):
                    last = tr(ps[0:KEYS, 5, t * P:(t + 1) * P], att[:, t, :], ident)
                last.then_inc(S["pt"], 1)
                hold(pe, S["pts"], b + 1, m["passed"]["pe"])
                for t in range(TPB):
                    if t >= 2:
                        hold(pe, S["x3"], b * TPB + t - 1, m["passed"]["pe"])
                    mm(ps[:, 6 + t % 2, :], att_t[:, t, :], tile_at(ctx_sb, b)[0:KEYS, :], start=True, stop=True).then_inc(S["o"], 1)
                for t in range(TPB):
                    pe.wait_ge(S["hn"], b * TPB + t + 1)
                    if t >= 2:
                        pe.wait_ge(S["hnts"], b * TPB + t - 1)
                    four(t % 2, hn[:, t, :]).then_inc(S["hnt"], 1)
                    pe.wait_ge(S["hnts"], b * TPB + t + 1)
                    for k in range(DC):
                        last = mm(ps[:, 2, t * N:(t + 1) * N], hn_t[:, t % 2, k, :], w_rt[:, k, :], start=(k == 0), stop=(k == DC - 1))
                    last.then_inc(S["logit"], 1)
                pe.wait_ge(S["masked"], 3 + b + 1)
                places(nc, r, MOE1, c, m, m["before1"], 3).then_inc(S["ranked"], 1)
                pe.wait_ge(S["scattered"], 16 * TPB * MOE1.top * (b + 1))



_INS = ["x", "ctx_2048", "mask_BxS2_bk0", "L0_ffn_ln1_w", "L0_ffn_ln2_w", "L0_ffn_kv_d_w", "L0_ffn_q_d_w", "L0_ffn_k_u_w",
        "L0_ffn_v_u_w", "L0_ffn_q_u_w", "L0_ffn_rope_k_w", "L0_ffn_rope_q_w", "L0_ffn_o_w", "L0_ffn_sh_gate", "L0_ffn_sh_up",
        "L0_ffn_sh_down", "L0_ffn_r_gate", "L0_ffn_r_up", "L0_ffn_r_down", "L0_ffn_router_w", "L0_ffn_router_b",
        "L1_ffn_router_w", "L1_ffn_w_gate", "L1_ffn_w_up", "L1_ffn_w_down"]


def constants():
    import numpy as np

    f = np.float32
    row, col = np.arange(P)[:, None], np.arange(P)[None, :]
    angle = np.outer(np.arange(SEQ, dtype=f), (1.0 / 10000.0 ** (np.arange(0, ROT, 2, dtype=f) / f(ROT))).astype(f)).astype(f)
    cos, sin = np.cos(angle).astype(f), np.sin(angle).astype(f)
    by_tile = lambda t: t.reshape(TPB, P, -1).transpose(1, 0, 2).reshape(P, -1)
    seen = np.arange(KEYS)[None, :] <= np.arange(SEQ - P, SEQ)[:, None] + KEYS - SEQ
    parts = {
        "ident": np.eye(P), "earlier": row < col, "future": np.where(col <= row, 0.0, -1e38),
        "allowed": seen, "barred": np.where(seen, 0.0, -10000.0),
        "cos": by_tile(np.concatenate([cos, cos], 1)), "sin": by_tile(sin),
        "expert": np.tile(np.arange(32), (P, 1)),
        "offset0": np.tile((np.arange(8) + MOE0.first) * TOKENS, (P, 1)),
        "offset1": np.tile(np.arange(32) * TOKENS, (P, 1)),
        "token": row + P * np.arange(TILES)[None, :], "tile": row + P * np.arange(2)[None, :],
    }
    out = {"const": np.concatenate([np.asarray(parts[k], f) for k in CONST], 1), "zero_rows": np.zeros((SPARE, D), f)}
    for moe in (MOE0, MOE1):
        empty = np.zeros((moe.blocks, P, 2), f)
        empty[:, :, 0] = TOKENS + np.arange(P)
        for e in range(moe.first):
            part = empty[e * BLOCKS:(e + 1) * BLOCKS]
            part[:, :, 0] = np.arange(TOKENS).reshape(BLOCKS, P)
            part[:, :, 1] = 1.0
        out[moe.name + "_empty"] = empty.reshape(moe.blocks, 2 * P)
    return out


def kernel(**inputs):
    import numpy as np
    import concourse.bacc as bacc
    from concourse.bass_utils import run_bass_kernel_spmd

    nc = bacc.Bacc("TRN2", target_bir_lowering=False, num_devices=1)
    arrays = {n: np.ascontiguousarray(inputs[n]) for n in _INS}
    arrays["L1_router_t"] = np.ascontiguousarray(arrays.pop("L1_ffn_router_w").T)
    arrays.update(constants())
    aps = {n: nc.dram_tensor(f"in_{n}", v.shape, mybir.dt.from_np(v.dtype), kind="ExternalInput").ap() for n, v in arrays.items()}
    out = nc.dram_tensor("out", (BATCH, SEQ, D), F32, kind="ExternalOutput").ap()
    build(nc, aps, out)
    r = run_bass_kernel_spmd(nc, [{f"in_{n}": v for n, v in arrays.items()}], core_ids=[0])
    return r.results[0]["out"]
```

```python
from contextlib import ExitStack

import concourse.bass as bass
from concourse import mybir

F32, BF16, I32, U32, U8 = mybir.dt.float32, mybir.dt.bfloat16, mybir.dt.int32, mybir.dt.uint32, mybir.dt.uint8
ALU, ACT, AX = mybir.AluOpType, mybir.ActivationFunctionType, mybir.AxisListType

P = 128
BATCH, SEQ, D = 4, 512, 512
TOKENS = BATCH * SEQ
TILES = TOKENS // P
TPB = SEQ // P
DC = D // P
KEYS = 64
HEADS, HD = 16, 32
ROT = HD // 2
LAT = 128
EPS = 1e-5
SPARE = P
BLOCKS = TOKENS // P
RING = 4
GROUP = 8
RESULTS = 4
AHEAD = 4

QUERY_ORDER = (3, 0, 2, 1)
STEPS = [(i, hp) for pair in (QUERY_ORDER[0:2], QUERY_ORDER[2:4]) for hp in range(HEADS // 2) for i in pair]
NS = len(STEPS)


def tiles_through(s):
    return sum(hp == HEADS // 2 - 1 for _, hp in STEPS[:max(0, s - 1)])


def wide_steps(s):
    return sum(i >= 2 for i, _ in STEPS[:s])


CONST = {}
_at = 0
for _name, _n in [("ident", P), ("earlier", P), ("future", P), ("allowed", KEYS), ("barred", KEYS),
                  ("cos", TPB * ROT), ("sin", TPB * ROT // 2), ("expert", 32), ("offset0", 8),
                  ("offset1", 32), ("token", TILES), ("tile", 2)]:
    CONST[_name] = (_at, _at + _n)
    _at += _n
CONST_COLS = _at


class Moe:

    def __init__(self, name, experts, routed, top, inner, scaling):
        self.name, self.experts, self.routed, self.top = name, experts, routed, top
        self.first = experts - routed
        self.inner, self.scaling = inner, scaling
        self.blocks = experts * BLOCKS + 1
        most = self.first * BLOCKS + (TOKENS * top) // P + routed
        self.tiles = -(-most // GROUP) * GROUP
        self.groups = -(-self.tiles // P)
        self.fc = [(f, min(P, inner - f)) for f in range(0, inner, P)]
        self.loads = 16 * (2 + len(self.fc))
        self.up = 2 * inner
        self.cols = DC * self.up + len(self.fc) * D


MOE0 = Moe("moe0", 8, 7, 2, 256, 8.0)
MOE1 = Moe("moe1", 32, 32, 8, 192, 1.0)


class Steps:

    def __init__(self, eng, sem, base=0, passed=None):
        self.eng, self.sem, self.base, self.passed, self.n = eng, sem, base, passed, 0

    def did(self, ins):
        ins.then_inc(self.sem, 1)
        self.n += 1

    def wait(self):
        self.eng.wait_ge(self.sem, self.base + self.n)

    def hold(self):
        hold(self.eng, self.sem, self.base + self.n, self.passed)

    def run(self, ins):
        self.did(ins)
        self.wait()


def hold(eng, sem, count, passed):
    eng.wait_ge(sem, count)
    eng.sem_inc(passed, 1)


def since(eng, sem, count):
    if not isinstance(count, int) or count > 0:
        eng.wait_ge(sem, count)


def tile_at(a, i):
    return a[:, bass.ds(i, 1), :].rearrange("p a n -> p (a n)")


def build(nc, a, out, stop=None, debug=None):
    ctx = ExitStack()

    def sb(name, shape, dt=F32):
        return ctx.enter_context(nc.sbuf_tensor(name, shape, dt))

    def sem(name):
        return ctx.enter_context(nc.semaphore(name))

    with ctx:
        m = {
            "x": sb("x_sb", [P, TILES, D]), "const": sb("const_sb", [P, CONST_COLS]),
            "ident16": sb("ident16", [P, P], BF16), "future16": sb("future16", [P, P], BF16),
            "ones": sb("ones", [P, P]), "mean_w": sb("mean_w", [KEYS, P]), "power": sb("power", [P, TILES]), "eps": sb("eps", [P, TILES]),
            "ctx": sb("ctx_sb", [P, BATCH, D]), "ctx_t": sb("ctx_t", [P, BATCH, DC, KEYS]),
            "psum": ctx.enter_context(nc.psum_tensor("psum", [P, 8, 512], F32)),
            "before0": sb("before0", [P, TPB + 1, MOE0.routed]),
            "before1": sb("before1", [P, TPB + 1, MOE1.routed]),
        }
        c = {k: m["const"][:, u:v] for k, (u, v) in CONST.items()}
        dram = {}
        for moe in (MOE0, MOE1):
            n = moe.name
            dram[n] = {
                "rows": nc.dram_tensor(f"{n}_rows", (TOKENS + SPARE, D), F32, kind="Internal").ap(),
                "sum": nc.dram_tensor(f"{n}_sum", (TOKENS + SPARE, D), F32, kind="Internal").ap(),
                "slots": nc.dram_tensor(f"{n}_slots", (moe.blocks * P, 2), F32, kind="Internal").ap(),
            }
        s_init = sem("tables_set")
        m["loaded"] = [sem(f"loaded{u}") for u in range(RING)]
        m["gathered"] = [sem(f"gathered{u}") for u in range(GROUP)]
        m["passed"] = {e: sem(f"passed_{e}") for e in ("dve", "pool", "pe", "sp")}
        front(nc, a, m, c, dram, s_init)
        if stop == "front":
            dump(nc, debug, dram["moe0"], m["before0"], MOE0)
            return
        mixture(nc, a, m, c, dram["moe0"], MOE0, m["before0"], None)
        if stop == "moe0":
            dump(nc, debug, dram["moe0"], m["before0"], MOE0)
            return
        middle(nc, a, m, c, dram)
        if stop == "middle":
            dump(nc, debug, dram["moe1"], m["before1"], MOE1)
            return
        mixture(nc, a, m, c, dram["moe1"], MOE1, m["before1"], out)


def dump(nc, debug, d, before, moe):
    with nc.semaphore("dumped") as s, nc.Block() as block:
        @block.sync
        def _(sp):
            sp.dma_start(debug[0], d["rows"]).then_inc(s, 16)
            sp.dma_start(debug[1], d["sum"]).then_inc(s, 16)
            sp.dma_start(debug[2], d["slots"]).then_inc(s, 16)
            sp.dma_start(debug[3], before[:, TPB, :]).then_inc(s, 16)
            sp.wait_ge(s, 64)




def route_memory(sb, moe):
    n, k = moe.routed, moe.top
    return {
        "prob": sb(f"{moe.name}_prob", [P, TPB, max(n, 8)]), "logit": sb(f"{moe.name}_logit", [P, TPB, n]),
        "value": sb(f"{moe.name}_value", [P, TPB, 8]), "index": sb(f"{moe.name}_index", [P, TPB, 8], U32),
        "chosen": sb(f"{moe.name}_chosen", [P, TPB, k]), "total": sb(f"{moe.name}_total", [P, TPB, 1]),
        "hot": sb(f"{moe.name}_hot", [P, TPB * k, n]), "picked": sb(f"{moe.name}_picked", [P, TPB * k, n]),
        "mask": sb(f"{moe.name}_mask", [P, TPB, n]), "place": sb(f"{moe.name}_place", [P, TPB, n]),
        "slot_f": sb(f"{moe.name}_slot_f", [P, TPB * k]), "slot": sb(f"{moe.name}_slot", [P, TPB * k], I32),
        "entry": sb(f"{moe.name}_entry", [P, TPB * k, 2]),
    }


def choose(nc, steps, r, moe, c, token, before, masked):
    v, n, k = nc.vector, moe.routed, moe.top
    steps.hold()
    for t in range(TPB):
        steps.did(v.max(r["value"][:, t, :], r["prob"][:, t, :]))
    steps.hold()
    for t in range(TPB):
        steps.did(v.max_index(r["index"][:, t, :], r["value"][:, t, :], r["prob"][:, t, :]))
    steps.did(v.tensor_reduce(r["total"][:, :, 0], r["value"][:, :, 0:k], AX.X, ALU.add))
    entry = r["entry"][:, :, :].rearrange("p (t k) e -> p t k e", k=k)
    steps.did(v.tensor_copy(entry[:, :, :, 0], token.unsqueeze(2).to_broadcast([P, TPB, k])))
    steps.wait()
    steps.did(v.tensor_copy(r["chosen"][:, :, :], r["index"][:, :, 0:k]))
    steps.did(v.reciprocal(r["total"][:, :, :], r["total"][:, :, :]))
    steps.wait()
    steps.did(v.tensor_tensor(entry[:, :, :, 1], r["value"][:, :, 0:k],
                              r["total"][:, :, :].to_broadcast([P, TPB, k]), ALU.mult))
    chosen = r["chosen"][:, :, :].rearrange("p t k -> p (t k)")
    steps.run(v.tensor_tensor(r["hot"][:, :, :], c["expert"][:, 0:n].unsqueeze(1).to_broadcast([P, TPB * k, n]),
                              chosen.unsqueeze(2).to_broadcast([P, TPB * k, n]), ALU.is_equal))
    steps.run(v.tensor_reduce(r["mask"][:, :, :], r["hot"][:, :, :].rearrange("p (t k) e -> p t e k", k=k),
                              AX.X, ALU.add))
    for t in range(TPB):
        ins = v.tensor_tensor(before[:, t + 1, :], before[:, t, :], r["mask"][:, t, :], ALU.add)
        if t < TPB - 1:
            steps.run(ins)
    ins.then_inc(masked, 1)


def places(nc, r, moe, c, m, before, bank):
    n = moe.routed
    for t in range(TPB):
        o = m["psum"][:, bank, t * n:(t + 1) * n]
        nc.tensor.matmul(o, c["earlier"], r["mask"][:, t, :], start=True, stop=False)
        last = nc.tensor.matmul(o, m["ones"][:, :], before[:, t, :], start=False, stop=True)
    return last


def find_slots(nc, steps, r, moe, c, m, before, bank, offset):
    v, n, k = nc.vector, moe.routed, moe.top
    rank = m["psum"][:, bank, 0:TPB * n].rearrange("p (t e) -> p t e", e=n)
    steps.did(v.tensor_tensor(r["place"][:, :, :], rank, offset.unsqueeze(1).to_broadcast([P, TPB, n]), ALU.add))
    steps.did(v.tensor_copy(before[:, 0, :], before[:, TPB, :]))
    steps.wait()
    hot = r["hot"][:, :, :].rearrange("p (t k) e -> p t k e", k=k)
    picked = r["picked"][:, :, :].rearrange("p (t k) e -> p t k e", k=k)
    for t in range(TPB):
        steps.did(v.tensor_tensor(picked[:, t], hot[:, t], r["place"][:, t, :].unsqueeze(1).to_broadcast([P, k, n]), ALU.mult))
    steps.wait()
    steps.run(v.tensor_reduce(r["slot_f"][:, :], r["picked"][:, :, :], AX.X, ALU.add))


def scatter(pool, r, choices, table, written):
    for j in choices:
        pool.indirect_dma_start(table, bass.IndirectOffsetOnAxis(r["slot"][:, j:j + 1], 0),
                                r["entry"][:, j, :], None).then_inc(written, 16)




def cross(nc, a, m, c, dram, s_init, mv, rstd, rms, weights):
    ctx = ExitStack()
    with ctx:
        def sb(name, shape, dt=F32):
            return ctx.enter_context(nc.sbuf_tensor("c_" + name, shape, dt))

        ps, x, ctx_sb = m["psum"], m["x"], m["ctx"]
        GH = P // HD
        ctx_heads = sb("ctx_heads", [P, BATCH, DC, GH * KEYS])
        ctx_pairs = sb("ctx_pairs", [P, BATCH, HEADS // 2, 2 * HD])
        stats, mv_q, var_q, rstd_q = sb("stats", [P, TILES, 6]), sb("mv_q", [P, BATCH, 2]), sb("var_q", [P, BATCH]), sb("rstd_q", [P, BATCH])
        var = sb("var", [P, TILES])
        xn, xn_t = sb("xn", [P, BATCH, D]), sb("xn_t", [P, BATCH, DC, P])
        mean = sb("mean", [P, BATCH, D])
        att = sb("att", [P, BATCH, HEADS, KEYS])
        top, total = sb("top", [P, BATCH, HEADS]), sb("total", [P, BATCH, HEADS])
        att_t = sb("att_t", [P, BATCH, HEADS // 2, P])
        S = {n: ctx.enter_context(nc.semaphore("c_" + n)) for n in
             ("const x weights ones_set ctxt ctxts means means_out meaned var_q rstd_q xn xnt xnts s shift e p pt pts o "
              "var dve pool").split()}
        m["s_weights"] = S["weights"]
        block = ctx.enter_context(nc.Block())

        @block.sync
        def _(sp):
            sp.dma_start(m["const"][:, :], a["const"]).then_inc(S["const"], 16)
            for half in range(2):
                sp.dma_start(ctx_sb[half * KEYS:(half + 1) * KEYS, :, :],
                             a["ctx_2048"].rearrange("b k d -> k b d")).then_inc(S["const"], 16)
            sp.dma_start(x[:, :, :], a["x"].rearrange("b (t p) d -> p (b t) d", p=P)).then_inc(S["x"], 16)
            for dst, src in weights:
                sp.dma_start(dst, src).then_inc(S["weights"], 16)
            for moe in (MOE0, MOE1):
                d = dram[moe.name]
                sp.dma_start(d["slots"].rearrange("(b p) e -> b (p e)", p=P), a[moe.name + "_empty"]).then_inc(s_init, 16)
                for n in ("rows", "sum"):
                    sp.dma_start(d[n][TOKENS:TOKENS + SPARE, :], a["zero_rows"]).then_inc(s_init, 16)
            sp.wait_ge(S["weights"], 16 * len(weights))
            sp.wait_ge(s_init, 96)

        @block.gpsimd
        def _(pool):
            g = nc.gpsimd
            g.memset(m["ones"][:, :], 1.0)
            g.memset(m["mean_w"][:, :], 1.0 / KEYS)
            g.memset(m["power"][:, :], -0.5)
            g.memset(m["eps"][:, :], EPS)
            g.memset(m["before0"][:, 0, :], 0.0)
            g.memset(m["before1"][:, 0, :], 0.0).then_inc(S["ones_set"], 1)
            pool.wait_ge(S["ones_set"], 1)
            own = Steps(pool, S["pool"])
            pool.wait_ge(S["var_q"], 1)
            g.tensor_tensor(rstd_q[:, :], var_q[:, :], m["power"][:, 0:BATCH], ALU.pow).then_inc(S["rstd_q"], 1)
            for b in range(BATCH):
                pool.wait_ge(S["means_out"], b + 1)
                for t in range(b * TPB, b * TPB + TPB - 1):
                    g.tensor_tensor(x[:, t, :], x[:, t, :], mean[:, b, :], ALU.add).then_inc(S["meaned"], 1)
            pool.wait_ge(S["var"], 1)
            own.run(g.tensor_tensor(rstd[:, :], var[:, :], m["power"][:, :], ALU.pow))
            own.run(g.tensor_tensor(rms[:, :], rstd[:, :], rstd[:, :], ALU.mult))
            own.run(g.tensor_tensor(rms[:, :], rms[:, :], mv[:, :, 1], ALU.mult))
            own.run(g.tensor_tensor(rms[:, :], rms[:, :], m["eps"][:, :], ALU.add))
            own.run(g.tensor_tensor(rms[:, :], rms[:, :], m["power"][:, :], ALU.pow))

        @block.scalar
        def _(act):
            sc = nc.scalar
            for b in range(BATCH):
                act.wait_ge(S["means"], b + 1)
                sc.activation(mean[:, b, :], ps[:, 4 + b, :], ACT.Copy).then_inc(S["means_out"], 1)
            for b in range(BATCH):
                act.wait_ge(S["xnt"], b + 1)
                sc.activation(xn_t[:, b].rearrange("p c q -> p (c q)"), ps[:, b, :], ACT.Copy).then_inc(S["xnts"], 1)
            for b in range(BATCH):
                act.wait_ge(S["shift"], b + 1)
                sc.activation(att[:, b], att[:, b], ACT.Exp).then_inc(S["e"], 1)
            for b in range(BATCH):
                act.wait_ge(S["pt"], b + 1)
                for j in range(2):
                    sc.activation(att_t[:, b, 4 * j:4 * j + 4, :].rearrange("p c q -> p (c q)"), ps[:, 2 * (b % 2) + j, :], ACT.Copy).then_inc(S["pts"], 1)

        @block.vector
        def _(dve):
            v = nc.vector
            own = Steps(dve, S["dve"], 0, m["passed"]["dve"])

            def stats_of(src, t, to):
                own.did(v.bn_stats(stats[:, t, :], src))
                own.hold()
                own.did(v.bn_aggr(to, stats[:, t, :]))

            own.did(v.memset(ctx_heads[:, :, :, :], 0.0))
            own.did(v.memset(ctx_pairs[:, :, :, :], 0.0))
            dve.wait_ge(S["x"], 16)
            for b in range(BATCH):
                stats_of(x[:, b * TPB + TPB - 1, :], b, mv_q[:, b, :])
            own.wait()
            dve.wait_ge(S["ones_set"], 1)
            v.tensor_scalar(var_q[:, :], mv_q[:, :, 1], EPS, None, ALU.add).then_inc(S["var_q"], 1)
            dve.wait_ge(S["const"], 48)
            v.tensor_copy(m["ident16"][:, :], c["ident"])
            v.tensor_copy(m["future16"][:, :], c["future"])
            for b in range(BATCH):
                dve.wait_ge(S["ctxt"], b + 1)
                for g in range(GH):
                    rows = slice(g * HD, (g + 1) * HD)
                    v.tensor_copy(ctx_heads[rows, b, :, g * KEYS:(g + 1) * KEYS],
                                  ps[rows, b, 0:DC * KEYS].rearrange("p (c k) -> p c k", k=KEYS))
                v.tensor_copy(m["ctx_t"][:, b, :, :], ps[:, b, 0:DC * KEYS].rearrange("p (c k) -> p c k", k=KEYS)).then_inc(S["ctxts"], 1)
            dve.wait_ge(S["rstd_q"], 1)
            for b in range(BATCH):
                v.tensor_scalar(xn[:, b, :], x[:, b * TPB + TPB - 1, :], mv_q[:, b, 0:1], rstd_q[:, b:b + 1], ALU.subtract, ALU.mult).then_inc(S["xn"], 1)
            pairs = ctx_sb[:, :, :].rearrange("p b (j two e) -> p b j two e", two=2, e=HD)
            for half in range(2):
                rows = slice(half * KEYS, (half + 1) * KEYS)
                for b in range(BATCH):
                    own.did(v.tensor_copy(ctx_pairs[rows, b, :, half * HD:(half + 1) * HD], pairs[rows, b, :, half, :]))
            for b in range(BATCH):
                dve.wait_ge(S["s"], b + 1)
                k = 4 + 2 * (b % 2)
                s2 = ps[:, k:k + 2, :].rearrange("p a (h k) -> p (a h) k", k=KEYS)
                own.run(v.scalar_tensor_tensor(att[:, b], s2, HD ** -0.5, c["allowed"].unsqueeze(1).to_broadcast([P, HEADS, KEYS]), ALU.mult, ALU.mult))
                own.run(v.tensor_tensor(att[:, b], att[:, b], c["barred"].unsqueeze(1).to_broadcast([P, HEADS, KEYS]), ALU.add))
                own.run(v.tensor_reduce(top[:, b, :], att[:, b], AX.X, ALU.max))
                v.tensor_tensor(att[:, b], att[:, b], top[:, b, :].unsqueeze(2).to_broadcast([P, HEADS, KEYS]), ALU.subtract).then_inc(S["shift"], 1)
            for b in range(BATCH):
                dve.wait_ge(S["e"], b + 1)
                own.run(v.tensor_reduce(total[:, b, :], att[:, b], AX.X, ALU.add))
                own.run(v.reciprocal(total[:, b, :], total[:, b, :]))
                v.tensor_tensor(att[:, b], att[:, b], total[:, b, :].unsqueeze(2).to_broadcast([P, HEADS, KEYS]), ALU.mult).then_inc(S["p"], 1)
            dve.wait_ge(S["meaned"], BATCH * (TPB - 1))
            for t in range(TILES):
                if t % TPB < TPB - 1:
                    stats_of(x[:, t, :], t, mv[:, t, :])
            for b in range(BATCH):
                dve.wait_ge(S["o"], b + 1)
                t = b * TPB + TPB - 1
                own.did(v.tensor_tensor(x[:, t, :], x[:, t, :], ps[:, 4 + b, :], ALU.add))
                own.hold()
                stats_of(x[:, t, :], t, mv[:, t, :])
            own.wait()
            v.tensor_scalar(var[:, :], mv[:, :, 1], EPS, None, ALU.add).then_inc(S["var"], 1)

        @block.tensor
        def _(pe):
            mm, tr = nc.tensor.matmul, nc.tensor.transpose
            ident = c["ident"]
            pe.wait_ge(S["const"], 48)
            for b in range(BATCH):
                for k in range(DC):
                    last = tr(ps[:, b, k * KEYS:(k + 1) * KEYS], ctx_sb[0:KEYS, b, k * P:(k + 1) * P], ident[0:KEYS, 0:KEYS])
                last.then_inc(S["ctxt"], 1)
            pe.wait_ge(S["ones_set"], 1)
            for b in range(BATCH):
                mm(ps[:, 4 + b, :], m["mean_w"][:, :], ctx_sb[0:KEYS, b, :], start=True, stop=True).then_inc(S["means"], 1)
            pe.wait_ge(S["ctxts"], BATCH)
            for b in range(BATCH):
                pe.wait_ge(S["xn"], b + 1)
                for k in range(DC):
                    last = tr(ps[:, b, k * P:(k + 1) * P], xn[:, b, k * P:(k + 1) * P], ident)
                last.then_inc(S["xnt"], 1)
            pe.wait_ge(S["means_out"], BATCH)
            for b in range(BATCH):
                pe.wait_ge(S["xnts"], b + 1)
                if b >= 2:
                    pe.wait_ge(S["shift"], b - 1)
                for k in range(DC):
                    last = mm(ps[:, 4 + 2 * (b % 2) + k // 2, (k % 2) * 256:(k % 2) * 256 + 256], xn_t[:, b, k, :],
                              ctx_heads[:, b, k, :], start=True, stop=True)
                last.then_inc(S["s"], 1)
            for b in range(BATCH):
                pe.wait_ge(S["p"], b + 1)
                if b >= 2:
                    pe.wait_ge(S["pts"], 2 * (b - 1))
                flat = att[:, b].rearrange("p h k -> p (h k)")
                for j in range(HEADS // 2):
                    last = tr(ps[:, 2 * (b % 2) + j // 4, (j % 4) * P:(j % 4 + 1) * P], flat[:, j * P:(j + 1) * P], ident)
                last.then_inc(S["pt"], 1)
            for b in range(BATCH):
                pe.wait_ge(S["pts"], 2 * (b + 1))
                for j in range(HEADS // 2):
                    last = mm(ps[:, 4 + b, j * 2 * HD:(j + 1) * 2 * HD], att_t[:, b, j, :], ctx_pairs[:, b, j, :], start=True, stop=True)
                last.then_inc(S["o"], 1)




def front(nc, a, m, c, dram, s_init):
    ctx = ExitStack()
    with ctx:
        def sb(name, shape, dt=F32):
            return ctx.enter_context(nc.sbuf_tensor(name, shape, dt))

        def sem(name):
            return ctx.enter_context(nc.semaphore(name))

        ps, x, ctx_sb = m["psum"], m["x"], m["ctx"]
        GH = P // HD
        w_kvd, w_qd = sb("w_kvd", [P, DC, LAT]), sb("w_qd", [P, DC, LAT])
        w_kr = sb("w_kr", [P, DC, D // 2])
        w_q = sb("w_q", [LAT, D])
        w_ku, w_vu = sb("w_ku", [LAT, D // 2]), sb("w_vu", [LAT, D])
        w_o = sb("w_o", [P, DC, D])
        w_rt = sb("w_rt", [P, DC, MOE0.routed])
        bias_rt = sb("bias_rt", [P, MOE0.routed])
        ln1, ln2 = sb("ln1", [P, D]), sb("ln2", [P, D])
        mv, rstd, rms = sb("mv", [P, TILES, 2]), sb("rstd", [P, TILES]), sb("rms", [P, TILES])
        cross(nc, a, m, c, dram, s_init, mv, rstd, rms, [
            (w_kvd[:, :, :], a["L0_ffn_kv_d_w"].rearrange("(c p) n -> p c n", p=P)),
            (w_qd[:, :, :], a["L0_ffn_q_d_w"].rearrange("(c p) n -> p c n", p=P)),
            (w_kr[:, :, :], a["L0_ffn_rope_k_w"].rearrange("(c p) n -> p c n", p=P)),
            (w_q[:, 0:D // 2], a["L0_ffn_q_u_w"]), (w_q[:, D // 2:D], a["L0_ffn_rope_q_w"]),
            (w_ku[:, :], a["L0_ffn_k_u_w"]), (w_vu[:, :], a["L0_ffn_v_u_w"]),
            (w_o[:, :, :], a["L0_ffn_o_w"].rearrange("(c p) n -> p c n", p=P)),
            (w_rt[:, :, :], a["L0_ffn_router_w"].rearrange("(c p) n -> p c n", p=P)),
            (bias_rt[:, :], a["L0_ffn_router_b"].partition_broadcast(P)),
            (ln1[:, :], a["L0_ffn_ln1_w"].partition_broadcast(P)),
            (ln2[:, :], a["L0_ffn_ln2_w"].partition_broadcast(P))])
        stats, mv_h = sb("stats", [P, TPB, 6]), sb("mv_h", [P, TPB, 2])
        var_h, rms_h = sb("var_h", [P, TPB]), sb("rms_h", [P, TPB])
        y, z = sb("y", [P, TPB, D]), sb("z", [P, TPB, D])
        z_t = sb("z_t", [P, DC, SEQ])
        kv_d, q_d = sb("kv_d", [LAT, SEQ]), sb("q_d", [LAT, SEQ])
        v_sb = sb("v_sb", [P, TPB, D])
        qk = sb("qk", [P, 2, 2 * HEADS, HD])
        rot_a, rot_b = sb("rot_a", [P, 2 * HEADS, ROT]), sb("rot_b", [P, 2 * HEADS, ROT])
        q_t, k_t = sb("q_t", [P, HEADS, SEQ]), sb("k_t", [P, DC, SEQ])
        neg_top = sb("neg_top", [P, 2, 2])
        prob = sb("prob", [P, 2, 2, SEQ])
        prob_t = sb("prob_t", [P, 2, 2 * TPB, P])
        den = sb("den", [P, TPB, HEADS])
        over_den, att_t = sb("over_den", [P, HEADS, HD]), sb("att_t", [P, TPB, DC, P])
        ident16, future16 = m["ident16"], m["future16"]
        h, acc, hn = v_sb, y, z
        hn_t = sb("hn_t", [P, 2, DC, P])
        r = route_memory(sb, MOE0)

        names = ("zeroed z zt zts kvd qd kvds qds pp pr pv_ qkp qkr vs qkt qts kts st ntop pexp pt pta ptb pv "
                 "rden rdt rdts attd hres oproj var2 rms2 hn hnt hnts logit lgs lge masked ranked slotted scattered rows_out dve").split()
        S = {n: sem("f_" + n) for n in names}
        r0 = dram["moe0"]

        block = ctx.enter_context(nc.Block())

        @block.sync
        def _(sp):
            with sp.Fori(0, BATCH) as b:
                sp.wait_ge(S["hn"], TPB * (b + 1))
                sp.dma_start(r0["sum"][bass.ds(b * SEQ, SEQ), :].rearrange("(t p) d -> p t d", p=P), acc[:, :, :]).then_inc(S["rows_out"], 16)
                sp.dma_start(r0["rows"][bass.ds(b * SEQ, SEQ), :].rearrange("(t p) d -> p t d", p=P), hn[:, :, :]).then_inc(S["rows_out"], 16)
                hold(sp, S["rows_out"], 32 * (b + 1), m["passed"]["sp"])

        @block.gpsimd
        def _(pool):
            g = nc.gpsimd
            g.memset(q_t[:, :, :], 0.0).then_inc(S["zeroed"], 1)
            g.memset(r["prob"][:, :, :], -1.0).then_inc(S["zeroed"], 1)
            with pool.Fori(0, BATCH) as b:
                pool.wait_ge(S["var2"], b + 1)
                g.tensor_tensor(rms_h[:, :], var_h[:, :], m["power"][:, 0:TPB], ALU.pow).then_inc(S["rms2"], 1)
                hold(pool, S["slotted"], b + 1, m["passed"]["pool"])
                scatter(pool, r, range(TPB * MOE0.top), r0["slots"], S["scattered"])
                pool.wait_ge(S["scattered"], 16 * TPB * MOE0.top * (b + 1))

        def prob_t_second(act, sc, b, s):
            act.wait_ge(S["pt"], b * NS + s + 1)
            if s >= 2:
                act.wait_ge(S["pv"], b * NS + s - 1)
            w = (STEPS[s][0] + 1) * 2 * P - 512
            sc.activation(prob_t[:, s % 2, 4:4 + w // P, :].rearrange("p c q -> p (c q)"), ps[:, 5, 0:w], ACT.Copy).then_inc(S["ptb"], 1)

        @block.scalar
        def _(act):
            sc = nc.scalar
            act.wait_ge(S["zeroed"], 2)
            with act.Fori(0, BATCH) as b:
                for t in range(TPB):
                    act.wait_ge(S["zt"], b * TPB + t + 1)
                    sc.activation(z_t[:, :, t * P:(t + 1) * P], ps[:, t, :].rearrange("p (c q) -> p c q", q=P), ACT.Copy).then_inc(S["zts"], 1)
                act.wait_ge(S["kvd"], b + 1)
                sc.activation(kv_d[:, :], ps[:, 4, :], ACT.Copy).then_inc(S["kvds"], 1)
                for t in range(TPB):
                    i = t % 2
                    act.wait_ge(S["pp"], b * TPB + t + 1)
                    if t >= 2:
                        act.wait_ge(S["qkt"], b * TPB + t - 1)
                    sc.activation(qk[:, i, :, 0:ROT], ps[:, 2 * i, :].rearrange("p (h e) -> p h e", e=ROT), ACT.Copy).then_inc(S["qkp"], 1)
                    act.wait_ge(S["pv_"], b * TPB + t + 1)
                    sc.activation(v_sb[:, t, :], ps[:, 6 + i, :], ACT.Copy).then_inc(S["vs"], 1)
                    act.wait_ge(S["qkt"], b * TPB + t + 1)
                    for g in range(GH):
                        rows = slice(g * HD, (g + 1) * HD)
                        ins = sc.activation(q_t[rows, :, t * P:(t + 1) * P].rearrange("p (c g) q -> p c g q", g=GH)[:, :, g, :],
                                            ps[rows, 4, :].rearrange("p (c q) -> p c q", q=P), ACT.Copy, scale=HD ** -0.5)
                    ins.then_inc(S["qts"], 1)
                for s, (i, hp) in enumerate(STEPS):
                    n, u = (i + 1) * P, s % 2
                    act.wait_ge(S["ntop"], b * NS + s + 1)
                    if s >= 2:
                        act.wait_ge(S["pt"], b * NS + s - 1)
                    for e in range(2):
                        ins = sc.activation(prob[:, u, e, 0:n], ps[:, 2 * u + e, 0:n], ACT.Exp, bias=neg_top[:, u, e:e + 1],
                                            accum_out=den[:, i, 2 * hp + e:2 * hp + e + 1])
                    ins.then_inc(S["pexp"], 1)
                    if s >= 1 and STEPS[s - 1][0] >= 2:
                        prob_t_second(act, sc, b, s - 1)
                if STEPS[NS - 1][0] >= 2:
                    prob_t_second(act, sc, b, NS - 1)
                for t in range(TPB):
                    act.wait_ge(S["hnt"], b * TPB + t + 1)
                    if t >= 2:
                        act.wait_ge(S["logit"], b * TPB + t - 1)
                    sc.activation(hn_t[:, t % 2, :, :].rearrange("p c q -> p (c q)"), ps[:, 4 + t % 2, :], ACT.Copy).then_inc(S["hnts"], 1)
                act.wait_ge(S["lgs"], b + 1)
                sc.activation(r["logit"][:, :, :], r["logit"][:, :, :], ACT.Exp, scale=-1.0).then_inc(S["lge"], 1)

        DVE_STEPS = 64

        @block.vector
        def _(dve):
            v = nc.vector
            dve.wait_ge(S["zeroed"], 2)
            with dve.Fori(0, BATCH) as b:
                own = Steps(dve, S["dve"], b * DVE_STEPS, m["passed"]["dve"])

                def stats_of(src, t):
                    own.did(v.bn_stats(stats[:, t, :], src))
                    own.hold()
                    own.did(v.bn_aggr(mv_h[:, t, :], stats[:, t, :]))

                for t in range(TPB):
                    at = bass.ds(b * TPB + t, 1)
                    own.run(v.tensor_scalar(y[:, t, :], tile_at(x, b * TPB + t), mv[:, at, 0:1].rearrange("p a e -> p (a e)"), rstd[:, at], ALU.subtract, ALU.mult))
                    v.scalar_tensor_tensor(z[:, t, :], y[:, t, :], rms[:, at], ln1[:, :], ALU.mult, ALU.mult).then_inc(S["z"], 1)
                dve.wait_ge(S["qd"], b + 1)
                v.tensor_copy(q_d[:, :], ps[:, 5, :]).then_inc(S["qds"], 1)

                for t in range(TPB):
                    i = t % 2
                    dve.wait_ge(S["pr"], b * TPB + t + 1)
                    src = ps[:, 2 * i + 1, :].rearrange("p (h e) -> p h e", e=ROT)
                    cos = c["cos"][:, t * ROT:(t + 1) * ROT].unsqueeze(1).to_broadcast([P, 2 * HEADS, ROT])
                    sin = c["sin"][:, t * ROT // 2:(t + 1) * ROT // 2].unsqueeze(1).to_broadcast([P, 2 * HEADS, ROT // 2])
                    own.did(v.tensor_tensor(rot_a[:, :, :], src, cos, ALU.mult))
                    own.did(v.tensor_tensor(rot_b[:, :, 0:ROT // 2], src[:, :, ROT // 2:ROT], sin, ALU.mult))
                    own.did(v.tensor_tensor(rot_b[:, :, ROT // 2:ROT], src[:, :, 0:ROT // 2], sin, ALU.mult))
                    own.wait()
                    if t >= 2:
                        dve.wait_ge(S["qkt"], b * TPB + t - 1)
                    own.did(v.tensor_tensor(qk[:, i, :, ROT:ROT + ROT // 2], rot_a[:, :, 0:ROT // 2], rot_b[:, :, 0:ROT // 2], ALU.subtract))
                    v.tensor_tensor(qk[:, i, :, ROT + ROT // 2:HD], rot_a[:, :, ROT // 2:ROT], rot_b[:, :, ROT // 2:ROT], ALU.add).then_inc(S["qkr"], 1)
                    dve.wait_ge(S["qkt"], b * TPB + t + 1)
                    dve.wait_ge(S["qkr"], b * TPB + t + 1)
                    v.tensor_copy(k_t[:, :, t * P:(t + 1) * P], ps[:, 5, :].rearrange("p (c q) -> p c q", q=P)).then_inc(S["kts"], 1)

                def denominators(i, s):
                    dve.wait_ge(S["pexp"], b * NS + s + 1)
                    if QUERY_ORDER[0] != i:
                        dve.wait_ge(S["rdt"], b * TPB + QUERY_ORDER.index(i))
                    own.run(v.reciprocal(den[:, i, :], den[:, i, :]))
                    v.tensor_copy(over_den[:, :, :], den[:, i, :].unsqueeze(2).to_broadcast([P, HEADS, HD])).then_inc(S["rden"], 1)

                def attended(i, s):
                    dve.wait_ge(S["rdt"], b * TPB + QUERY_ORDER.index(i) + 1)
                    v.tensor_copy(att_t[:, i].rearrange("p c q -> p (c q)"), ps[:, 5, :]).then_inc(S["rdts"], 1)
                    dve.wait_ge(S["pv"], b * NS + s + 1)
                    dve.wait_ge(S["rdts"], b * TPB + QUERY_ORDER.index(i) + 1)
                    v.tensor_tensor(att_t[:, i].rearrange("p c q -> p (c q)"), ps[:, 6 + i % 2, :],
                                    att_t[:, i].rearrange("p c q -> p (c q)"), ALU.mult).then_inc(S["attd"], 1)

                def maxima(s):
                    u, n = s % 2, (STEPS[s][0] + 1) * P
                    dve.wait_ge(S["st"], b * NS + s + 1)
                    if s >= 2:
                        dve.wait_ge(S["pexp"], b * NS + s - 1)
                    v.tensor_reduce(neg_top[:, u, :], ps[:, 2 * u:2 * u + 2, 0:n], AX.X, ALU.max, negate=True).then_inc(S["ntop"], 1)

                maxima(0)
                for s in range(NS + 2):
                    if s + 1 < NS:
                        maxima(s + 1)
                    if 1 <= s <= NS:
                        q = s - 1
                        w = min(512, (STEPS[q][0] + 1) * 2 * P)
                        dve.wait_ge(S["pt"], b * NS + q + 1)
                        if q >= 2:
                            dve.wait_ge(S["pv"], b * NS + q - 1)
                        v.tensor_copy(prob_t[:, q % 2, 0:w // P, :].rearrange("p c q -> p (c q)"), ps[:, 4, 0:w]).then_inc(S["pta"], 1)
                    if s >= 2 and STEPS[s - 2][1] == HEADS // 2 - 1:
                        attended(STEPS[s - 2][0], s - 2)
                    if 1 <= s <= NS and STEPS[s - 1][1] == HEADS // 2 - 1:
                        denominators(STEPS[s - 1][0], s - 1)

                for n, t in enumerate(QUERY_ORDER):
                    dve.wait_ge(S["oproj"], b * TPB + n + 1)
                    v.tensor_tensor(h[:, t, :], y[:, t, :], ps[:, n, :], ALU.add).then_inc(S["hres"], 1)
                    dve.wait_ge(S["hres"], b * TPB + n + 1)
                    own.did(v.tensor_tensor(acc[:, t, :], tile_at(x, b * TPB + t), h[:, t, :], ALU.add))
                    stats_of(h[:, t, :], t)
                own.wait()
                own.run(v.tensor_tensor(var_h[:, :], mv_h[:, :, 0], mv_h[:, :, 0], ALU.mult))
                v.scalar_tensor_tensor(var_h[:, :], var_h[:, :], EPS, mv_h[:, :, 1], ALU.add, ALU.add).then_inc(S["var2"], 1)
                dve.wait_ge(S["rms2"], b + 1)
                for t in range(TPB):
                    v.scalar_tensor_tensor(hn[:, t, :], h[:, t, :], rms_h[:, t:t + 1], ln2[:, :], ALU.mult, ALU.mult).then_inc(S["hn"], 1)

                dve.wait_ge(S["logit"], b * TPB + TPB)
                n = MOE0.routed
                v.tensor_tensor(r["logit"][:, :, :], ps[:, 6, 0:TPB * 8].rearrange("p (t e) -> p t e", e=8)[:, :, 0:n],
                                bias_rt[:, :].unsqueeze(1).to_broadcast([P, TPB, n]), ALU.add).then_inc(S["lgs"], 1)
                dve.wait_ge(S["lge"], b + 1)
                own.run(v.tensor_scalar(r["logit"][:, :, :], r["logit"][:, :, :], 1.0, None, ALU.add))
                own.run(v.reciprocal(r["prob"][:, :, 0:n], r["logit"][:, :, :]))
                token = c["token"][:, bass.ds(b * TPB, TPB)]
                choose(nc, own, r, MOE0, c, token, m["before0"], S["masked"])
                dve.wait_ge(S["ranked"], b + 1)
                find_slots(nc, own, r, MOE0, c, m, m["before0"], 7, c["offset0"][:, 0:n])
                v.tensor_copy(r["slot"][:, :], r["slot_f"][:, :]).then_inc(S["slotted"], 1)
                dve.wait_ge(S["scattered"], 16 * TPB * MOE0.top * (b + 1))
                dve.wait_ge(S["rows_out"], 32 * (b + 1))
                assert own.n == DVE_STEPS, own.n

        @block.tensor
        def _(pe):
            mm, tr = nc.tensor.matmul, nc.tensor.transpose
            ident = c["ident"]
            with pe.Fori(0, BATCH) as b:
                def four(bank, src):
                    for k in range(DC):
                        last = tr(ps[:, bank, k * P:(k + 1) * P], src[:, k * P:(k + 1) * P], ident)
                    return last

                for t in range(TPB):
                    pe.wait_ge(S["z"], b * TPB + t + 1)
                    four(t, z[:, t, :]).then_inc(S["zt"], 1)
                pe.wait_ge(S["zts"], TPB * (b + 1))
                for bank, w, done in ((4, w_kvd, "kvd"), (5, w_qd, "qd")):
                    for k in range(DC):
                        last = mm(ps[:, bank, :], w[:, k, :], z_t[:, k, :], start=(k == 0), stop=(k == DC - 1))
                    last.then_inc(S[done], 1)
                pe.wait_ge(S["kvds"], b + 1)
                pe.wait_ge(S["qds"], b + 1)

                def project(t):
                    i, q = t % 2, slice(t * P, (t + 1) * P)
                    if t >= 2:
                        pe.wait_ge(S["vs"], b * TPB + t - 1)
                    mm(ps[:, 2 * i, 0:256], q_d[:, q], w_q[:, 0:256], start=True, stop=True)
                    mm(ps[:, 2 * i, 256:512], kv_d[:, q], w_ku[:, :], start=True, stop=True).then_inc(S["pp"], 1)
                    mm(ps[:, 2 * i + 1, 0:256], q_d[:, q], w_q[:, 256:512], start=True, stop=True)
                    for k in range(DC):
                        last = mm(ps[:, 2 * i + 1, 256:512], z_t[:, k, q], w_kr[:, k, :], start=(k == 0), stop=(k == DC - 1))
                    last.then_inc(S["pr"], 1)
                    mm(ps[:, 6 + i, :], kv_d[:, q], w_vu[:, :], start=True, stop=True).then_inc(S["pv_"], 1)

                project(0)
                for t in range(TPB):
                    if t + 1 < TPB:
                        project(t + 1)
                    pe.wait_ge(S["qkp"], b * TPB + t + 1)
                    pe.wait_ge(S["qkr"], b * TPB + t + 1)
                    if t >= 1:
                        pe.wait_ge(S["qts"], b * TPB + t)
                        pe.wait_ge(S["kts"], b * TPB + t)
                    flat = qk[:, t % 2, :, :].rearrange("p h e -> p (h e)")
                    four(4, flat[:, 0:D])
                    four(5, flat[:, D:2 * D]).then_inc(S["qkt"], 1)
                pe.wait_ge(S["qts"], TPB * (b + 1))
                pe.wait_ge(S["kts"], TPB * (b + 1))
                pe.wait_ge(S["vs"], TPB * (b + 1))

                def scores(s):
                    (i, hp), u = STEPS[s], s % 2
                    n = (i + 1) * P
                    for e in range(2):
                        k = (2 * hp + e) // GH
                        mm(ps[:, 2 * u + e, 0:n], q_t[:, 2 * hp + e, i * P:(i + 1) * P], k_t[:, k, 0:n], start=True, stop=False)
                        last = mm(ps[:, 2 * u + e, n - P:n], ident16[:, :], future16[:, :], start=False, stop=True)
                    last.then_inc(S["st"], 1)

                def attend(s):
                    (i, hp), u = STEPS[s], s % 2
                    pe.wait_ge(S["pta"], b * NS + s + 1)
                    if i >= 2:
                        pe.wait_ge(S["ptb"], b * wide_steps(NS) + wide_steps(s + 1))
                    if hp == 0 and QUERY_ORDER.index(i) >= 2:
                        pe.wait_ge(S["attd"], b * TPB + (2 if i % 2 == QUERY_ORDER[1] % 2 else 1))
                    for j in range(i + 1):
                        for e in range(2):
                            k, g = (2 * hp + e) // GH, (2 * hp + e) % GH
                            cols = slice((2 * hp + e) * HD, (2 * hp + e + 1) * HD)
                            last = mm(ps[g * HD:(g + 1) * HD, 6 + i % 2, k * P:(k + 1) * P], v_sb[:, j, cols],
                                      prob_t[:, u, 2 * j + e, :], start=(j == 0), stop=(j == i))
                    last.then_inc(S["pv"], 1)

                def denominators(i, s):
                    n = QUERY_ORDER.index(i)
                    pe.wait_ge(S["rden"], b * TPB + n + 1)
                    pe.wait_ge(S["ptb"], b * wide_steps(NS) + wide_steps(s))
                    if n >= 1:
                        pe.wait_ge(S["rdts"], b * TPB + n)
                    four(5, over_den[:, :, :].rearrange("p h e -> p (h e)")).then_inc(S["rdt"], 1)

                scores(0)
                scores(1)
                for s in range(NS + 2):
                    if s < NS:
                        pe.wait_ge(S["pexp"], b * NS + s + 1)
                    if s + 2 < NS:
                        scores(s + 2)
                    if s >= 2 and STEPS[s - 2][1] == HEADS // 2 - 1:
                        denominators(STEPS[s - 2][0], s)
                    if 1 <= s <= NS:
                        attend(s - 1)
                    if s < NS:
                        if STEPS[s][0] >= 2 and tiles_through(s) > 0:
                            pe.wait_ge(S["rdts"], b * TPB + tiles_through(s))
                        for j in range(STEPS[s][0] + 1):
                            for e in range(2):
                                q = 2 * j + e
                                last = tr(ps[:, 4 + q // 4, (q % 4) * P:(q % 4 + 1) * P], prob[:, s % 2, e, j * P:(j + 1) * P], ident)
                        last.then_inc(S["pt"], 1)

                for n, t in enumerate(QUERY_ORDER):
                    pe.wait_ge(S["attd"], b * TPB + n + 1)
                    for k in range(DC):
                        last = mm(ps[:, n, :], att_t[:, t, k, :], w_o[:, k, :], start=(k == 0), stop=(k == DC - 1))
                    last.then_inc(S["oproj"], 1)
                for t in range(TPB):
                    pe.wait_ge(S["hn"], b * TPB + t + 1)
                    if t >= 2:
                        pe.wait_ge(S["hnts"], b * TPB + t - 1)
                    four(4 + t % 2, hn[:, t, :]).then_inc(S["hnt"], 1)
                    pe.wait_ge(S["hnts"], b * TPB + t + 1)
                    for k in range(DC):
                        last = mm(ps[:, 6, t * 8:t * 8 + MOE0.routed], hn_t[:, t % 2, k, :], w_rt[:, k, :], start=(k == 0), stop=(k == DC - 1))
                    last.then_inc(S["logit"], 1)
                pe.wait_ge(S["masked"], b + 1)
                places(nc, r, MOE0, c, m, m["before0"], 7).then_inc(S["ranked"], 1)
                pe.wait_ge(S["scattered"], 16 * TPB * MOE0.top * (b + 1))




def mixture(nc, a, m, c, d, moe, before, out):
    ctx = ExitStack()
    with ctx:
        def sb(name, shape, dt=F32):
            return ctx.enter_context(nc.sbuf_tensor(f"{moe.name}_{name}", shape, dt))

        def sem(name):
            return ctx.enter_context(nc.semaphore(f"{moe.name}_{name}"))

        ps = m["psum"]
        E, N, G, I = moe.experts, moe.tiles, moe.groups, moe.inner
        full, n_fc = E * BLOCKS, len(moe.fc)
        ident = c["ident"]
        w_up = sb("w_up", [P, RING * DC, moe.up])
        w_down = sb("w_down", [P, RING * n_fc, D])
        count_i, tiles_of = sb("count_i", [P, E], I32), sb("tiles_of", [P, E])
        ends, starts = sb("ends", [P, E]), sb("starts", [P, E])
        starts_i = sb("starts_i", [1, E], I32)
        at_or_before, begun = sb("at_or_before", [P, G, E]), sb("begun", [P, G])
        first, valid = sb("first", [P, G]), sb("valid", [P, G])
        block_f, block = sb("block_f", [P, G]), sb("block", [P, G], I32)
        pair_i, pair = sb("pair_i", [P, G], I32), sb("pair", [P, G, 2])
        of_tile = sb("of_tile", [1, 2, G * P], I32)
        table = sb("table", [P, G, 2 * P])
        ids, weight = sb("ids", [P, G * P], I32), sb("weight", [P, G * P])
        idx = [sb(f"idx{u}", [P, 1], I32) for u in range(GROUP)]
        rows = [sb(f"rows{u}", [P, D]) for u in range(GROUP)]
        rows_t = [sb(f"rows_t{u}", [P, DC, P]) for u in range(2)]
        gate, hid = [sb(f"gate{u}", [P, I]) for u in range(2)], [sb(f"hid{u}", [P, I]) for u in range(2)]
        hid_t = [sb(f"hid_t{u}", [P, n_fc, P]) for u in range(2)]
        res = [sb(f"res{u}", [P, D]) for u in range(RESULTS)]
        loaded, gathered = m["loaded"], m["gathered"]
        loaded_0 = 0 if moe is MOE0 else MOE0.loads * (MOE0.experts // RING)
        gathered_0 = 0 if moe is MOE0 else 16 * (MOE0.tiles // GROUP)
        S = {n: sem(n) for n in ("counted chain tiled blocks flipped tables listed ready copied rt rts up silu "
                                 "hidden ht hts down res added stored").split()}

        def groups(eng, body):
            n = N // GROUP
            body(0, False)
            with eng.Fori(1, n - 1) as g:
                body(g, False)
            body(n - 1, True)

        block_ = ctx.enter_context(nc.Block())

        @block_.sync
        def _(sp):
            def load(e, u):
                up = w_up[:, u * DC:(u + 1) * DC, :]
                if isinstance(e, int) and e < moe.first:
                    gate_w, up_w, down_w = a["L0_ffn_sh_gate"], a["L0_ffn_sh_up"], a["L0_ffn_sh_down"]
                else:
                    pick = (lambda w: w[e - moe.first]) if isinstance(e, int) else \
                        (lambda w: w[bass.ds(e - moe.first, 1), :, :].rearrange("a d n -> (a d) n"))
                    names = ("L0_ffn_r_gate", "L0_ffn_r_up", "L0_ffn_r_down") if moe is MOE0 else \
                        ("L1_ffn_w_gate", "L1_ffn_w_up", "L1_ffn_w_down")
                    gate_w, up_w, down_w = (pick(a[n]) for n in names)
                sp.dma_start(up[:, :, 0:I], gate_w.rearrange("(c p) n -> p c n", p=P)).then_inc(loaded[u], 16)
                sp.dma_start(up[:, :, I:2 * I], up_w.rearrange("(c p) n -> p c n", p=P)).then_inc(loaded[u], 16)
                for j, (f, w) in enumerate(moe.fc):
                    sp.dma_start(w_down[0:w, u * n_fc + j, :], down_w[f:f + w, :]).then_inc(loaded[u], 16)

            for u in range(RING):
                load(u, u)
            for u in range(RING):
                sp.wait_ge(loaded[u], loaded_0 + moe.loads)
                sp.sem_inc(S["ready"], 1)
            sp.wait_ge(S["tiled"], 1)
            with sp.Fori(1, E // RING) as g:
                for u in range(RING):
                    free = sp.value_load(starts_i[0:1, bass.ds(g * RING + u - RING + 1, 1)], min_val=1, max_val=N)
                    hold(sp, S["down"], free, m["passed"]["sp"])
                    load(g * RING + u, u)
                    sp.wait_ge(loaded[u], loaded_0 + moe.loads * (g + 1))
                    sp.sem_inc(S["ready"], 1)
            if out is not None:
                sp.wait_ge(S["added"], 16 * N)
                sp.dma_start(out.rearrange("b s d -> (b s) d"), d["sum"][0:TOKENS, :]).then_inc(S["stored"], 16)
                sp.wait_ge(S["stored"], 16)

        @block_.gpsimd
        def _(pool):
            g = nc.gpsimd
            pool.wait_ge(S["blocks"], 1)
            table_rows = d["slots"].rearrange("(b p) e -> b (p e)", p=P)
            for j in range(G):
                pool.indirect_dma_start(table[:, j, :], None, table_rows, bass.IndirectOffsetOnAxis(block[:, j:j + 1], 0)).then_inc(S["tables"], 16)
            pool.wait_ge(S["listed"], 1)

            def gather(t, u):
                since(pool, S["added"], 16 * (t - GROUP + 1))
                g.tensor_copy(idx[u][:, :], ids[:, bass.ds(t, 1)]).then_inc(S["copied"], 1)
                pool.wait_ge(S["copied"], t + 1)
                since(pool, S["rt"], t - GROUP + 1)
                pool.sem_inc(m["passed"]["pool"], 1)
                pool.indirect_dma_start(rows[u][:, :], None, d["rows"], bass.IndirectOffsetOnAxis(idx[u][:, :], 0)).then_inc(gathered[u], 16)

            def tiles(g, last):
                for u in range(GROUP):
                    t = g * GROUP + u
                    if not last or u < GROUP - AHEAD:
                        gather(t + AHEAD, (u + AHEAD) % GROUP)
                    pool.wait_ge(S["res"], t + 1)
                    since(pool, S["added"], 16 * t)
                    pool.sem_inc(m["passed"]["pool"], 1)
                    pool.indirect_dma_start(d["sum"], bass.IndirectOffsetOnAxis(idx[u][:, :], 0), res[u % RESULTS][:, :], None,
                                            compute_op=ALU.add).then_inc(S["added"], 16)

            for t in range(AHEAD):
                gather(t, t)
            groups(pool, tiles)
            pool.wait_ge(S["added"], 16 * N)

        @block_.scalar
        def _(act):
            sc = nc.scalar

            def flip(t, u):
                i = u % 2
                act.wait_ge(S["rt"], t + 1)
                since(act, S["up"], t - 1)
                sc.activation(rows_t[i][:, :, :].rearrange("p c q -> p (c q)"), ps[:, i, :], ACT.Copy).then_inc(S["rts"], 1)

            def silu(t, u):
                i = u % 2
                act.wait_ge(S["up"], t + 1)
                since(act, S["hidden"], t - 1)
                sc.activation(gate[i][:, :], ps[:, 2 + i, 0:I], ACT.Silu).then_inc(S["silu"], 1)

            def tiles(g, last):
                for u in range(GROUP):
                    i, t = u % 2, g * GROUP + u
                    if not last or u < GROUP - 2:
                        flip(t + 2, u)
                    if not last or u < GROUP - 1:
                        silu(t + 1, u + 1)
                    act.wait_ge(S["down"], t + 1)
                    since(act, S["added"], 16 * (t - RESULTS + 1))
                    sc.activation(res[u % RESULTS][:, :], ps[:, 5 + i, :], ACT.Copy, scale=weight[:, bass.ds(t, 1)]).then_inc(S["res"], 1)

            act.wait_ge(S["listed"], 1)
            flip(0, 0)
            flip(1, 1)
            silu(0, 0)
            groups(act, tiles)

        @block_.vector
        def _(dve):
            v = nc.vector
            own = Steps(dve, S["chain"])
            dve.wait_ge(S["counted"], 1)
            if moe.first:
                own.did(v.memset(tiles_of[:, 0:moe.first], float(BLOCKS)))
            own.run(v.tensor_scalar(count_i[:, 0:moe.routed], ps[:, 0, 0:moe.routed], float(P - 1), None, ALU.add))
            own.run(v.tensor_scalar(count_i[:, 0:moe.routed], count_i[:, 0:moe.routed], P.bit_length() - 1, None, ALU.logical_shift_right))
            own.run(v.tensor_scalar(tiles_of[:, moe.first:E], count_i[:, 0:moe.routed], 1.0, None, ALU.max))
            own.run(v.tensor_tensor_scan(ends[:, :], m["ones"][:, 0:E], tiles_of[:, :], 0.0, ALU.mult, ALU.add))
            own.run(v.tensor_tensor(starts[:, :], ends[:, :], tiles_of[:, :], ALU.subtract))
            v.tensor_copy(starts_i[:, :], starts[0:1, :]).then_inc(S["tiled"], 1)
            for j in range(G):
                t = c["tile"][:, j:j + 1]
                own.run(v.tensor_scalar(at_or_before[:, j, :], starts[:, :], t, None, ALU.is_le, ALU.add, accum_out=begun[:, j:j + 1]))
                own.run(v.tensor_tensor(at_or_before[:, j, :], at_or_before[:, j, :], starts[:, :], ALU.mult))
                own.run(v.tensor_reduce(first[:, j:j + 1], at_or_before[:, j, :], AX.X, ALU.max))
                own.did(v.tensor_tensor(valid[:, j:j + 1], t, ends[:, E - 1:E], ALU.is_lt))
                own.run(v.tensor_tensor(first[:, j:j + 1], t, first[:, j:j + 1], ALU.subtract))
                own.run(v.scalar_tensor_tensor(block_f[:, j:j + 1], begun[:, j:j + 1], float(BLOCKS), first[:, j:j + 1], ALU.mult, ALU.add))
                own.run(v.scalar_tensor_tensor(block_f[:, j:j + 1], block_f[:, j:j + 1], -float(BLOCKS + full), valid[:, j:j + 1], ALU.add, ALU.mult))
            own.did(v.tensor_scalar(pair_i[:, :], begun[:, :], -1.0, None, ALU.add))
            v.tensor_scalar(block[:, :], block_f[:, :], float(full), None, ALU.add).then_inc(S["blocks"], 1)
            own.wait()
            own.run(v.tensor_scalar(pair_i[:, :], pair_i[:, :], RING - 1, None, ALU.bitwise_and))
            own.did(v.tensor_copy(pair[:, :, 0], pair_i[:, :]))
            v.tensor_copy(pair[:, :, 1], begun[:, :]).then_inc(S["tiled"], 1)
            dve.wait_ge(S["flipped"], 1)
            for j in range(G):
                own.did(v.tensor_copy(ids[:, j * P:(j + 1) * P], ps[:, 1 + 2 * j, 0:P]))
                own.did(v.tensor_scalar(weight[:, j * P:(j + 1) * P], ps[:, 2 + 2 * j, 0:P], 1.0 / moe.scaling, None, ALU.mult))
            own.wait()
            v.tensor_copy(of_tile[:, :, :].rearrange("p a t -> p (a t)"), ps[0:1, 5, 0:2 * G * P]).then_inc(S["listed"], 1)

            def flip(t, u):
                i = u % 2
                dve.wait_ge(S["ht"], t + 1)
                since(dve, S["down"], t - 1)
                if I % P == 0:
                    last = v.tensor_copy(hid_t[i][:, :, :].rearrange("p c q -> p (c q)"), ps[:, 4, 0:n_fc * P])
                else:
                    for j, (f, w) in enumerate(moe.fc):
                        last = v.tensor_copy(hid_t[i][0:w, j, :], ps[0:w, 4, j * P:(j + 1) * P])
                last.then_inc(S["hts"], 1)

            def tiles(g, last):
                for u in range(GROUP):
                    i, t = u % 2, g * GROUP + u
                    dve.wait_ge(S["silu"], t + 1)
                    since(dve, S["ht"], t - 1)
                    v.tensor_tensor(hid[i][:, :], gate[i][:, :], ps[:, 2 + i, I:2 * I], ALU.mult).then_inc(S["hidden"], 1)
                    flip(t, u)

            groups(dve, tiles)

        @block_.tensor
        def _(pe):
            mm, tr = nc.tensor.matmul, nc.tensor.transpose
            mm(ps[:, 0, 0:moe.routed], m["ones"][:, :], before[:, TPB, :], start=True, stop=True).then_inc(S["counted"], 1)
            pe.wait_ge(S["tiled"], 2)
            pe.wait_ge(S["tables"], 16 * G)
            for j in range(G):
                for e in range(2):
                    tr(ps[:, 1 + 2 * j + e, 0:P], table[:, j, :].rearrange("p (s e) -> p e s", e=2)[:, e, :], ident)
            for e in range(2):
                for j in range(G):
                    last = mm(ps[0:1, 5, (e * G + j) * P:(e * G + j + 1) * P], pair[:, j, e:e + 1], ident, start=True, stop=True)
            last.then_inc(S["flipped"], 1)
            pe.wait_ge(S["listed"], 1)

            def flip(g, u):
                i, t = u % 2, g * GROUP + u
                pe.wait_ge(gathered[u], gathered_0 + 16 * (g + 1))
                since(pe, S["rts"], t - 1)
                for k in range(DC):
                    last = tr(ps[:, i, k * P:(k + 1) * P], rows[u][:, k * P:(k + 1) * P], ident)
                last.then_inc(S["rt"], 1)

            def load(what, t, least, most):
                return pe.value_load(of_tile[0:1, what, bass.ds(t, 1)], min_val=least, max_val=most)

            def up(g, u, at, needed):
                i, t = u % 2, g * GROUP + u
                pe.wait_ge(S["ready"], needed)
                pe.wait_ge(S["rts"], t + 1)
                since(pe, S["hidden"], t - 1)
                for k in range(DC):
                    last = mm(ps[:, 2 + i, 0:2 * I], rows_t[i][:, k, :], w_up[:, bass.ds(at * DC + k, 1), :].rearrange("p a n -> p (a n)"),
                              start=(k == 0), stop=(k == DC - 1))
                last.then_inc(S["up"], 1)

            def tiles(g, last):
                at = load(0, g * GROUP, 0, RING - 1)
                for u in range(GROUP):
                    i, t = u % 2, g * GROUP + u
                    more, over = divmod(u + 1, GROUP)
                    if not last or u < GROUP - 1:
                        at_next, needed = load(0, t + 1, 0, RING - 1), load(1, t + 1, 1, E)
                    pe.wait_ge(S["hidden"], t + 1)
                    since(pe, S["hts"], t)
                    for j, (f, w) in enumerate(moe.fc):
                        done = tr(ps[0:w, 4, j * P:(j + 1) * P], hid[i][:, f:f + w], ident)
                    done.then_inc(S["ht"], 1)
                    if not last or u < GROUP - 2:
                        flip(g + (u + 2) // GROUP, (u + 2) % GROUP)
                    if not last or u < GROUP - 1:
                        up(g + more, over, at_next, needed)
                    pe.wait_ge(S["hts"], t + 1)
                    since(pe, S["res"], t - 1)
                    for j, (f, w) in enumerate(moe.fc):
                        done = mm(ps[:, 5 + i, :], hid_t[i][0:w, j, :], w_down[0:w, bass.ds(at * n_fc + j, 1), :].rearrange("p a n -> p (a n)"),
                                  start=(j == 0), stop=(j == n_fc - 1))
                    done.then_inc(S["down"], 1)
                    at = at_next

            flip(0, 0)
            flip(0, 1)
            up(0, 0, load(0, 0, 0, RING - 1), load(1, 0, 1, E))
            groups(pe, tiles)




def middle(nc, a, m, c, dram):
    ctx = ExitStack()
    with ctx:
        def sb(name, shape, dt=F32):
            return ctx.enter_context(nc.sbuf_tensor("m_" + name, shape, dt))

        def sem(name):
            return ctx.enter_context(nc.semaphore("m_" + name))

        ps, x, ctx_sb = m["psum"], m["x"], m["ctx"]
        N = MOE1.routed
        w_rt = sb("w_rt", [P, DC, N])
        mask_u8, mask, barred = sb("mask_u8", [P, BATCH, KEYS], U8), sb("mask", [P, BATCH, KEYS]), sb("barred", [P, BATCH, KEYS])
        any_key = sb("any_key", [P, BATCH])
        stats, mv, rstd, var_e = sb("stats", [P, TPB, 6]), sb("mv", [P, TPB, 2]), sb("rstd", [P, TPB]), sb("var_e", [P, TPB])
        stats2, mv2, rstd2, var2 = sb("stats2", [P, TPB, 6]), sb("mv2", [P, TPB, 2]), sb("rstd2", [P, TPB]), sb("var2", [P, TPB])
        xn, xn_t = sb("xn", [P, TPB, D]), sb("xn_t", [P, DC, SEQ])
        att, top, den = sb("att", [P, TPB, KEYS]), sb("top", [P, TPB]), sb("den", [P, TPB])
        att_t = sb("att_t", [KEYS, TPB, P])
        x3, hn, hn_t = sb("x3", [P, TPB, D]), sb("hn", [P, TPB, D]), sb("hn_t", [P, 2, DC, P])
        top_l, sum_l = sb("top_l", [P, TPB]), sb("sum_l", [P, TPB])
        r = route_memory(sb, MOE1)
        send = {"slot": r["slot"], "entry": sb("entry_out", [P, TPB * MOE1.top, 2])}
        names = ("w mask x_in var rstd xn ft fe s shift e p pt pts o x3 var2 rstd2 hn logit lsh le masked ranked "
                 "slotted scattered rows_out dve").split()
        S = {n: sem(n) for n in names}
        r0, r1 = dram["moe0"], dram["moe1"]
        SCATTERS = TPB * MOE1.top
        EARLY = 12

        def sequences(eng, body):
            body(0, True, False)
            with eng.Fori(1, BATCH - 1) as b:
                body(b, False, False)
            body(BATCH - 1, False, True)

        block = ctx.enter_context(nc.Block())

        @block.sync
        def _(sp):
            sp.dma_start(mask_u8[:, :, :].rearrange("p b k -> p (b k)"), a["mask_BxS2_bk0"].rearrange("b k -> (b k)").partition_broadcast(P)).then_inc(S["mask"], 16)
            for b in range(BATCH):
                sp.dma_start(x[:, b * TPB:(b + 1) * TPB, :], r0["sum"][b * SEQ:(b + 1) * SEQ, :].rearrange("(t p) d -> p t d", p=P)).then_inc(S["x_in"], 16)
                if b == 0:
                    sp.dma_start(w_rt[:, :, :], a["L1_router_t"].rearrange("(c p) n -> p c n", p=P)).then_inc(S["w"], 16)
                sp.wait_ge(S["x_in"], 16 * (b + 1))
            with sp.Fori(0, BATCH) as b:
                sp.wait_ge(S["x3"], TPB * (b + 1))
                sp.dma_start(r1["sum"][bass.ds(b * SEQ, SEQ), :].rearrange("(t p) d -> p t d", p=P), x3[:, :, :]).then_inc(S["rows_out"], 16)
                sp.wait_ge(S["hn"], TPB * (b + 1))
                sp.dma_start(r1["rows"][bass.ds(b * SEQ, SEQ), :].rearrange("(t p) d -> p t d", p=P), hn[:, :, :]).then_inc(S["rows_out"], 16)
                hold(sp, S["rows_out"], 32 * (b + 1), m["passed"]["sp"])

        @block.gpsimd
        def _(pool):
            g = nc.gpsimd

            def first_norm(b):
                pool.wait_ge(S["var"], b + 1)
                g.tensor_tensor(rstd[:, :], var_e[:, :], m["power"][:, 0:TPB], ALU.pow).then_inc(S["rstd"], 1)

            def sequence(b, first, last):
                pool.wait_ge(S["var2"], b + 1)
                g.tensor_tensor(rstd2[:, :], var2[:, :], m["power"][:, 0:TPB], ALU.pow).then_inc(S["rstd2"], 1)
                if not last:
                    first_norm(b + 1)
                if not first:
                    scatter(pool, send, range(EARLY, SCATTERS), r1["slots"], S["scattered"])
                hold(pool, S["slotted"], b + 1, m["passed"]["pool"])
                scatter(pool, send, range(EARLY), r1["slots"], S["scattered"])

            first_norm(0)
            sequences(pool, sequence)
            scatter(pool, send, range(EARLY, SCATTERS), r1["slots"], S["scattered"])
            pool.wait_ge(S["scattered"], 16 * SCATTERS * BATCH)

        @block.scalar
        def _(act):
            sc = nc.scalar

            def normed_out(b):
                for t in range(TPB):
                    act.wait_ge(S["ft"], b * 2 * TPB + t + 1)
                    sc.activation(xn_t[:, :, t * P:(t + 1) * P], ps[:, t % 2, :].rearrange("p (c q) -> p c q", q=P), ACT.Copy).then_inc(S["fe"], 1)

            def softmax(b):
                act.wait_ge(S["shift"], b + 1)
                sc.activation(att[:, :, :], att[:, :, :], ACT.Exp).then_inc(S["e"], 1)
                act.wait_ge(S["pt"], b + 1)
                sc.activation(att_t[:, :, :].rearrange("p t q -> p (t q)"), ps[0:KEYS, 5, :], ACT.Copy).then_inc(S["pts"], 1)

            def sequence(b, first, last):
                for t in range(TPB):
                    act.wait_ge(S["ft"], b * 2 * TPB + TPB + t + 1)
                    if t >= 2:
                        act.wait_ge(S["logit"], b * TPB + t - 1)
                    sc.activation(hn_t[:, t % 2, :, :].rearrange("p c q -> p (c q)"), ps[:, t % 2, :], ACT.Copy).then_inc(S["fe"], 1)
                if not last:
                    normed_out(b + 1)
                act.wait_ge(S["lsh"], b + 1)
                sc.activation(r["logit"][:, :, :], r["logit"][:, :, :], ACT.Exp).then_inc(S["le"], 1)
                if not last:
                    softmax(b + 1)

            normed_out(0)
            softmax(0)
            sequences(act, sequence)

        DVE_FIRST, DVE_TURN = 14, 52

        @block.vector
        def _(dve):
            v = nc.vector
            pre = Steps(dve, S["masked"])
            dve.wait_ge(S["mask"], 16)
            pre.run(v.tensor_copy(mask[:, :, :], mask_u8[:, :, :]))
            pre.did(v.tensor_scalar(barred[:, :, :], mask[:, :, :], 1.0, 1e30, ALU.subtract, ALU.mult))
            pre.did(v.tensor_reduce(any_key[:, :], mask[:, :, :], AX.X, ALU.max))
            pre.wait()

            def statistics(own, b):
                dve.wait_ge(S["x_in"], 16 * (b + 1))
                dve.sem_inc(m["passed"]["dve"], 1)
                for t in range(TPB):
                    own.did(v.bn_stats(stats[:, t, :], tile_at(x, b * TPB + t)))
                own.hold()
                for t in range(TPB):
                    own.did(v.bn_aggr(mv[:, t, :], stats[:, t, :]))
                own.wait()
                v.tensor_scalar(var_e[:, :], mv[:, :, 1], EPS, None, ALU.add).then_inc(S["var"], 1)

            def normed(b):
                dve.wait_ge(S["rstd"], b + 1)
                for t in range(TPB):
                    v.tensor_scalar(xn[:, t, :], tile_at(x, b * TPB + t), mv[:, t, 0:1], rstd[:, t:t + 1], ALU.subtract, ALU.mult).then_inc(S["xn"], 1)

            def softmax(own, b):
                dve.wait_ge(S["s"], b + 1)
                s2 = ps[:, 4, 0:TPB * KEYS].rearrange("p (t k) -> p t k", k=KEYS)
                own.run(v.scalar_tensor_tensor(att[:, :, :], s2, D ** -0.5, mask[:, bass.ds(b, 1), :].to_broadcast([P, TPB, KEYS]), ALU.mult, ALU.mult))
                own.run(v.tensor_tensor(att[:, :, :], att[:, :, :], barred[:, bass.ds(b, 1), :].to_broadcast([P, TPB, KEYS]), ALU.add))
                own.run(v.tensor_reduce(top[:, :], att[:, :, :], AX.X, ALU.max))
                v.tensor_tensor(att[:, :, :], att[:, :, :], top[:, :].unsqueeze(2).to_broadcast([P, TPB, KEYS]), ALU.subtract).then_inc(S["shift"], 1)
                dve.wait_ge(S["e"], b + 1)
                own.run(v.tensor_reduce(den[:, :], att[:, :, :], AX.X, ALU.add))
                own.run(v.reciprocal(den[:, :], den[:, :]))
                own.run(v.tensor_scalar(den[:, :], den[:, :], any_key[:, bass.ds(b, 1)], None, ALU.mult))
                v.tensor_tensor(att[:, :, :], att[:, :, :], den[:, :].unsqueeze(2).to_broadcast([P, TPB, KEYS]), ALU.mult).then_inc(S["p"], 1)

            def sequence(b, first, last):
                own = Steps(dve, S["dve"], DVE_FIRST + b * DVE_TURN, m["passed"]["dve"])
                if not first:
                    hold(dve, S["rows_out"], 32 * b, m["passed"]["dve"])
                for t in range(TPB):
                    dve.wait_ge(S["o"], b * TPB + t + 1)
                    v.tensor_tensor(x3[:, t, :], tile_at(x, b * TPB + t), ps[:, 6 + t % 2, :], ALU.add).then_inc(S["x3"], 1)
                    hold(dve, S["x3"], b * TPB + t + 1, m["passed"]["dve"])
                    own.did(v.bn_stats(stats2[:, t, :], x3[:, t, :]))
                own.hold()
                for t in range(TPB):
                    own.did(v.bn_aggr(mv2[:, t, :], stats2[:, t, :]))
                own.wait()
                v.tensor_scalar(var2[:, :], mv2[:, :, 1], EPS, None, ALU.add).then_inc(S["var2"], 1)
                if not last:
                    statistics(own, b + 1)
                dve.wait_ge(S["rstd2"], b + 1)
                for t in range(TPB):
                    v.tensor_scalar(hn[:, t, :], x3[:, t, :], mv2[:, t, 0:1], rstd2[:, t:t + 1], ALU.subtract, ALU.mult).then_inc(S["hn"], 1)
                if not last:
                    normed(b + 1)
                dve.wait_ge(S["logit"], TPB * (b + 1))
                lg = ps[:, 2, 0:TPB * N].rearrange("p (t e) -> p t e", e=N)
                own.run(v.tensor_reduce(top_l[:, :], lg, AX.X, ALU.max))
                v.tensor_tensor(r["logit"][:, :, :], lg, top_l[:, :].unsqueeze(2).to_broadcast([P, TPB, N]), ALU.subtract).then_inc(S["lsh"], 1)
                dve.wait_ge(S["le"], b + 1)
                own.run(v.tensor_reduce(sum_l[:, :], r["logit"][:, :, :], AX.X, ALU.add))
                own.run(v.reciprocal(sum_l[:, :], sum_l[:, :]))
                own.run(v.tensor_tensor(r["prob"][:, :, :], r["logit"][:, :, :], sum_l[:, :].unsqueeze(2).to_broadcast([P, TPB, N]), ALU.mult))
                token = c["token"][:, bass.ds(b * TPB, TPB)]
                choose(nc, own, r, MOE1, c, token, m["before1"], S["masked"])
                dve.wait_ge(S["ranked"], b + 1)
                find_slots(nc, own, r, MOE1, c, m, m["before1"], 3, c["offset1"])
                if not first:
                    dve.wait_ge(S["scattered"], 16 * SCATTERS * b)
                own.did(v.tensor_copy(send["entry"][:, :, :], r["entry"][:, :, :]))
                own.wait()
                v.tensor_copy(send["slot"][:, :], r["slot_f"][:, :]).then_inc(S["slotted"], 1)
                if not last:
                    softmax(own, b + 1)
                    assert own.n == DVE_TURN, own.n

            own = Steps(dve, S["dve"], 0, m["passed"]["dve"])
            statistics(own, 0)
            normed(0)
            softmax(own, 0)
            assert own.n == DVE_FIRST, own.n
            sequences(dve, sequence)

        @block.tensor
        def _(pe):
            mm, tr = nc.tensor.matmul, nc.tensor.transpose
            ident = c["ident"]
            pe.wait_ge(S["w"], 16)

            def flip(n, j, src):
                since(pe, S["fe"], n - 1)
                for k in range(DC):
                    last = tr(ps[:, j % 2, k * P:(k + 1) * P], src[:, k * P:(k + 1) * P], ident)
                last.then_inc(S["ft"], 1)

            def normed_flips(b):
                for t in range(TPB):
                    pe.wait_ge(S["xn"], b * TPB + t + 1)
                    flip(b * 2 * TPB + t, t, xn[:, t, :])

            def scores(b):
                for t in range(TPB):
                    pe.wait_ge(S["fe"], b * 2 * TPB + t + 1)
                    for k in range(DC):
                        last = mm(ps[:, 4, t * KEYS:(t + 1) * KEYS], xn_t[:, k, t * P:(t + 1) * P],
                                  m["ctx_t"][:, bass.ds(b, 1), k, :].rearrange("p a n -> p (a n)"), start=(k == 0), stop=(k == DC - 1))
                last.then_inc(S["s"], 1)

            def prob_flips(b):
                hold(pe, S["p"], b + 1, m["passed"]["pe"])
                for t in range(TPB):
                    last = tr(ps[0:KEYS, 5, t * P:(t + 1) * P], att[:, t, :], ident)
                last.then_inc(S["pt"], 1)

            def sequence(b, first, last):
                hold(pe, S["pts"], b + 1, m["passed"]["pe"])
                for t in range(TPB):
                    if t >= 2:
                        hold(pe, S["x3"], b * TPB + t - 1, m["passed"]["pe"])
                    mm(ps[:, 6 + t % 2, :], att_t[:, t, :], tile_at(ctx_sb, b)[0:KEYS, :], start=True, stop=True).then_inc(S["o"], 1)

                def hn_flip(t):
                    pe.wait_ge(S["hn"], b * TPB + t + 1)
                    flip(b * 2 * TPB + TPB + t, t, hn[:, t, :])

                hn_flip(0)
                for t in range(TPB):
                    if t + 1 < TPB:
                        hn_flip(t + 1)
                    pe.wait_ge(S["fe"], b * 2 * TPB + TPB + t + 1)
                    for k in range(DC):
                        done = mm(ps[:, 2, t * N:(t + 1) * N], hn_t[:, t % 2, k, :], w_rt[:, k, :], start=(k == 0), stop=(k == DC - 1))
                    done.then_inc(S["logit"], 1)
                if not last:
                    normed_flips(b + 1)
                    scores(b + 1)
                pe.wait_ge(S["masked"], 3 + b + 1)
                places(nc, r, MOE1, c, m, m["before1"], 3).then_inc(S["ranked"], 1)
                if not last:
                    prob_flips(b + 1)

            normed_flips(0)
            scores(0)
            prob_flips(0)
            sequences(pe, sequence)



_INS = ["x", "ctx_2048", "mask_BxS2_bk0", "L0_ffn_ln1_w", "L0_ffn_ln2_w", "L0_ffn_kv_d_w", "L0_ffn_q_d_w", "L0_ffn_k_u_w",
        "L0_ffn_v_u_w", "L0_ffn_q_u_w", "L0_ffn_rope_k_w", "L0_ffn_rope_q_w", "L0_ffn_o_w", "L0_ffn_sh_gate", "L0_ffn_sh_up",
        "L0_ffn_sh_down", "L0_ffn_r_gate", "L0_ffn_r_up", "L0_ffn_r_down", "L0_ffn_router_w", "L0_ffn_router_b",
        "L1_ffn_router_w", "L1_ffn_w_gate", "L1_ffn_w_up", "L1_ffn_w_down"]


def constants():
    import numpy as np

    f = np.float32
    row, col = np.arange(P)[:, None], np.arange(P)[None, :]
    angle = np.outer(np.arange(SEQ, dtype=f), (1.0 / 10000.0 ** (np.arange(0, ROT, 2, dtype=f) / f(ROT))).astype(f)).astype(f)
    cos, sin = np.cos(angle).astype(f), np.sin(angle).astype(f)
    by_tile = lambda t: t.reshape(TPB, P, -1).transpose(1, 0, 2).reshape(P, -1)
    seen = np.arange(KEYS)[None, :] <= np.arange(SEQ - P, SEQ)[:, None] + KEYS - SEQ
    parts = {
        "ident": np.eye(P), "earlier": row < col, "future": np.where(col <= row, 0.0, -1e38),
        "allowed": seen, "barred": np.where(seen, 0.0, -10000.0),
        "cos": by_tile(np.concatenate([cos, cos], 1)), "sin": by_tile(sin),
        "expert": np.tile(np.arange(32), (P, 1)),
        "offset0": np.tile((np.arange(8) + MOE0.first) * TOKENS, (P, 1)),
        "offset1": np.tile(np.arange(32) * TOKENS, (P, 1)),
        "token": row + P * np.arange(TILES)[None, :], "tile": row + P * np.arange(2)[None, :],
    }
    out = {"const": np.concatenate([np.asarray(parts[k], f) for k in CONST], 1), "zero_rows": np.zeros((SPARE, D), f)}
    for moe in (MOE0, MOE1):
        empty = np.zeros((moe.blocks, P, 2), f)
        empty[:, :, 0] = TOKENS + np.arange(P)
        for e in range(moe.first):
            part = empty[e * BLOCKS:(e + 1) * BLOCKS]
            part[:, :, 0] = np.arange(TOKENS).reshape(BLOCKS, P)
            part[:, :, 1] = 1.0
        out[moe.name + "_empty"] = empty.reshape(moe.blocks, 2 * P)
    return out


def kernel(**inputs):
    import numpy as np
    import concourse.bacc as bacc
    from concourse.bass_utils import run_bass_kernel_spmd

    nc = bacc.Bacc("TRN2", target_bir_lowering=False, num_devices=1)
    arrays = {n: np.ascontiguousarray(inputs[n]) for n in _INS}
    arrays["L1_router_t"] = np.ascontiguousarray(arrays.pop("L1_ffn_router_w").T)
    arrays.update(constants())
    aps = {n: nc.dram_tensor(f"in_{n}", v.shape, mybir.dt.from_np(v.dtype), kind="ExternalInput").ap() for n, v in arrays.items()}
    out = nc.dram_tensor("out", (BATCH, SEQ, D), F32, kind="ExternalOutput").ap()
    build(nc, aps, out)
    r = run_bass_kernel_spmd(nc, [{f"in_{n}": v for n, v in arrays.items()}], core_ids=[0])
    return r.results[0]["out"]
```

```python
from contextlib import ExitStack

import concourse.bass as bass
from concourse import mybir

F32, F32R, BF16, I32, U32, U8 = mybir.dt.float32, mybir.dt.float32r, mybir.dt.bfloat16, mybir.dt.int32, mybir.dt.uint32, mybir.dt.uint8
ALU, ACT, AX = mybir.AluOpType, mybir.ActivationFunctionType, mybir.AxisListType

P = 128
BATCH, SEQ, D = 4, 512, 512
TOKENS = BATCH * SEQ
TILES = TOKENS // P
TPB = SEQ // P
DC = D // P
KEYS = 64
HEADS, HD = 16, 32
ROT = HD // 2
LAT = 128
EPS = 1e-5
SPARE = P
BLOCKS = TOKENS // P
RING = 4
GROUP = 8
SPLITS = 4
RESULTS = 4
AHEAD = 4

QUERY_ORDER = (3, 0, 2, 1)
STEPS = [(i, hp) for pair in (QUERY_ORDER[0:2], QUERY_ORDER[2:4]) for hp in range(HEADS // 2) for i in pair]
NS = len(STEPS)


def tiles_through(s):
    return sum(hp == HEADS // 2 - 1 for _, hp in STEPS[:max(0, s - 1)])


def wide_steps(s):
    return sum(i >= 2 for i, _ in STEPS[:s])


CONST = {}
_at = 0
for _name, _n in [("ident", P), ("earlier", P), ("future", P), ("allowed", KEYS), ("barred", KEYS),
                  ("cos", TPB * ROT), ("sin", TPB * ROT // 2), ("expert", 32), ("offset0", 8),
                  ("offset1", 32), ("token", TILES), ("tile", 2)]:
    CONST[_name] = (_at, _at + _n)
    _at += _n
CONST_COLS = _at


class Moe:

    def __init__(self, name, experts, routed, top, inner, scaling):
        self.name, self.experts, self.routed, self.top = name, experts, routed, top
        self.first = experts - routed
        self.inner, self.scaling = inner, scaling
        self.blocks = experts * BLOCKS + 1
        most = self.first * BLOCKS + (TOKENS * top) // P + routed
        self.tiles = -(-most // GROUP) * GROUP
        self.groups = -(-self.tiles // P)
        self.fc = [(f, min(P, inner - f)) for f in range(0, inner, P)]
        self.tail = inner % P
        assert self.tail in (0, P // 2)
        self.loads = 16 * (2 + len(self.fc) + (self.tail > 0))
        self.up = 2 * inner
        self.cols = DC * self.up + len(self.fc) * D


MOE0 = Moe("moe0", 8, 7, 2, 256, 8.0)
MOE1 = Moe("moe1", 32, 32, 8, 192, 1.0)


class Steps:

    def __init__(self, eng, sem, base=0, passed=None):
        self.eng, self.sem, self.base, self.passed, self.n = eng, sem, base, passed, 0

    def did(self, ins):
        ins.then_inc(self.sem, 1)
        self.n += 1

    def wait(self):
        self.eng.wait_ge(self.sem, self.base + self.n)

    def hold(self):
        hold(self.eng, self.sem, self.base + self.n, self.passed)

    def run(self, ins):
        self.did(ins)
        self.wait()


def hold(eng, sem, count, passed):
    eng.wait_ge(sem, count)
    eng.sem_inc(passed, 1)


def since(eng, sem, count):
    if not isinstance(count, int) or count > 0:
        eng.wait_ge(sem, count)


def tile_at(a, i):
    return a[:, bass.ds(i, 1), :].rearrange("p a n -> p (a n)")


def build(nc, a, out, stop=None, debug=None):
    ctx = ExitStack()

    def sb(name, shape, dt=F32):
        return ctx.enter_context(nc.sbuf_tensor(name, shape, dt))

    def sem(name):
        return ctx.enter_context(nc.semaphore(name))

    with ctx:
        m = {
            "const": sb("const_sb", [P, CONST_COLS]),
            "ident16": sb("ident16", [P, P], BF16), "future16": sb("future16", [P, P], BF16),
            "ones": sb("ones", [P, P]), "mean_w": sb("mean_w", [KEYS, P]), "power": sb("power", [P, TILES]), "eps": sb("eps", [P, TILES]),
            "ctx": sb("ctx_sb", [P, BATCH, D]), "ctx_t": sb("ctx_t", [P, BATCH, DC, KEYS]),
            "psum": ctx.enter_context(nc.psum_tensor("psum", [P, 8, 512], F32)),
            "before0": sb("before0", [P, TPB + 1, MOE0.routed]),
            "before1": sb("before1", [P, TPB + 1, MOE1.routed]),
        }
        c = {k: m["const"][:, u:v] for k, (u, v) in CONST.items()}
        dram = {}
        for moe in (MOE0, MOE1):
            n = moe.name
            dram[n] = {
                "rows": nc.dram_tensor(f"{n}_rows", (TOKENS + SPARE, D), F32, kind="Internal").ap(),
                "sum": nc.dram_tensor(f"{n}_sum", (TOKENS + SPARE, D), F32, kind="Internal").ap(),
                "slots": nc.dram_tensor(f"{n}_slots", (moe.blocks * P, 2), F32, kind="Internal").ap(),
            }
        s_init = sem("tables_set")
        m["loaded"] = [sem(f"loaded{u}") for u in range(RING)]
        m["gathered"] = [sem(f"gathered{u}") for u in range(GROUP)]
        m["tile_steps"] = {n: sem("tile_" + n) for n in "copied rt rth rts wh wl up silu hidden ht hts res".split()}
        m["passed"] = {e: sem(f"passed_{e}") for e in ("dve", "pool", "pe", "act", "sp")}
        front(nc, a, m, c, dram, s_init)
        if stop == "front":
            dump(nc, debug, dram["moe0"], m["before0"], MOE0)
            return
        mixture(nc, a, m, c, dram["moe0"], MOE0, m["before0"], None)
        if stop == "moe0":
            dump(nc, debug, dram["moe0"], m["before0"], MOE0)
            return
        middle(nc, a, m, c, dram)
        if stop == "middle":
            dump(nc, debug, dram["moe1"], m["before1"], MOE1)
            return
        mixture(nc, a, m, c, dram["moe1"], MOE1, m["before1"], out)


def dump(nc, debug, d, before, moe):
    with nc.semaphore("dumped") as s, nc.Block() as block:
        @block.sync
        def _(sp):
            sp.dma_start(debug[0], d["rows"]).then_inc(s, 16)
            sp.dma_start(debug[1], d["sum"]).then_inc(s, 16)
            sp.dma_start(debug[2], d["slots"]).then_inc(s, 16)
            sp.dma_start(debug[3], before[:, TPB, :]).then_inc(s, 16)
            sp.wait_ge(s, 64)




def route_memory(sb, moe):
    n, k = moe.routed, moe.top
    return {
        "prob": sb(f"{moe.name}_prob", [P, TPB, max(n, 8)]), "logit": sb(f"{moe.name}_logit", [P, TPB, n]),
        "value": sb(f"{moe.name}_value", [P, TPB, 8]), "index": sb(f"{moe.name}_index", [P, TPB, 8], U32),
        "chosen": sb(f"{moe.name}_chosen", [P, TPB, k]), "total": sb(f"{moe.name}_total", [P, TPB, 1]),
        "hot": sb(f"{moe.name}_hot", [P, TPB * k, n]), "picked": sb(f"{moe.name}_picked", [P, TPB * k, n]),
        "mask": sb(f"{moe.name}_mask", [P, TPB, n]), "place": sb(f"{moe.name}_place", [P, TPB, n]),
        "slot_f": sb(f"{moe.name}_slot_f", [P, TPB * k]), "slot": sb(f"{moe.name}_slot", [P, TPB * k], I32),
        "entry": sb(f"{moe.name}_entry", [P, TPB * k, 2]),
    }


def choose(nc, steps, r, moe, token):
    v, n, k = nc.vector, moe.routed, moe.top
    steps.hold()
    for t in range(TPB):
        steps.did(v.max(r["value"][:, t, :], r["prob"][:, t, :]))
    steps.hold()
    for t in range(TPB):
        steps.did(v.max_index(r["index"][:, t, :], r["value"][:, t, :], r["prob"][:, t, :]))
    steps.did(v.tensor_reduce(r["total"][:, :, 0], r["value"][:, :, 0:k], AX.X, ALU.add))
    entry = r["entry"][:, :, :].rearrange("p (t k) e -> p t k e", k=k)
    steps.did(v.tensor_copy(entry[:, :, :, 0], token.unsqueeze(2).to_broadcast([P, TPB, k])))


def count(nc, steps, r, moe, c, before, masked):
    v, n, k = nc.vector, moe.routed, moe.top
    entry = r["entry"][:, :, :].rearrange("p (t k) e -> p t k e", k=k)
    steps.wait()
    steps.did(v.tensor_copy(r["chosen"][:, :, :], r["index"][:, :, 0:k]))
    steps.did(v.reciprocal(r["total"][:, :, :], r["total"][:, :, :]))
    steps.wait()
    steps.did(v.tensor_tensor(entry[:, :, :, 1], r["value"][:, :, 0:k],
                              r["total"][:, :, :].to_broadcast([P, TPB, k]), ALU.mult))
    chosen = r["chosen"][:, :, :].rearrange("p t k -> p (t k)")
    steps.run(v.tensor_tensor(r["hot"][:, :, :], c["expert"][:, 0:n].unsqueeze(1).to_broadcast([P, TPB * k, n]),
                              chosen.unsqueeze(2).to_broadcast([P, TPB * k, n]), ALU.is_equal))
    steps.run(v.tensor_reduce(r["mask"][:, :, :], r["hot"][:, :, :].rearrange("p (t k) e -> p t e k", k=k),
                              AX.X, ALU.add))
    for t in range(TPB):
        ins = v.tensor_tensor(before[:, t + 1, :], before[:, t, :], r["mask"][:, t, :], ALU.add)
        if t < TPB - 1:
            steps.run(ins)
    ins.then_inc(masked, 1)


def places(nc, r, moe, c, m, before, bank):
    n = moe.routed
    for t in range(TPB):
        o = m["psum"][:, bank, t * n:(t + 1) * n]
        nc.tensor.matmul(o, c["earlier"], r["mask"][:, t, :], start=True, stop=False)
        last = nc.tensor.matmul(o, m["ones"][:, :], before[:, t, :], start=False, stop=True)
    return last


def find_slots(nc, steps, r, moe, c, m, before, bank, offset):
    v, n, k = nc.vector, moe.routed, moe.top
    rank = m["psum"][:, bank, 0:TPB * n].rearrange("p (t e) -> p t e", e=n)
    steps.did(v.tensor_tensor(r["place"][:, :, :], rank, offset.unsqueeze(1).to_broadcast([P, TPB, n]), ALU.add))
    steps.did(v.tensor_copy(before[:, 0, :], before[:, TPB, :]))
    steps.wait()
    hot = r["hot"][:, :, :].rearrange("p (t k) e -> p t k e", k=k)
    picked = r["picked"][:, :, :].rearrange("p (t k) e -> p t k e", k=k)
    for t in range(TPB):
        steps.did(v.tensor_tensor(picked[:, t], hot[:, t], r["place"][:, t, :].unsqueeze(1).to_broadcast([P, k, n]), ALU.mult))
    steps.wait()
    steps.run(v.tensor_reduce(r["slot_f"][:, :], r["picked"][:, :, :], AX.X, ALU.add))


def scatter(pool, r, choices, table, written):
    for j in choices:
        pool.indirect_dma_start(table, bass.IndirectOffsetOnAxis(r["slot"][:, j:j + 1], 0),
                                r["entry"][:, j, :], None).then_inc(written, 16)




def cross(nc, a, m, c, dram, s_init, x, mv, rstd, rms, q_t, weights):
    ctx = ExitStack()
    with ctx:
        def sb(name, shape, dt=F32):
            return ctx.enter_context(nc.sbuf_tensor("c_" + name, shape, dt))

        ps, ctx_sb = m["psum"], m["ctx"]
        GH = P // HD
        ctx_heads = sb("ctx_heads", [P, BATCH, DC, GH * KEYS])
        ctx_pairs = sb("ctx_pairs", [P, BATCH, HEADS // 2, 2 * HD])
        stats, mv_q, var_q, rstd_q = sb("stats", [P, TILES, 6]), sb("mv_q", [P, BATCH, 2]), sb("var_q", [P, BATCH]), sb("rstd_q", [P, BATCH])
        var = sb("var", [P, TILES])
        xn, xn_t = sb("xn", [P, BATCH, D]), sb("xn_t", [P, BATCH, DC, P])
        mean = sb("mean", [P, BATCH, D])
        att = sb("att", [P, BATCH, HEADS, KEYS])
        top, total = sb("top", [P, BATCH, HEADS]), sb("total", [P, BATCH, HEADS])
        att_t = sb("att_t", [P, BATCH, HEADS // 2, P])
        S = {n: ctx.enter_context(nc.semaphore("c_" + n)) for n in
             ("const x_q x weights ones_set ctxt ctxts means means_out meaned var_q rstd_q xn xnt xnts s shift e p pt pts o "
              "var zeroed dve pool").split()}
        m["s_weights"] = S["weights"]
        block = ctx.enter_context(nc.Block())

        @block.sync
        def _(sp):
            sp.dma_start(m["const"][:, :], a["const"]).then_inc(S["const"], 16)
            for half in range(2):
                sp.dma_start(ctx_sb[half * KEYS:(half + 1) * KEYS, :, :],
                             a["ctx_2048"].rearrange("b k d -> k b d")).then_inc(S["const"], 16)
            x_tiles = x[:, :, :].rearrange("p (b t) d -> p b t d", t=TPB)
            x_in = a["x"].rearrange("b (t p) d -> p b t d", p=P)
            sp.dma_start(x_tiles[:, :, TPB - 1, :], x_in[:, :, TPB - 1, :]).then_inc(S["x_q"], 16)
            for b in range(BATCH):
                sp.dma_start(x_tiles[:, b, 0:TPB - 1, :], x_in[:, b, 0:TPB - 1, :]).then_inc(S["x"], 16)
            for dst, src in weights:
                sp.dma_start(dst, src).then_inc(S["weights"], 16)
            for moe in (MOE0, MOE1):
                d = dram[moe.name]
                sp.dma_start(d["slots"].rearrange("(b p) e -> b (p e)", p=P), a[moe.name + "_empty"]).then_inc(s_init, 16)
                for n in ("rows", "sum"):
                    sp.dma_start(d[n][TOKENS:TOKENS + SPARE, :], a["zero_rows"]).then_inc(s_init, 16)
            sp.wait_ge(S["weights"], 16 * len(weights))
            sp.wait_ge(s_init, 96)

        @block.gpsimd
        def _(pool):
            g = nc.gpsimd
            g.memset(ctx_heads[:, :, :, :], 0.0).then_inc(S["zeroed"], 1)
            g.memset(ctx_pairs[:, :, :, :], 0.0).then_inc(S["zeroed"], 1)
            g.memset(m["ones"][:, :], 1.0)
            g.memset(m["mean_w"][:, :], 1.0 / KEYS)
            g.memset(m["power"][:, :], -0.5)
            g.memset(m["eps"][:, :], EPS)
            g.memset(m["before0"][:, 0, :], 0.0)
            g.memset(m["before1"][:, 0, :], 0.0).then_inc(S["ones_set"], 1)
            pool.wait_ge(S["ones_set"], 1)
            own = Steps(pool, S["pool"])
            pool.wait_ge(S["var_q"], 1)
            g.tensor_tensor(rstd_q[:, :], var_q[:, :], m["power"][:, 0:BATCH], ALU.pow).then_inc(S["rstd_q"], 1)
            pool.wait_ge(S["x"], 16 * BATCH)
            for b in range(BATCH):
                pool.wait_ge(S["means_out"], b + 1)
                for t in range(b * TPB, b * TPB + TPB - 1):
                    g.tensor_tensor(x[:, t, :], x[:, t, :], mean[:, b, :], ALU.add).then_inc(S["meaned"], 1)
            own.did(g.memset(q_t, 0.0))
            pool.wait_ge(S["var"], 1)
            own.run(g.tensor_tensor(rstd[:, :], var[:, :], m["power"][:, :], ALU.pow))
            own.run(g.tensor_tensor(rms[:, :], rstd[:, :], rstd[:, :], ALU.mult))
            own.run(g.tensor_tensor(rms[:, :], rms[:, :], mv[:, :, 1], ALU.mult))
            own.run(g.tensor_tensor(rms[:, :], rms[:, :], m["eps"][:, :], ALU.add))
            own.run(g.tensor_tensor(rms[:, :], rms[:, :], m["power"][:, :], ALU.pow))

        @block.scalar
        def _(act):
            sc = nc.scalar
            for b in range(BATCH):
                act.wait_ge(S["means"], b + 1)
                sc.activation(mean[:, b, :], ps[:, 4 + b, :], ACT.Copy).then_inc(S["means_out"], 1)
            for b in range(BATCH):
                act.wait_ge(S["xnt"], b + 1)
                sc.activation(xn_t[:, b].rearrange("p c q -> p (c q)"), ps[:, b, :], ACT.Copy).then_inc(S["xnts"], 1)
            for b in range(BATCH):
                act.wait_ge(S["shift"], b + 1)
                sc.activation(att[:, b], att[:, b], ACT.Exp).then_inc(S["e"], 1)
            for b in range(BATCH):
                act.wait_ge(S["pt"], b + 1)
                for j in range(2):
                    sc.activation(att_t[:, b, 4 * j:4 * j + 4, :].rearrange("p c q -> p (c q)"), ps[:, 2 * (b % 2) + j, :], ACT.Copy).then_inc(S["pts"], 1)

        @block.vector
        def _(dve):
            v = nc.vector
            own = Steps(dve, S["dve"], 0, m["passed"]["dve"])

            def stats_of(src, t, to):
                own.did(v.bn_stats(stats[:, t, :], src))
                own.hold()
                own.did(v.bn_aggr(to, stats[:, t, :]))

            dve.wait_ge(S["const"], 48)
            v.tensor_copy(m["ident16"][:, :], c["ident"])
            v.tensor_copy(m["future16"][:, :], c["future"])
            dve.wait_ge(S["zeroed"], 2)
            for b in range(BATCH):
                dve.wait_ge(S["ctxt"], b + 1)
                for g in range(GH):
                    rows = slice(g * HD, (g + 1) * HD)
                    v.tensor_copy(ctx_heads[rows, b, :, g * KEYS:(g + 1) * KEYS],
                                  ps[rows, b, 0:DC * KEYS].rearrange("p (c k) -> p c k", k=KEYS))
                v.tensor_copy(m["ctx_t"][:, b, :, :], ps[:, b, 0:DC * KEYS].rearrange("p (c k) -> p c k", k=KEYS)).then_inc(S["ctxts"], 1)
            dve.wait_ge(S["x_q"], 16)
            for b in range(BATCH):
                stats_of(x[:, b * TPB + TPB - 1, :], b, mv_q[:, b, :])
            own.wait()
            dve.wait_ge(S["ones_set"], 1)
            v.tensor_scalar(var_q[:, :], mv_q[:, :, 1], EPS, None, ALU.add).then_inc(S["var_q"], 1)
            pairs = ctx_sb[:, :, :].rearrange("p b (j two e) -> p b j two e", two=2, e=HD)
            for half in range(2):
                rows = slice(half * KEYS, (half + 1) * KEYS)
                for b in range(BATCH):
                    own.did(v.tensor_copy(ctx_pairs[rows, b, :, half * HD:(half + 1) * HD], pairs[rows, b, :, half, :]))
            dve.wait_ge(S["rstd_q"], 1)
            for b in range(BATCH):
                v.tensor_scalar(xn[:, b, :], x[:, b * TPB + TPB - 1, :], mv_q[:, b, 0:1], rstd_q[:, b:b + 1], ALU.subtract, ALU.mult).then_inc(S["xn"], 1)
            for b in range(BATCH):
                dve.wait_ge(S["s"], b + 1)
                k = 4 + 2 * (b % 2)
                s2 = ps[:, k:k + 2, :].rearrange("p a (h k) -> p (a h) k", k=KEYS)
                own.run(v.scalar_tensor_tensor(att[:, b], s2, HD ** -0.5, c["allowed"].unsqueeze(1).to_broadcast([P, HEADS, KEYS]), ALU.mult, ALU.mult))
                own.run(v.tensor_tensor(att[:, b], att[:, b], c["barred"].unsqueeze(1).to_broadcast([P, HEADS, KEYS]), ALU.add))
                own.run(v.tensor_reduce(top[:, b, :], att[:, b], AX.X, ALU.max))
                v.tensor_tensor(att[:, b], att[:, b], top[:, b, :].unsqueeze(2).to_broadcast([P, HEADS, KEYS]), ALU.subtract).then_inc(S["shift"], 1)
            for b in range(BATCH):
                dve.wait_ge(S["e"], b + 1)
                own.run(v.tensor_reduce(total[:, b, :], att[:, b], AX.X, ALU.add))
                own.run(v.reciprocal(total[:, b, :], total[:, b, :]))
                v.tensor_tensor(att[:, b], att[:, b], total[:, b, :].unsqueeze(2).to_broadcast([P, HEADS, KEYS]), ALU.mult).then_inc(S["p"], 1)
            dve.wait_ge(S["meaned"], BATCH * (TPB - 1))
            for t in range(TILES):
                if t % TPB < TPB - 1:
                    stats_of(x[:, t, :], t, mv[:, t, :])
            for b in range(BATCH):
                dve.wait_ge(S["o"], b + 1)
                t = b * TPB + TPB - 1
                own.did(v.tensor_tensor(x[:, t, :], x[:, t, :], ps[:, 4 + b, :], ALU.add))
                own.hold()
                stats_of(x[:, t, :], t, mv[:, t, :])
            own.wait()
            v.tensor_scalar(var[:, :], mv[:, :, 1], EPS, None, ALU.add).then_inc(S["var"], 1)

        @block.tensor
        def _(pe):
            mm, tr = nc.tensor.matmul, nc.tensor.transpose
            ident = c["ident"]
            pe.wait_ge(S["const"], 48)
            for b in range(BATCH):
                for k in range(DC):
                    last = tr(ps[:, b, k * KEYS:(k + 1) * KEYS], ctx_sb[0:KEYS, b, k * P:(k + 1) * P], ident[0:KEYS, 0:KEYS])
                last.then_inc(S["ctxt"], 1)
            pe.wait_ge(S["ones_set"], 1)
            for b in range(BATCH):
                mm(ps[:, 4 + b, :], m["mean_w"][:, :], ctx_sb[0:KEYS, b, :], start=True, stop=True).then_inc(S["means"], 1)
            pe.wait_ge(S["ctxts"], BATCH)
            for b in range(BATCH):
                pe.wait_ge(S["xn"], b + 1)
                for k in range(DC):
                    last = tr(ps[:, b, k * P:(k + 1) * P], xn[:, b, k * P:(k + 1) * P], ident)
                last.then_inc(S["xnt"], 1)
            pe.wait_ge(S["means_out"], BATCH)
            for b in range(BATCH):
                pe.wait_ge(S["xnts"], b + 1)
                if b >= 2:
                    pe.wait_ge(S["shift"], b - 1)
                for k in range(DC):
                    last = mm(ps[:, 4 + 2 * (b % 2) + k // 2, (k % 2) * 256:(k % 2) * 256 + 256], xn_t[:, b, k, :],
                              ctx_heads[:, b, k, :], start=True, stop=True)
                last.then_inc(S["s"], 1)
            for b in range(BATCH):
                pe.wait_ge(S["p"], b + 1)
                if b >= 2:
                    pe.wait_ge(S["pts"], 2 * (b - 1))
                flat = att[:, b].rearrange("p h k -> p (h k)")
                for j in range(HEADS // 2):
                    last = tr(ps[:, 2 * (b % 2) + j // 4, (j % 4) * P:(j % 4 + 1) * P], flat[:, j * P:(j + 1) * P], ident)
                last.then_inc(S["pt"], 1)
            for b in range(BATCH):
                pe.wait_ge(S["pts"], 2 * (b + 1))
                for j in range(HEADS // 2):
                    last = mm(ps[:, 4 + b, j * 2 * HD:(j + 1) * 2 * HD], att_t[:, b, j, :], ctx_pairs[:, b, j, :], start=True, stop=True)
                last.then_inc(S["o"], 1)




def front(nc, a, m, c, dram, s_init):
    ctx = ExitStack()
    with ctx:
        def sb(name, shape, dt=F32):
            return ctx.enter_context(nc.sbuf_tensor(name, shape, dt))

        def sem(name):
            return ctx.enter_context(nc.semaphore(name))

        ps, x, ctx_sb = m["psum"], sb("x_sb", [P, TILES, D]), m["ctx"]
        GH = P // HD
        w_kvd, w_qd = sb("w_kvd", [P, DC, LAT]), sb("w_qd", [P, DC, LAT])
        w_kr = sb("w_kr", [P, DC, D // 2])
        w_q = sb("w_q", [LAT, D])
        w_ku, w_vu = sb("w_ku", [LAT, D // 2]), sb("w_vu", [LAT, D])
        w_o = sb("w_o", [P, DC, D])
        w_rt = sb("w_rt", [P, DC, MOE0.routed])
        bias_rt = sb("bias_rt", [P, MOE0.routed])
        ln1, ln2 = sb("ln1", [P, D]), sb("ln2", [P, D])
        mv, rstd, rms = sb("mv", [P, TILES, 2]), sb("rstd", [P, TILES]), sb("rms", [P, TILES])
        q_t = sb("q_t", [P, HEADS, SEQ])
        cross(nc, a, m, c, dram, s_init, x, mv, rstd, rms, q_t[:, :, :], [
            (w_kvd[:, :, :], a["L0_ffn_kv_d_w"].rearrange("(c p) n -> p c n", p=P)),
            (w_qd[:, :, :], a["L0_ffn_q_d_w"].rearrange("(c p) n -> p c n", p=P)),
            (w_kr[:, :, :], a["L0_ffn_rope_k_w"].rearrange("(c p) n -> p c n", p=P)),
            (w_q[:, 0:D // 2], a["L0_ffn_q_u_w"]), (w_q[:, D // 2:D], a["L0_ffn_rope_q_w"]),
            (w_ku[:, :], a["L0_ffn_k_u_w"]), (w_vu[:, :], a["L0_ffn_v_u_w"]),
            (w_o[:, :, :], a["L0_ffn_o_w"].rearrange("(c p) n -> p c n", p=P)),
            (w_rt[:, :, :], a["L0_ffn_router_w"].rearrange("(c p) n -> p c n", p=P)),
            (bias_rt[:, :], a["L0_ffn_router_b"].partition_broadcast(P)),
            (ln1[:, :], a["L0_ffn_ln1_w"].partition_broadcast(P)),
            (ln2[:, :], a["L0_ffn_ln2_w"].partition_broadcast(P))])
        stats, mv_h = sb("stats", [P, TPB, 6]), sb("mv_h", [P, TPB, 2])
        var_h, rms_h = sb("var_h", [P, TPB]), sb("rms_h", [P, TPB])
        y, z = sb("y", [P, TPB, D]), sb("z", [P, TPB, D])
        z_t = sb("z_t", [P, DC, SEQ])
        kv_d, q_d = sb("kv_d", [LAT, SEQ]), sb("q_d", [LAT, SEQ])
        v_sb = sb("v_sb", [P, TPB, D])
        qk = sb("qk", [P, 2, 2 * HEADS, HD])
        rot_a, rot_b = sb("rot_a", [P, 2 * HEADS, ROT]), sb("rot_b", [P, 2 * HEADS, ROT])
        k_t = sb("k_t", [P, DC, SEQ])
        neg_top = sb("neg_top", [P, 2, 2])
        prob = sb("prob", [P, 2, 2, SEQ])
        prob_t = sb("prob_t", [P, 2, 2 * TPB, P])
        den = sb("den", [P, TPB, HEADS])
        over_den, att_t = sb("over_den", [P, HEADS, HD]), sb("att_t", [P, TPB, DC, P])
        ident16, future16 = m["ident16"], m["future16"]
        h = v_sb
        acc = prob[:, :, :, :].rearrange("p a e k -> p (a e) k")
        hn = prob_t[:, :, :, :].rearrange("p a c q -> p (a c q)").rearrange("p (t d) -> p t d", d=D)
        hn_t = sb("hn_t", [P, 2, DC, P])
        r = route_memory(sb, MOE0)

        names = ("zeroed z zt zts kvd qd kvds qds pp pr pv_ qkp qkr vs qkt qts kts st ntop pexp pt pta ptb pv rden rdt rdts "
                 "attd hres acc oproj var2 rms2 hn hnt hnts logit lgs lge masked ranked slotted scattered sent rows_out dve").split()
        S = {n: sem("f_" + n) for n in names}
        r0 = dram["moe0"]
        SCATTERS = TPB * MOE0.top
        LAST = BATCH - 1

        block = ctx.enter_context(nc.Block())


        @block.sync
        def _(sp):
            with sp.Fori(0, BATCH) as b:
                sp.wait_ge(S["acc"], TPB * (b + 1))
                sp.dma_start(r0["sum"][bass.ds(b * SEQ, SEQ), :].rearrange("(t p) d -> p t d", p=P), acc).then_inc(S["rows_out"], 16)
                sp.wait_ge(S["hn"], TPB * (b + 1))
                sp.dma_start(r0["rows"][bass.ds(b * SEQ, SEQ), :].rearrange("(t p) d -> p t d", p=P), hn).then_inc(S["rows_out"], 16)
                hold(sp, S["rows_out"], 32 * (b + 1), m["passed"]["sp"])

        @block.gpsimd
        def _(pool):
            g = nc.gpsimd
            g.memset(r["prob"][:, :, :], -1.0).then_inc(S["zeroed"], 1)
            pool.sem_inc(S["sent"], 1)
            with pool.Fori(0, BATCH) as b:
                for n, t in enumerate(QUERY_ORDER):
                    pool.wait_ge(S["hres"], b * TPB + n + 1)
                    g.tensor_tensor(acc[:, t, :], tile_at(x, b * TPB + t), h[:, t, :], ALU.add).then_inc(S["acc"], 1)
                pool.wait_ge(S["var2"], b + 1)
                g.tensor_tensor(rms_h[:, :], var_h[:, :], m["power"][:, 0:TPB], ALU.pow).then_inc(S["rms2"], 1)
                hold(pool, S["slotted"], b + 1, m["passed"]["pool"])
                scatter(pool, r, range(SCATTERS), r0["slots"], S["scattered"])
                pool.wait_ge(S["scattered"], 16 * SCATTERS * (b + 1))
                pool.sem_inc(S["sent"], 1)

        def prob_t_second(act, sc, b, s):
            act.wait_ge(S["pt"], b * NS + s + 1)
            if s >= 2:
                act.wait_ge(S["pv"], b * NS + s - 1)
            w = (STEPS[s][0] + 1) * 2 * P - 512
            sc.activation(prob_t[:, s % 2, 4:4 + w // P, :].rearrange("p c q -> p (c q)"), ps[:, 5, 0:w], ACT.Copy).then_inc(S["ptb"], 1)

        @block.scalar
        def _(act):
            sc = nc.scalar

            def attention(b):
                for s, (i, hp) in enumerate(STEPS):
                    n, u = (i + 1) * P, s % 2
                    if s >= 2:
                        act.wait_ge(S["pt"], b * NS + s - 1)
                    for e in range(2):
                        act.wait_ge(S["ntop"], (b * NS + s) * 2 + e + 1)
                        sc.activation(prob[:, u, e, 0:n], ps[:, 2 * u + e, 0:n], ACT.Exp, bias=neg_top[:, u, e:e + 1],
                                      accum_out=den[:, i, 2 * hp + e:2 * hp + e + 1]).then_inc(S["pexp"], 1)
                    if s >= 1 and STEPS[s - 1][0] >= 2:
                        prob_t_second(act, sc, b, s - 1)
                if STEPS[NS - 1][0] >= 2:
                    prob_t_second(act, sc, b, NS - 1)

            def project(b, t):
                i = t % 2
                act.wait_ge(S["pp"], b * TPB + t + 1)
                if t >= 2:
                    act.wait_ge(S["qkt"], b * TPB + t - 1)
                sc.activation(qk[:, i, :, 0:ROT], ps[:, 2 * i, :].rearrange("p (h e) -> p h e", e=ROT), ACT.Copy).then_inc(S["qkp"], 1)
                act.wait_ge(S["pv_"], b * TPB + t + 1)
                sc.activation(v_sb[:, t, :], ps[:, 6 + i, :], ACT.Copy).then_inc(S["vs"], 1)
                act.wait_ge(S["qkt"], b * TPB + t + 1)
                for g in range(GH):
                    rows = slice(g * HD, (g + 1) * HD)
                    ins = sc.activation(q_t[rows, :, t * P:(t + 1) * P].rearrange("p (c g) q -> p c g q", g=GH)[:, :, g, :],
                                        ps[rows, 4, :].rearrange("p (c q) -> p c q", q=P), ACT.Copy, scale=HD ** -0.5)
                ins.then_inc(S["qts"], 1)

            def between(b, then):
                if then is not None:
                    for t in range(TPB):
                        act.wait_ge(S["zt"], then * TPB + t + 1)
                        sc.activation(z_t[:, :, t * P:(t + 1) * P], ps[:, 4 + t, :].rearrange("p (c q) -> p c q", q=P), ACT.Copy).then_inc(S["zts"], 1)
                if b is not None:
                    for t in range(TPB):
                        act.wait_ge(S["hnt"], b * TPB + t + 1)
                        if t >= 2:
                            act.wait_ge(S["logit"], b * TPB + t - 1)
                        sc.activation(hn_t[:, t % 2, :, :].rearrange("p c q -> p (c q)"), ps[:, t % 2, :], ACT.Copy).then_inc(S["hnts"], 1)
                if then is not None:
                    act.wait_ge(S["kvd"], then + 1)
                    sc.activation(kv_d[:, :], ps[:, 4, :], ACT.Copy).then_inc(S["kvds"], 1)
                if b is not None:
                    act.wait_ge(S["lgs"], b + 1)
                    sc.activation(r["logit"][:, :, :], r["logit"][:, :, :], ACT.Exp, scale=-1.0).then_inc(S["lge"], 1)
                if then is not None:
                    if b is not None:
                        act.wait_ge(S["acc"], TPB * (b + 1))
                        act.wait_ge(S["hn"], TPB * (b + 1))
                    for t in range(TPB):
                        project(then, t)
                    if b is not None:
                        act.wait_ge(S["rows_out"], 32 * (b + 1))

            between(None, 0)
            with act.Fori(0, LAST) as b:
                attention(b)
                between(b, b + 1)
            attention(LAST)
            between(LAST, None)

        DVE_FIRST, DVE_TURN = 20, 60

        @block.vector
        def _(dve):
            v = nc.vector

            def attention(own, b):
                def maxima(s):
                    u, n = s % 2, (STEPS[s][0] + 1) * P
                    for e in range(2):
                        dve.wait_ge(S["st"], (b * NS + s) * 2 + e + 1)
                        if s >= 2:
                            dve.wait_ge(S["pexp"], (b * NS + s - 2) * 2 + e + 1)
                        v.tensor_reduce(neg_top[:, u, e:e + 1], ps[:, 2 * u + e, 0:n], AX.X, ALU.max, negate=True).then_inc(S["ntop"], 1)

                def denominators(i, s):
                    dve.wait_ge(S["pexp"], (b * NS + s) * 2 + 2)
                    if QUERY_ORDER[0] != i:
                        dve.wait_ge(S["rdt"], b * TPB + QUERY_ORDER.index(i))
                    own.run(v.reciprocal(den[:, i, :], den[:, i, :]))
                    v.tensor_copy(over_den[:, :, :], den[:, i, :].unsqueeze(2).to_broadcast([P, HEADS, HD])).then_inc(S["rden"], 1)

                def attended(i, s):
                    dve.wait_ge(S["rdt"], b * TPB + QUERY_ORDER.index(i) + 1)
                    v.tensor_copy(att_t[:, i].rearrange("p c q -> p (c q)"), ps[:, 5, :]).then_inc(S["rdts"], 1)
                    dve.wait_ge(S["pv"], b * NS + s + 1)
                    dve.wait_ge(S["rdts"], b * TPB + QUERY_ORDER.index(i) + 1)
                    v.tensor_tensor(att_t[:, i].rearrange("p c q -> p (c q)"), ps[:, 6 + i % 2, :],
                                    att_t[:, i].rearrange("p c q -> p (c q)"), ALU.mult).then_inc(S["attd"], 1)

                maxima(0)
                for s in range(NS + 2):
                    if s + 1 < NS:
                        maxima(s + 1)
                    if 1 <= s <= NS:
                        q = s - 1
                        w = min(512, (STEPS[q][0] + 1) * 2 * P)
                        dve.wait_ge(S["pt"], b * NS + q + 1)
                        if q >= 2:
                            dve.wait_ge(S["pv"], b * NS + q - 1)
                        v.tensor_copy(prob_t[:, q % 2, 0:w // P, :].rearrange("p c q -> p (c q)"), ps[:, 4, 0:w]).then_inc(S["pta"], 1)
                    if s >= 2 and STEPS[s - 2][1] == HEADS // 2 - 1:
                        attended(STEPS[s - 2][0], s - 2)
                    if 1 <= s <= NS and STEPS[s - 1][1] == HEADS // 2 - 1:
                        denominators(STEPS[s - 1][0], s - 1)

            def residual(own, b):
                for n, t in enumerate(QUERY_ORDER):
                    dve.wait_ge(S["oproj"], b * TPB + n + 1)
                    v.tensor_tensor(h[:, t, :], y[:, t, :], ps[:, n, :], ALU.add).then_inc(S["hres"], 1)
                    hold(dve, S["hres"], b * TPB + n + 1, m["passed"]["dve"])
                    own.did(v.bn_stats(stats[:, t, :], h[:, t, :]))
                own.hold()
                for t in range(TPB):
                    own.did(v.bn_aggr(mv_h[:, t, :], stats[:, t, :]))
                own.wait()
                own.run(v.tensor_tensor(var_h[:, :], mv_h[:, :, 0], mv_h[:, :, 0], ALU.mult))
                v.scalar_tensor_tensor(var_h[:, :], var_h[:, :], EPS, mv_h[:, :, 1], ALU.add, ALU.add).then_inc(S["var2"], 1)

            def norms(own, b):
                for t in range(TPB):
                    at = bass.ds(b * TPB + t, 1)
                    own.did(v.tensor_scalar(y[:, t, :], tile_at(x, b * TPB + t), mv[:, at, 0:1].rearrange("p a e -> p (a e)"), rstd[:, at], ALU.subtract, ALU.mult))
                    own.wait()
                    v.scalar_tensor_tensor(z[:, t, :], y[:, t, :], rms[:, at], ln1[:, :], ALU.mult, ALU.mult).then_inc(S["z"], 1)

            def rotate(own, b, t):
                i = t % 2
                dve.wait_ge(S["pr"], b * TPB + t + 1)
                src = ps[:, 2 * i + 1, :].rearrange("p (h e) -> p h e", e=ROT)
                cos = c["cos"][:, t * ROT:(t + 1) * ROT].unsqueeze(1).to_broadcast([P, 2 * HEADS, ROT])
                sin = c["sin"][:, t * ROT // 2:(t + 1) * ROT // 2].unsqueeze(1).to_broadcast([P, 2 * HEADS, ROT // 2])
                own.did(v.tensor_tensor(rot_a[:, :, :], src, cos, ALU.mult))
                own.did(v.tensor_tensor(rot_b[:, :, 0:ROT // 2], src[:, :, ROT // 2:ROT], sin, ALU.mult))
                own.did(v.tensor_tensor(rot_b[:, :, ROT // 2:ROT], src[:, :, 0:ROT // 2], sin, ALU.mult))
                own.wait()
                if t >= 2:
                    dve.wait_ge(S["qkt"], b * TPB + t - 1)
                own.did(v.tensor_tensor(qk[:, i, :, ROT:ROT + ROT // 2], rot_a[:, :, 0:ROT // 2], rot_b[:, :, 0:ROT // 2], ALU.subtract))
                v.tensor_tensor(qk[:, i, :, ROT + ROT // 2:HD], rot_a[:, :, ROT // 2:ROT], rot_b[:, :, ROT // 2:ROT], ALU.add).then_inc(S["qkr"], 1)

            def keys_out(b, t):
                dve.wait_ge(S["qkt"], b * TPB + t + 1)
                dve.wait_ge(S["qkr"], b * TPB + t + 1)
                v.tensor_copy(k_t[:, :, t * P:(t + 1) * P], ps[:, 5, :].rearrange("p (c q) -> p c q", q=P)).then_inc(S["kts"], 1)

            def route(own, b, part):
                n = MOE0.routed
                if part == 0:
                    dve.wait_ge(S["logit"], b * TPB + TPB)
                    v.tensor_tensor(r["logit"][:, :, :], ps[:, 2, 0:TPB * 8].rearrange("p (t e) -> p t e", e=8)[:, :, 0:n],
                                    bias_rt[:, :].unsqueeze(1).to_broadcast([P, TPB, n]), ALU.add).then_inc(S["lgs"], 1)
                if part == 1:
                    dve.wait_ge(S["lge"], b + 1)
                    own.run(v.tensor_scalar(r["logit"][:, :, :], r["logit"][:, :, :], 1.0, None, ALU.add))
                    own.run(v.reciprocal(r["prob"][:, :, 0:n], r["logit"][:, :, :]))
                    hold(dve, S["sent"], b + 1, m["passed"]["dve"])
                    choose(nc, own, r, MOE0, c["token"][:, bass.ds(b * TPB, TPB)])
                if part == 2:
                    count(nc, own, r, MOE0, c, m["before0"], S["masked"])
                if part == 3:
                    dve.wait_ge(S["ranked"], b + 1)
                    find_slots(nc, own, r, MOE0, c, m, m["before0"], 6, c["offset0"][:, 0:n])
                    v.tensor_copy(r["slot"][:, :], r["slot_f"][:, :]).then_inc(S["slotted"], 1)

            def between(own, b, then):
                if b is not None:
                    residual(own, b)
                if then is not None:
                    norms(own, then)
                if b is not None:
                    dve.wait_ge(S["rms2"], b + 1)
                    for t in range(TPB):
                        v.scalar_tensor_tensor(hn[:, t, :], h[:, t, :], rms_h[:, t:t + 1], ln2[:, :], ALU.mult, ALU.mult).then_inc(S["hn"], 1)
                if then is not None:
                    dve.wait_ge(S["qd"], then + 1)
                    v.tensor_copy(q_d[:, :], ps[:, 5, :]).then_inc(S["qds"], 1)
                for t in range(TPB):
                    if b is not None:
                        route(own, b, t)
                    if then is not None:
                        rotate(own, then, t)
                        keys_out(then, t)
                if b is not None and then is not None:
                    hold(dve, S["rows_out"], 32 * (b + 1), m["passed"]["dve"])

            dve.wait_ge(S["zeroed"], 1)
            own = Steps(dve, S["dve"], 0, m["passed"]["dve"])
            between(own, None, 0)
            assert own.n == DVE_FIRST, own.n
            with dve.Fori(0, LAST) as b:
                own = Steps(dve, S["dve"], DVE_FIRST + b * DVE_TURN, m["passed"]["dve"])
                attention(own, b)
                between(own, b, b + 1)
                assert own.n == DVE_TURN, own.n
            own = Steps(dve, S["dve"], DVE_FIRST + LAST * DVE_TURN, m["passed"]["dve"])
            attention(own, LAST)
            between(own, LAST, None)

        @block.tensor
        def _(pe):
            mm, tr = nc.tensor.matmul, nc.tensor.transpose
            ident = c["ident"]

            def four(bank, src):
                for k in range(DC):
                    last = tr(ps[:, bank, k * P:(k + 1) * P], src[:, k * P:(k + 1) * P], ident)
                return last

            def attention(b):
                def scores(s):
                    (i, hp), u = STEPS[s], s % 2
                    n = (i + 1) * P
                    for e in range(2):
                        k = (2 * hp + e) // GH
                        if s >= 2:
                            pe.wait_ge(S["pexp"], (b * NS + s - 2) * 2 + e + 1)
                        mm(ps[:, 2 * u + e, 0:n], q_t[:, 2 * hp + e, i * P:(i + 1) * P], k_t[:, k, 0:n], start=True, stop=False)
                        mm(ps[:, 2 * u + e, n - P:n], ident16[:, :], future16[:, :], start=False, stop=True).then_inc(S["st"], 1)

                def attend(s):
                    (i, hp), u = STEPS[s], s % 2
                    pe.wait_ge(S["pta"], b * NS + s + 1)
                    if i >= 2:
                        pe.wait_ge(S["ptb"], b * wide_steps(NS) + wide_steps(s + 1))
                    if hp == 0 and QUERY_ORDER.index(i) >= 2:
                        pe.wait_ge(S["attd"], b * TPB + (2 if i % 2 == QUERY_ORDER[1] % 2 else 1))
                    for j in range(i + 1):
                        for e in range(2):
                            k, g = (2 * hp + e) // GH, (2 * hp + e) % GH
                            cols = slice((2 * hp + e) * HD, (2 * hp + e + 1) * HD)
                            last = mm(ps[g * HD:(g + 1) * HD, 6 + i % 2, k * P:(k + 1) * P], v_sb[:, j, cols],
                                      prob_t[:, u, 2 * j + e, :], start=(j == 0), stop=(j == i))
                    last.then_inc(S["pv"], 1)

                def denominators(i, s):
                    n = QUERY_ORDER.index(i)
                    pe.wait_ge(S["rden"], b * TPB + n + 1)
                    pe.wait_ge(S["ptb"], b * wide_steps(NS) + wide_steps(s))
                    if n >= 1:
                        pe.wait_ge(S["rdts"], b * TPB + n)
                    four(5, over_den[:, :, :].rearrange("p h e -> p (h e)")).then_inc(S["rdt"], 1)

                scores(0)
                scores(1)
                for s in range(NS + 2):
                    if s + 2 < NS:
                        scores(s + 2)
                    elif s < NS:
                        pe.wait_ge(S["pexp"], (b * NS + s) * 2 + 2)
                    if s >= 2 and STEPS[s - 2][1] == HEADS // 2 - 1:
                        denominators(STEPS[s - 2][0], s)
                    if 1 <= s <= NS:
                        attend(s - 1)
                    if s < NS:
                        if STEPS[s][0] >= 2 and tiles_through(s) > 0:
                            pe.wait_ge(S["rdts"], b * TPB + tiles_through(s))
                        for j in range(STEPS[s][0] + 1):
                            for e in range(2):
                                q = 2 * j + e
                                last = tr(ps[:, 4 + q // 4, (q % 4) * P:(q % 4 + 1) * P], prob[:, s % 2, e, j * P:(j + 1) * P], ident)
                        last.then_inc(S["pt"], 1)

            def output(b):
                for n, t in enumerate(QUERY_ORDER):
                    pe.wait_ge(S["attd"], b * TPB + n + 1)
                    for k in range(DC):
                        last = mm(ps[:, n, :], att_t[:, t, k, :], w_o[:, k, :], start=(k == 0), stop=(k == DC - 1))
                    last.then_inc(S["oproj"], 1)

            def logits(b):
                def flip(t):
                    pe.wait_ge(S["hn"], b * TPB + t + 1)
                    if t >= 2:
                        pe.wait_ge(S["hnts"], b * TPB + t - 1)
                    four(t % 2, hn[:, t, :]).then_inc(S["hnt"], 1)

                flip(0)
                for t in range(TPB):
                    if t + 1 < TPB:
                        flip(t + 1)
                    pe.wait_ge(S["hnts"], b * TPB + t + 1)
                    for k in range(DC):
                        last = mm(ps[:, 2, t * 8:t * 8 + MOE0.routed], hn_t[:, t % 2, k, :], w_rt[:, k, :], start=(k == 0), stop=(k == DC - 1))
                    last.then_inc(S["logit"], 1)

            def down(b):
                pe.wait_ge(S["zts"], TPB * (b + 1))
                for bank, w, done in ((4, w_kvd, "kvd"), (5, w_qd, "qd")):
                    for k in range(DC):
                        last = mm(ps[:, bank, :], w[:, k, :], z_t[:, k, :], start=(k == 0), stop=(k == DC - 1))
                    last.then_inc(S[done], 1)
                pe.wait_ge(S["kvds"], b + 1)
                pe.wait_ge(S["qds"], b + 1)

            def project(b, t):
                i, q = t % 2, slice(t * P, (t + 1) * P)
                if t >= 2:
                    pe.wait_ge(S["vs"], b * TPB + t - 1)
                mm(ps[:, 2 * i, 0:256], q_d[:, q], w_q[:, 0:256], start=True, stop=True)
                mm(ps[:, 2 * i, 256:512], kv_d[:, q], w_ku[:, :], start=True, stop=True).then_inc(S["pp"], 1)
                mm(ps[:, 2 * i + 1, 0:256], q_d[:, q], w_q[:, 256:512], start=True, stop=True)
                for k in range(DC):
                    last = mm(ps[:, 2 * i + 1, 256:512], z_t[:, k, q], w_kr[:, k, :], start=(k == 0), stop=(k == DC - 1))
                last.then_inc(S["pr"], 1)
                mm(ps[:, 6 + i, :], kv_d[:, q], w_vu[:, :], start=True, stop=True).then_inc(S["pv_"], 1)

            def between(b, then):
                if b is not None:
                    output(b)
                if then is not None:
                    for t in range(TPB):
                        pe.wait_ge(S["z"], then * TPB + t + 1)
                        four(4 + t, z[:, t, :]).then_inc(S["zt"], 1)
                if b is not None:
                    pe.wait_ge(S["hres"], TPB * (b + 1))
                    logits(b)
                if then is not None:
                    down(then)
                    project(then, 0)
                    if b is not None:
                        pe.wait_ge(S["lgs"], b + 1)
                for t in range(TPB):
                    if then is not None and t + 1 < TPB:
                        project(then, t + 1)
                    if b is not None and t == 2:
                        if then is not None:
                            pe.wait_ge(S["vs"], then * TPB + t + 1)
                        pe.wait_ge(S["masked"], b + 1)
                        places(nc, r, MOE0, c, m, m["before0"], 6).then_inc(S["ranked"], 1)
                    if then is not None:
                        pe.wait_ge(S["qkp"], then * TPB + t + 1)
                        pe.wait_ge(S["qkr"], then * TPB + t + 1)
                        if t >= 1:
                            pe.wait_ge(S["qts"], then * TPB + t)
                            pe.wait_ge(S["kts"], then * TPB + t)
                        flat = qk[:, t % 2, :, :].rearrange("p h e -> p (h e)")
                        four(4, flat[:, 0:D])
                        four(5, flat[:, D:2 * D]).then_inc(S["qkt"], 1)
                if then is not None:
                    pe.wait_ge(S["qts"], TPB * (then + 1))
                    pe.wait_ge(S["kts"], TPB * (then + 1))
                    pe.wait_ge(S["vs"], TPB * (then + 1))
                    if b is not None:
                        pe.wait_ge(S["slotted"], b + 1)

            between(None, 0)
            with pe.Fori(0, LAST) as b:
                attention(b)
                between(b, b + 1)
            attention(LAST)
            between(LAST, None)




def mixture(nc, a, m, c, d, moe, before, out):
    ctx = ExitStack()
    with ctx:
        def sb(name, shape, dt=F32):
            return ctx.enter_context(nc.sbuf_tensor(f"{moe.name}_{name}", shape, dt))

        def sem(name):
            return ctx.enter_context(nc.semaphore(f"{moe.name}_{name}"))

        ps = m["psum"]
        E, N, G, I = moe.experts, moe.tiles, moe.groups, moe.inner
        full, n_fc = E * BLOCKS, len(moe.fc)
        ident = c["ident"]
        w_up = sb("w_up", [P, RING * DC, moe.up])
        w_down = sb("w_down", [P, RING * n_fc, D])
        count_i, tiles_of = sb("count_i", [P, E], I32), sb("tiles_of", [P, E])
        ends, starts = sb("ends", [P, E]), sb("starts", [P, E])
        starts_i = sb("starts_i", [1, E], I32)
        at_or_before, begun = sb("at_or_before", [P, G, E]), sb("begun", [P, G])
        first, valid = sb("first", [P, G]), sb("valid", [P, G])
        block_f, block = sb("block_f", [P, G]), sb("block", [P, G], I32)
        pair_i, pair = sb("pair_i", [P, G], I32), sb("pair", [P, G, 2])
        of_tile = sb("of_tile", [1, 2, G * P], I32)
        table = sb("table", [P, G, 2 * P])
        ids, weight = sb("ids", [P, G * P], I32), sb("weight", [P, G * P])
        idx = [sb(f"idx{u}", [P, 1], I32) for u in range(GROUP)]
        rows = [sb(f"rows{u}", [P, D]) for u in range(GROUP)]
        rows_hi = [sb(f"rows_hi{u}", [P, DC * P], F32R) for u in range(2)]
        rows_lo = [sb(f"rows_lo{u}", [P, DC * P], F32R) for u in range(2)]
        w_hi = [sb(f"w_hi{u}", [P, DC * 2 * I], F32R) for u in range(SPLITS)]
        w_lo = [sb(f"w_lo{u}", [P, DC * 2 * I], F32R) for u in range(SPLITS)]
        gate, hid = [sb(f"gate{u}", [P, I]) for u in range(2)], [sb(f"hid{u}", [P, n_fc * P]) for u in range(2)]
        hid_t = [sb(f"hid_t{u}", [P, n_fc, P]) for u in range(2)]
        if moe.tail:
            tail_t = [sb(f"tail_t{u}", [P, P], F32R) for u in range(2)]
            tail_hi = [sb(f"tail_hi{u}", [P, D], F32R) for u in range(GROUP)]
            tail_lo = [sb(f"tail_lo{u}", [P, D], F32R) for u in range(GROUP)]
            tail_made = {n: sem("tail_" + n) for n in "t hi lo".split()}
        res = [sb(f"res{u}", [P, D]) for u in range(RESULTS)]
        loaded, gathered = m["loaded"], m["gathered"]
        loaded_0 = 0 if moe is MOE0 else MOE0.loads * (MOE0.experts // RING)
        gathered_0 = 0 if moe is MOE0 else 16 * (MOE0.tiles // GROUP)
        S = {n: sem(n) for n in ("counted chain tiled blocks flipped tables listed ready down added stored").split()}
        T, tiles_0 = m["tile_steps"], 0 if moe is MOE0 else MOE0.tiles

        def tiles_done(eng, name, count):
            if not isinstance(count, int) or count > 0:
                eng.wait_ge(T[name], tiles_0 + count)

        def groups(eng, body):
            n = N // GROUP
            body(0, False)
            with eng.Fori(1, n - 1) as g:
                body(g, False)
            body(n - 1, True)

        block_ = ctx.enter_context(nc.Block())

        @block_.sync
        def _(sp):
            def load(e, u):
                up = w_up[:, u * DC:(u + 1) * DC, :]
                if isinstance(e, int) and e < moe.first:
                    gate_w, up_w, down_w = a["L0_ffn_sh_gate"], a["L0_ffn_sh_up"], a["L0_ffn_sh_down"]
                else:
                    pick = (lambda w: w[e - moe.first]) if isinstance(e, int) else \
                        (lambda w: w[bass.ds(e - moe.first, 1), :, :].rearrange("a d n -> (a d) n"))
                    names = ("L0_ffn_r_gate", "L0_ffn_r_up", "L0_ffn_r_down") if moe is MOE0 else \
                        ("L1_ffn_w_gate", "L1_ffn_w_up", "L1_ffn_w_down")
                    gate_w, up_w, down_w = (pick(a[n]) for n in names)
                sp.dma_start(up[:, :, 0:I], gate_w.rearrange("(c p) n -> p c n", p=P)).then_inc(loaded[u], 16)
                sp.dma_start(up[:, :, I:2 * I], up_w.rearrange("(c p) n -> p c n", p=P)).then_inc(loaded[u], 16)
                for j, (f, w) in enumerate(moe.fc):
                    sp.dma_start(w_down[0:w, u * n_fc + j, :], down_w[f:f + w, :]).then_inc(loaded[u], 16)
                if moe.tail:
                    sp.dma_start(w_down[w:2 * w, u * n_fc + j, :], down_w[f:f + w, :]).then_inc(loaded[u], 16)

            for u in range(RING):
                load(u, u)
            for u in range(RING):
                sp.wait_ge(loaded[u], loaded_0 + moe.loads)
                sp.sem_inc(S["ready"], 1)
            sp.wait_ge(S["tiled"], 1)
            with sp.Fori(1, E // RING) as g:
                for u in range(RING):
                    free = sp.value_load(starts_i[0:1, bass.ds(g * RING + u - RING + 1, 1)], min_val=1, max_val=N)
                    hold(sp, S["down"], free, m["passed"]["sp"])
                    load(g * RING + u, u)
                    sp.wait_ge(loaded[u], loaded_0 + moe.loads * (g + 1))
                    sp.sem_inc(S["ready"], 1)
            if out is not None:
                sp.wait_ge(S["added"], 16 * N)
                sp.dma_start(out.rearrange("b s d -> (b s) d"), d["sum"][0:TOKENS, :]).then_inc(S["stored"], 16)
                sp.wait_ge(S["stored"], 16)

        @block_.gpsimd
        def _(pool):
            g = nc.gpsimd
            pool.wait_ge(S["blocks"], 1)
            table_rows = d["slots"].rearrange("(b p) e -> b (p e)", p=P)
            for j in range(G):
                pool.indirect_dma_start(table[:, j, :], None, table_rows, bass.IndirectOffsetOnAxis(block[:, j:j + 1], 0)).then_inc(S["tables"], 16)
            pool.wait_ge(S["listed"], 1)

            def gather(t, u):
                since(pool, S["added"], 16 * (t - GROUP + 1))
                g.tensor_copy(idx[u][:, :], ids[:, bass.ds(t, 1)]).then_inc(T["copied"], 1)
                tiles_done(pool, "copied", t + 1)
                tiles_done(pool, "rt", t - GROUP + 1)
                pool.sem_inc(m["passed"]["pool"], 1)
                pool.indirect_dma_start(rows[u][:, :], None, d["rows"], bass.IndirectOffsetOnAxis(idx[u][:, :], 0)).then_inc(gathered[u], 16)

            def tiles(g, last):
                for u in range(GROUP):
                    t = g * GROUP + u
                    if not last or u < GROUP - AHEAD:
                        gather(t + AHEAD, (u + AHEAD) % GROUP)
                    tiles_done(pool, "res", t + 1)
                    since(pool, S["added"], 16 * t)
                    pool.sem_inc(m["passed"]["pool"], 1)
                    pool.indirect_dma_start(d["sum"], bass.IndirectOffsetOnAxis(idx[u][:, :], 0), res[u % RESULTS][:, :], None,
                                            compute_op=ALU.add).then_inc(S["added"], 16)

            for t in range(AHEAD):
                gather(t, t)
            groups(pool, tiles)
            pool.wait_ge(S["added"], 16 * N)

        @block_.scalar
        def _(act):
            sc = nc.scalar

            def flip(t, u):
                i = u % 2
                tiles_done(act, "rt", t + 1)
                tiles_done(act, "up", t - 1)
                sc.activation(rows_hi[i][:, :], ps[:, i, :], ACT.Copy).then_inc(T["rth"], 1)

            def expert_of(t):
                needed = act.value_load(of_tile[0:1, 1, bass.ds(t, 1)], min_val=1, max_val=E)
                return (needed - 1) % RING, needed

            def split(t, u, at, needed):
                act.wait_ge(S["ready"], needed)
                tiles_done(act, "up", t - SPLITS + 1)
                act.sem_inc(m["passed"]["act"], 1)
                sc.activation(w_hi[u % SPLITS][:, :], w_up[:, bass.ds(at * DC, DC), :].rearrange("p a n -> p (a n)"), ACT.Copy).then_inc(T["wh"], 1)

            def tail_of_hidden(t, u):
                act.wait_ge(T["ht"], tiles_0 + t + 1)
                since(act, S["down"], t - 1)
                sc.activation(tail_t[u % 2][:, :], ps[:, 7, 0:P], ACT.Copy).then_inc(tail_made["t"], 1)

            def tail_of_weights(t, u, at, needed):
                act.wait_ge(S["ready"], needed)
                since(act, S["down"], t - GROUP + 1)
                act.sem_inc(m["passed"]["act"], 1)
                sc.activation(tail_hi[u % GROUP][:, :], tile_at(w_down, at * n_fc + n_fc - 1), ACT.Copy).then_inc(tail_made["hi"], 1)

            def silu(t, u):
                i = u % 2
                tiles_done(act, "up", t + 1)
                tiles_done(act, "hidden", t - 1)
                sc.activation(gate[i][:, :], ps[:, 2 + i, 0:I], ACT.Silu).then_inc(T["silu"], 1)

            def tiles(g, last):
                for u in range(GROUP):
                    i, t = u % 2, g * GROUP + u
                    if moe.tail:
                        tail_of_hidden(t, u)
                    if not last or u < GROUP - 2:
                        flip(t + 2, u)
                    if not last or u < GROUP - SPLITS:
                        at, needed = expert_of(t + SPLITS)
                        if moe.tail:
                            tail_of_weights(t + SPLITS, u + SPLITS, at, needed)
                    if not last or u < GROUP - 1:
                        silu(t + 1, u + 1)
                    if not last or u < GROUP - SPLITS:
                        split(t + SPLITS, u + SPLITS, at, needed)
                    act.wait_ge(S["down"], t + 1)
                    since(act, S["added"], 16 * (t - RESULTS + 1))
                    sc.activation(res[u % RESULTS][:, :], ps[:, 5 + i, :], ACT.Copy, scale=weight[:, bass.ds(t, 1)]).then_inc(T["res"], 1)

            act.wait_ge(S["listed"], 1)
            for t in range(SPLITS):
                at, needed = expert_of(t)
                if moe.tail:
                    tail_of_weights(t, t, at, needed)
                split(t, t, at, needed)
            flip(0, 0)
            flip(1, 1)
            silu(0, 0)
            groups(act, tiles)

        @block_.vector
        def _(dve):
            v = nc.vector
            own = Steps(dve, S["chain"])
            dve.wait_ge(S["counted"], 1)
            if moe.first:
                own.did(v.memset(tiles_of[:, 0:moe.first], float(BLOCKS)))
            own.run(v.tensor_scalar(count_i[:, 0:moe.routed], ps[:, 0, 0:moe.routed], float(P - 1), None, ALU.add))
            own.run(v.tensor_scalar(count_i[:, 0:moe.routed], count_i[:, 0:moe.routed], P.bit_length() - 1, None, ALU.logical_shift_right))
            own.run(v.tensor_scalar(tiles_of[:, moe.first:E], count_i[:, 0:moe.routed], 1.0, None, ALU.max))
            own.run(v.tensor_tensor_scan(ends[:, :], m["ones"][:, 0:E], tiles_of[:, :], 0.0, ALU.mult, ALU.add))
            own.run(v.tensor_tensor(starts[:, :], ends[:, :], tiles_of[:, :], ALU.subtract))
            v.tensor_copy(starts_i[:, :], starts[0:1, :]).then_inc(S["tiled"], 1)
            for j in range(G):
                t = c["tile"][:, j:j + 1]
                own.run(v.tensor_scalar(at_or_before[:, j, :], starts[:, :], t, None, ALU.is_le, ALU.add, accum_out=begun[:, j:j + 1]))
                own.run(v.tensor_tensor(at_or_before[:, j, :], at_or_before[:, j, :], starts[:, :], ALU.mult))
                own.run(v.tensor_reduce(first[:, j:j + 1], at_or_before[:, j, :], AX.X, ALU.max))
                own.did(v.tensor_tensor(valid[:, j:j + 1], t, ends[:, E - 1:E], ALU.is_lt))
                own.run(v.tensor_tensor(first[:, j:j + 1], t, first[:, j:j + 1], ALU.subtract))
                own.run(v.scalar_tensor_tensor(block_f[:, j:j + 1], begun[:, j:j + 1], float(BLOCKS), first[:, j:j + 1], ALU.mult, ALU.add))
                own.run(v.scalar_tensor_tensor(block_f[:, j:j + 1], block_f[:, j:j + 1], -float(BLOCKS + full), valid[:, j:j + 1], ALU.add, ALU.mult))
            own.did(v.tensor_scalar(pair_i[:, :], begun[:, :], -1.0, None, ALU.add))
            v.tensor_scalar(block[:, :], block_f[:, :], float(full), None, ALU.add).then_inc(S["blocks"], 1)
            own.wait()
            own.run(v.tensor_scalar(pair_i[:, :], pair_i[:, :], RING - 1, None, ALU.bitwise_and))
            own.did(v.tensor_copy(pair[:, :, 0], pair_i[:, :]))
            v.tensor_copy(pair[:, :, 1], begun[:, :]).then_inc(S["tiled"], 1)
            dve.wait_ge(S["flipped"], 1)
            for j in range(G):
                own.did(v.tensor_copy(ids[:, j * P:(j + 1) * P], ps[:, 1 + 2 * j, 0:P]))
                own.did(v.tensor_scalar(weight[:, j * P:(j + 1) * P], ps[:, 2 + 2 * j, 0:P], 1.0 / moe.scaling, None, ALU.mult))
            own.wait()
            v.tensor_copy(of_tile[:, :, :].rearrange("p a t -> p (a t)"), ps[0:1, 5, 0:2 * G * P]).then_inc(S["listed"], 1)
            dve.wait_ge(S["listed"], 1)

            def flip(t, u):
                i = u % 2
                tiles_done(dve, "ht", t + 1)
                since(dve, S["down"], t - 1)
                if not moe.tail:
                    v.tensor_copy(hid_t[i][:, :, :].rearrange("p c q -> p (c q)"), ps[:, 4, 0:n_fc * P]).then_inc(T["hts"], 1)
                else:
                    v.tensor_copy(hid_t[i][:, 0, :], ps[:, 4, 0:P])
                    dve.wait_ge(tail_made["t"], t + 1)
                    lo = tail_t[i][P // 2:P, :]
                    v.tensor_tensor(lo, ps[P // 2:P, 7, 0:P], lo.bitcast(F32), ALU.subtract).then_inc(T["hts"], 1)

            def rows_rest(t, u):
                i = u % 2
                tiles_done(dve, "rth", t + 1)
                tiles_done(dve, "up", t - 1)
                v.tensor_tensor(rows_lo[i][:, :], ps[:, i, :], rows_hi[i][:, :].bitcast(F32), ALU.subtract).then_inc(T["rts"], 1)

            def split_rest(t, u, at):
                tiles_done(dve, "wh", t + 1)
                tiles_done(dve, "up", t - SPLITS + 1)
                dve.sem_inc(m["passed"]["dve"], 1)
                v.tensor_tensor(w_lo[u % SPLITS][:, :], w_up[:, bass.ds(at * DC, DC), :].rearrange("p a n -> p (a n)"),
                                w_hi[u % SPLITS][:, :].bitcast(F32), ALU.subtract).then_inc(T["wl"], 1)

            def tail_rest(t, u, at):
                dve.wait_ge(tail_made["hi"], t + 1)
                since(dve, S["down"], t - GROUP + 1)
                dve.sem_inc(m["passed"]["dve"], 1)
                v.tensor_tensor(tail_lo[u % GROUP][:, :], tile_at(w_down, at * n_fc + n_fc - 1),
                                tail_hi[u % GROUP][:, :].bitcast(F32), ALU.subtract).then_inc(tail_made["lo"], 1)

            def product(t, u):
                i = u % 2
                tiles_done(dve, "silu", t + 1)
                tiles_done(dve, "ht", t - 1)
                if moe.tail:
                    v.tensor_tensor(hid[i][:, I:I + moe.tail], gate[i][:, I - moe.tail:I], ps[:, 2 + i, 2 * I - moe.tail:2 * I], ALU.mult)
                v.tensor_tensor(hid[i][:, 0:I], gate[i][:, :], ps[:, 2 + i, I:2 * I], ALU.mult).then_inc(T["hidden"], 1)

            def tiles(g, last):
                for u in range(GROUP):
                    t = g * GROUP + u
                    flip(t, u)
                    if not last or u < GROUP - 3:
                        at = place_of(t + 3)
                    if not last or u < GROUP - 2:
                        rows_rest(t + 2, u)
                    if moe.tail and (not last or u < GROUP - 3):
                        tail_rest(t + 3, u + 3, at)
                    if not last or u < GROUP - 1:
                        product(t + 1, u + 1)
                    if not last or u < GROUP - 3:
                        split_rest(t + 3, u + 3, at)

            def place_of(t):
                return dve.value_load(of_tile[0:1, 0, bass.ds(t, 1)], min_val=0, max_val=RING - 1)

            for t in range(3):
                at = place_of(t)
                split_rest(t, t, at)
                if moe.tail:
                    tail_rest(t, t, at)
            rows_rest(0, 0)
            rows_rest(1, 1)
            product(0, 0)
            groups(dve, tiles)

        @block_.tensor
        def _(pe):
            mm, tr = nc.tensor.matmul, nc.tensor.transpose
            mm(ps[:, 0, 0:moe.routed], m["ones"][:, :], before[:, TPB, :], start=True, stop=True).then_inc(S["counted"], 1)
            pe.wait_ge(S["tiled"], 2)
            pe.wait_ge(S["tables"], 16 * G)
            for j in range(G):
                for e in range(2):
                    tr(ps[:, 1 + 2 * j + e, 0:P], table[:, j, :].rearrange("p (s e) -> p e s", e=2)[:, e, :], ident)
            for e in range(2):
                for j in range(G):
                    last = mm(ps[0:1, 5, (e * G + j) * P:(e * G + j + 1) * P], pair[:, j, e:e + 1], ident, start=True, stop=True)
            last.then_inc(S["flipped"], 1)
            pe.wait_ge(S["listed"], 1)

            def flip(g, u):
                i, t = u % 2, g * GROUP + u
                pe.wait_ge(gathered[u], gathered_0 + 16 * (g + 1))
                tiles_done(pe, "rts", t - 1)
                for k in range(DC):
                    last = tr(ps[:, i, k * P:(k + 1) * P], rows[u][:, k * P:(k + 1) * P], ident)
                last.then_inc(T["rt"], 1)

            def load(what, t, least, most):
                return pe.value_load(of_tile[0:1, what, bass.ds(t, 1)], min_val=least, max_val=most)

            def up(g, u):
                i, t = u % 2, g * GROUP + u
                tiles_done(pe, "rts", t + 1)
                tiles_done(pe, "hidden", t - 1)
                tiles_done(pe, "wl", t + 1)
                for k in range(DC):
                    rows_k, w_k = slice(k * P, (k + 1) * P), slice(k * 2 * I, (k + 1) * 2 * I)
                    hi, lo = rows_hi[i][:, rows_k], rows_lo[i][:, rows_k]
                    w_h, w_l = w_hi[u % SPLITS][:, w_k], w_lo[u % SPLITS][:, w_k]
                    mm(ps[:, 2 + i, 0:2 * I], hi, w_h, start=(k == 0), stop=False)
                    mm(ps[:, 2 + i, 0:2 * I], hi, w_l, start=False, stop=False)
                    last = mm(ps[:, 2 + i, 0:2 * I], lo, w_h, start=False, stop=(k == DC - 1))
                last.then_inc(T["up"], 1)

            def tiles(g, last):
                at = load(0, g * GROUP, 0, RING - 1)
                for u in range(GROUP):
                    i, t = u % 2, g * GROUP + u
                    more, over = divmod(u + 1, GROUP)
                    if not last or u < GROUP - 1:
                        at_next = load(0, t + 1, 0, RING - 1)
                    tiles_done(pe, "hidden", t + 1)
                    tiles_done(pe, "hts", t)
                    for j in range(n_fc):
                        at_tail = moe.tail and j == n_fc - 1
                        done = tr(ps[:, 7, 0:P] if at_tail else ps[:, 4, j * P:(j + 1) * P], hid[i][:, j * P:(j + 1) * P], ident)
                    done.then_inc(T["ht"], 1)
                    if not last or u < GROUP - 2:
                        flip(g + (u + 2) // GROUP, (u + 2) % GROUP)
                    if not last or u < GROUP - 1:
                        up(g + more, over)
                    tiles_done(pe, "hts", t + 1)
                    tiles_done(pe, "res", t - 1)
                    whole = n_fc - (moe.tail > 0)
                    for j in range(whole):
                        done = mm(ps[:, 5 + i, :], hid_t[i][:, j, :], tile_at(w_down, at * n_fc + j), start=(j == 0), stop=(j == n_fc - 1))
                    if moe.tail:
                        pe.wait_ge(tail_made["lo"], t + 1)
                        mm(ps[:, 5 + i, :], tail_t[i][:, :], tail_hi[u][:, :], start=False, stop=False)
                        done = mm(ps[:, 5 + i, :], tail_t[i][:, :], tail_lo[u][:, :], start=False, stop=True)
                    done.then_inc(S["down"], 1)
                    at = at_next

            flip(0, 0)
            flip(0, 1)
            up(0, 0)
            groups(pe, tiles)




def middle(nc, a, m, c, dram):
    ctx = ExitStack()
    with ctx:
        def sb(name, shape, dt=F32):
            return ctx.enter_context(nc.sbuf_tensor("m_" + name, shape, dt))

        def sem(name):
            return ctx.enter_context(nc.semaphore("m_" + name))

        ps, x, ctx_sb = m["psum"], sb("x_sb", [P, TILES, D]), m["ctx"]
        N = MOE1.routed
        w_rt = sb("w_rt", [P, DC, N])
        mask_u8, mask, barred = sb("mask_u8", [P, BATCH, KEYS], U8), sb("mask", [P, BATCH, KEYS]), sb("barred", [P, BATCH, KEYS])
        any_key = sb("any_key", [P, BATCH])
        stats, mv, rstd, var_e = sb("stats", [P, TPB, 6]), sb("mv", [P, TPB, 2]), sb("rstd", [P, TPB]), sb("var_e", [P, TPB])
        stats2, mv2, rstd2, var2 = sb("stats2", [P, TPB, 6]), sb("mv2", [P, TPB, 2]), sb("rstd2", [P, TPB]), sb("var2", [P, TPB])
        xn, xn_t = sb("xn", [P, TPB, D]), sb("xn_t", [P, DC, SEQ])
        att, top, den = sb("att", [P, TPB, KEYS]), sb("top", [P, TPB]), sb("den", [P, TPB])
        att_t = sb("att_t", [KEYS, TPB, P])
        x3, hn, hn_t = sb("x3", [P, TPB, D]), sb("hn", [P, TPB, D]), sb("hn_t", [P, 2, DC, P])
        top_l, sum_l = sb("top_l", [P, TPB]), sb("sum_l", [P, TPB])
        r = route_memory(sb, MOE1)
        send = {"slot": r["slot"], "entry": sb("entry_out", [P, TPB * MOE1.top, 2])}
        names = ("w mask x_in var rstd xn ft fe s shift e p pt pts o x3 var2 rstd2 hn logit lsh le masked ranked "
                 "slotted scattered rows_out dve").split()
        S = {n: sem(n) for n in names}
        r0, r1 = dram["moe0"], dram["moe1"]
        SCATTERS = TPB * MOE1.top
        EARLY = 12

        def sequences(eng, body):
            body(0, True, False)
            with eng.Fori(1, BATCH - 1) as b:
                body(b, False, False)
            body(BATCH - 1, False, True)

        block = ctx.enter_context(nc.Block())

        @block.sync
        def _(sp):
            sp.dma_start(mask_u8[:, :, :].rearrange("p b k -> p (b k)"), a["mask_BxS2_bk0"].rearrange("b k -> (b k)").partition_broadcast(P)).then_inc(S["mask"], 16)
            for b in range(BATCH):
                sp.dma_start(x[:, b * TPB:(b + 1) * TPB, :], r0["sum"][b * SEQ:(b + 1) * SEQ, :].rearrange("(t p) d -> p t d", p=P)).then_inc(S["x_in"], 16)
                if b == 0:
                    sp.dma_start(w_rt[:, :, :], a["L1_router_t"].rearrange("(c p) n -> p c n", p=P)).then_inc(S["w"], 16)
                sp.wait_ge(S["x_in"], 16 * (b + 1))
            with sp.Fori(0, BATCH) as b:
                sp.wait_ge(S["x3"], TPB * (b + 1))
                sp.dma_start(r1["sum"][bass.ds(b * SEQ, SEQ), :].rearrange("(t p) d -> p t d", p=P), x3[:, :, :]).then_inc(S["rows_out"], 16)
                sp.wait_ge(S["hn"], TPB * (b + 1))
                sp.dma_start(r1["rows"][bass.ds(b * SEQ, SEQ), :].rearrange("(t p) d -> p t d", p=P), hn[:, :, :]).then_inc(S["rows_out"], 16)
                hold(sp, S["rows_out"], 32 * (b + 1), m["passed"]["sp"])

        @block.gpsimd
        def _(pool):
            g = nc.gpsimd

            def first_norm(b):
                pool.wait_ge(S["var"], b + 1)
                g.tensor_tensor(rstd[:, :], var_e[:, :], m["power"][:, 0:TPB], ALU.pow).then_inc(S["rstd"], 1)

            def sequence(b, first, last):
                pool.wait_ge(S["var2"], b + 1)
                g.tensor_tensor(rstd2[:, :], var2[:, :], m["power"][:, 0:TPB], ALU.pow).then_inc(S["rstd2"], 1)
                if not last:
                    first_norm(b + 1)
                if not first:
                    scatter(pool, send, range(EARLY, SCATTERS), r1["slots"], S["scattered"])
                hold(pool, S["slotted"], b + 1, m["passed"]["pool"])
                scatter(pool, send, range(EARLY), r1["slots"], S["scattered"])

            first_norm(0)
            sequences(pool, sequence)
            scatter(pool, send, range(EARLY, SCATTERS), r1["slots"], S["scattered"])
            pool.wait_ge(S["scattered"], 16 * SCATTERS * BATCH)

        @block.scalar
        def _(act):
            sc = nc.scalar

            def normed_out(b):
                for t in range(TPB):
                    act.wait_ge(S["ft"], b * 2 * TPB + t + 1)
                    sc.activation(xn_t[:, :, t * P:(t + 1) * P], ps[:, t % 2, :].rearrange("p (c q) -> p c q", q=P), ACT.Copy).then_inc(S["fe"], 1)

            def softmax(b):
                act.wait_ge(S["shift"], b + 1)
                sc.activation(att[:, :, :], att[:, :, :], ACT.Exp).then_inc(S["e"], 1)
                act.wait_ge(S["pt"], b + 1)
                sc.activation(att_t[:, :, :].rearrange("p t q -> p (t q)"), ps[0:KEYS, 5, :], ACT.Copy).then_inc(S["pts"], 1)

            def sequence(b, first, last):
                for t in range(TPB):
                    act.wait_ge(S["ft"], b * 2 * TPB + TPB + t + 1)
                    if t >= 2:
                        act.wait_ge(S["logit"], b * TPB + t - 1)
                    sc.activation(hn_t[:, t % 2, :, :].rearrange("p c q -> p (c q)"), ps[:, t % 2, :], ACT.Copy).then_inc(S["fe"], 1)
                if not last:
                    normed_out(b + 1)
                act.wait_ge(S["lsh"], b + 1)
                sc.activation(r["logit"][:, :, :], r["logit"][:, :, :], ACT.Exp).then_inc(S["le"], 1)
                if not last:
                    softmax(b + 1)

            normed_out(0)
            softmax(0)
            sequences(act, sequence)

        DVE_FIRST, DVE_TURN = 14, 52

        @block.vector
        def _(dve):
            v = nc.vector
            pre = Steps(dve, S["masked"])
            dve.wait_ge(S["mask"], 16)
            pre.run(v.tensor_copy(mask[:, :, :], mask_u8[:, :, :]))
            pre.did(v.tensor_scalar(barred[:, :, :], mask[:, :, :], 1.0, 1e30, ALU.subtract, ALU.mult))
            pre.did(v.tensor_reduce(any_key[:, :], mask[:, :, :], AX.X, ALU.max))
            pre.wait()

            def statistics(own, b):
                dve.wait_ge(S["x_in"], 16 * (b + 1))
                dve.sem_inc(m["passed"]["dve"], 1)
                for t in range(TPB):
                    own.did(v.bn_stats(stats[:, t, :], tile_at(x, b * TPB + t)))
                own.hold()
                for t in range(TPB):
                    own.did(v.bn_aggr(mv[:, t, :], stats[:, t, :]))
                own.wait()
                v.tensor_scalar(var_e[:, :], mv[:, :, 1], EPS, None, ALU.add).then_inc(S["var"], 1)

            def normed(b):
                dve.wait_ge(S["rstd"], b + 1)
                for t in range(TPB):
                    v.tensor_scalar(xn[:, t, :], tile_at(x, b * TPB + t), mv[:, t, 0:1], rstd[:, t:t + 1], ALU.subtract, ALU.mult).then_inc(S["xn"], 1)

            def softmax(own, b):
                dve.wait_ge(S["s"], b + 1)
                s2 = ps[:, 4, 0:TPB * KEYS].rearrange("p (t k) -> p t k", k=KEYS)
                own.run(v.scalar_tensor_tensor(att[:, :, :], s2, D ** -0.5, mask[:, bass.ds(b, 1), :].to_broadcast([P, TPB, KEYS]), ALU.mult, ALU.mult))
                own.run(v.tensor_tensor(att[:, :, :], att[:, :, :], barred[:, bass.ds(b, 1), :].to_broadcast([P, TPB, KEYS]), ALU.add))
                own.run(v.tensor_reduce(top[:, :], att[:, :, :], AX.X, ALU.max))
                v.tensor_tensor(att[:, :, :], att[:, :, :], top[:, :].unsqueeze(2).to_broadcast([P, TPB, KEYS]), ALU.subtract).then_inc(S["shift"], 1)
                dve.wait_ge(S["e"], b + 1)
                own.run(v.tensor_reduce(den[:, :], att[:, :, :], AX.X, ALU.add))
                own.run(v.reciprocal(den[:, :], den[:, :]))
                own.run(v.tensor_scalar(den[:, :], den[:, :], any_key[:, bass.ds(b, 1)], None, ALU.mult))
                v.tensor_tensor(att[:, :, :], att[:, :, :], den[:, :].unsqueeze(2).to_broadcast([P, TPB, KEYS]), ALU.mult).then_inc(S["p"], 1)

            def sequence(b, first, last):
                own = Steps(dve, S["dve"], DVE_FIRST + b * DVE_TURN, m["passed"]["dve"])
                if not first:
                    hold(dve, S["rows_out"], 32 * b, m["passed"]["dve"])
                for t in range(TPB):
                    dve.wait_ge(S["o"], b * TPB + t + 1)
                    v.tensor_tensor(x3[:, t, :], tile_at(x, b * TPB + t), ps[:, 6 + t % 2, :], ALU.add).then_inc(S["x3"], 1)
                    hold(dve, S["x3"], b * TPB + t + 1, m["passed"]["dve"])
                    own.did(v.bn_stats(stats2[:, t, :], x3[:, t, :]))
                own.hold()
                for t in range(TPB):
                    own.did(v.bn_aggr(mv2[:, t, :], stats2[:, t, :]))
                own.wait()
                v.tensor_scalar(var2[:, :], mv2[:, :, 1], EPS, None, ALU.add).then_inc(S["var2"], 1)
                if not last:
                    statistics(own, b + 1)
                dve.wait_ge(S["rstd2"], b + 1)
                for t in range(TPB):
                    v.tensor_scalar(hn[:, t, :], x3[:, t, :], mv2[:, t, 0:1], rstd2[:, t:t + 1], ALU.subtract, ALU.mult).then_inc(S["hn"], 1)
                if not last:
                    normed(b + 1)
                dve.wait_ge(S["logit"], TPB * (b + 1))
                lg = ps[:, 2, 0:TPB * N].rearrange("p (t e) -> p t e", e=N)
                own.run(v.tensor_reduce(top_l[:, :], lg, AX.X, ALU.max))
                v.tensor_tensor(r["logit"][:, :, :], lg, top_l[:, :].unsqueeze(2).to_broadcast([P, TPB, N]), ALU.subtract).then_inc(S["lsh"], 1)
                dve.wait_ge(S["le"], b + 1)
                own.run(v.tensor_reduce(sum_l[:, :], r["logit"][:, :, :], AX.X, ALU.add))
                own.run(v.reciprocal(sum_l[:, :], sum_l[:, :]))
                own.run(v.tensor_tensor(r["prob"][:, :, :], r["logit"][:, :, :], sum_l[:, :].unsqueeze(2).to_broadcast([P, TPB, N]), ALU.mult))
                token = c["token"][:, bass.ds(b * TPB, TPB)]
                choose(nc, own, r, MOE1, token)
                count(nc, own, r, MOE1, c, m["before1"], S["masked"])
                dve.wait_ge(S["ranked"], b + 1)
                find_slots(nc, own, r, MOE1, c, m, m["before1"], 3, c["offset1"])
                if not first:
                    dve.wait_ge(S["scattered"], 16 * SCATTERS * b)
                own.did(v.tensor_copy(send["entry"][:, :, :], r["entry"][:, :, :]))
                own.wait()
                v.tensor_copy(send["slot"][:, :], r["slot_f"][:, :]).then_inc(S["slotted"], 1)
                if not last:
                    softmax(own, b + 1)
                    assert own.n == DVE_TURN, own.n

            own = Steps(dve, S["dve"], 0, m["passed"]["dve"])
            statistics(own, 0)
            normed(0)
            softmax(own, 0)
            assert own.n == DVE_FIRST, own.n
            sequences(dve, sequence)

        @block.tensor
        def _(pe):
            mm, tr = nc.tensor.matmul, nc.tensor.transpose
            ident = c["ident"]
            pe.wait_ge(S["w"], 16)

            def flip(n, j, src):
                since(pe, S["fe"], n - 1)
                for k in range(DC):
                    last = tr(ps[:, j % 2, k * P:(k + 1) * P], src[:, k * P:(k + 1) * P], ident)
                last.then_inc(S["ft"], 1)

            def normed_flips(b):
                for t in range(TPB):
                    pe.wait_ge(S["xn"], b * TPB + t + 1)
                    flip(b * 2 * TPB + t, t, xn[:, t, :])

            def scores(b):
                for t in range(TPB):
                    pe.wait_ge(S["fe"], b * 2 * TPB + t + 1)
                    for k in range(DC):
                        last = mm(ps[:, 4, t * KEYS:(t + 1) * KEYS], xn_t[:, k, t * P:(t + 1) * P],
                                  m["ctx_t"][:, bass.ds(b, 1), k, :].rearrange("p a n -> p (a n)"), start=(k == 0), stop=(k == DC - 1))
                last.then_inc(S["s"], 1)

            def prob_flips(b):
                hold(pe, S["p"], b + 1, m["passed"]["pe"])
                for t in range(TPB):
                    last = tr(ps[0:KEYS, 5, t * P:(t + 1) * P], att[:, t, :], ident)
                last.then_inc(S["pt"], 1)

            def sequence(b, first, last):
                hold(pe, S["pts"], b + 1, m["passed"]["pe"])
                for t in range(TPB):
                    if t >= 2:
                        hold(pe, S["x3"], b * TPB + t - 1, m["passed"]["pe"])
                    mm(ps[:, 6 + t % 2, :], att_t[:, t, :], tile_at(ctx_sb, b)[0:KEYS, :], start=True, stop=True).then_inc(S["o"], 1)

                def hn_flip(t):
                    pe.wait_ge(S["hn"], b * TPB + t + 1)
                    flip(b * 2 * TPB + TPB + t, t, hn[:, t, :])

                hn_flip(0)
                for t in range(TPB):
                    if t + 1 < TPB:
                        hn_flip(t + 1)
                    pe.wait_ge(S["fe"], b * 2 * TPB + TPB + t + 1)
                    for k in range(DC):
                        done = mm(ps[:, 2, t * N:(t + 1) * N], hn_t[:, t % 2, k, :], w_rt[:, k, :], start=(k == 0), stop=(k == DC - 1))
                    done.then_inc(S["logit"], 1)
                if not last:
                    normed_flips(b + 1)
                    scores(b + 1)
                pe.wait_ge(S["masked"], 3 + b + 1)
                places(nc, r, MOE1, c, m, m["before1"], 3).then_inc(S["ranked"], 1)
                if not last:
                    prob_flips(b + 1)

            normed_flips(0)
            scores(0)
            prob_flips(0)
            sequences(pe, sequence)



_INS = ["x", "ctx_2048", "mask_BxS2_bk0", "L0_ffn_ln1_w", "L0_ffn_ln2_w", "L0_ffn_kv_d_w", "L0_ffn_q_d_w", "L0_ffn_k_u_w",
        "L0_ffn_v_u_w", "L0_ffn_q_u_w", "L0_ffn_rope_k_w", "L0_ffn_rope_q_w", "L0_ffn_o_w", "L0_ffn_sh_gate", "L0_ffn_sh_up",
        "L0_ffn_sh_down", "L0_ffn_r_gate", "L0_ffn_r_up", "L0_ffn_r_down", "L0_ffn_router_w", "L0_ffn_router_b",
        "L1_ffn_router_w", "L1_ffn_w_gate", "L1_ffn_w_up", "L1_ffn_w_down"]


def constants():
    import numpy as np

    f = np.float32
    row, col = np.arange(P)[:, None], np.arange(P)[None, :]
    angle = np.outer(np.arange(SEQ, dtype=f), (1.0 / 10000.0 ** (np.arange(0, ROT, 2, dtype=f) / f(ROT))).astype(f)).astype(f)
    cos, sin = np.cos(angle).astype(f), np.sin(angle).astype(f)
    by_tile = lambda t: t.reshape(TPB, P, -1).transpose(1, 0, 2).reshape(P, -1)
    seen = np.arange(KEYS)[None, :] <= np.arange(SEQ - P, SEQ)[:, None] + KEYS - SEQ
    parts = {
        "ident": np.eye(P), "earlier": row < col, "future": np.where(col <= row, 0.0, -1e38),
        "allowed": seen, "barred": np.where(seen, 0.0, -10000.0),
        "cos": by_tile(np.concatenate([cos, cos], 1)), "sin": by_tile(sin),
        "expert": np.tile(np.arange(32), (P, 1)),
        "offset0": np.tile((np.arange(8) + MOE0.first) * TOKENS, (P, 1)),
        "offset1": np.tile(np.arange(32) * TOKENS, (P, 1)),
        "token": row + P * np.arange(TILES)[None, :], "tile": row + P * np.arange(2)[None, :],
    }
    out = {"const": np.concatenate([np.asarray(parts[k], f) for k in CONST], 1), "zero_rows": np.zeros((SPARE, D), f)}
    for moe in (MOE0, MOE1):
        empty = np.zeros((moe.blocks, P, 2), f)
        empty[:, :, 0] = TOKENS + np.arange(P)
        for e in range(moe.first):
            part = empty[e * BLOCKS:(e + 1) * BLOCKS]
            part[:, :, 0] = np.arange(TOKENS).reshape(BLOCKS, P)
            part[:, :, 1] = 1.0
        out[moe.name + "_empty"] = empty.reshape(moe.blocks, 2 * P)
    return out


def kernel(**inputs):
    import numpy as np
    import concourse.bacc as bacc
    from concourse.bass_utils import run_bass_kernel_spmd

    nc = bacc.Bacc("TRN2", target_bir_lowering=False, num_devices=1)
    arrays = {n: np.ascontiguousarray(inputs[n]) for n in _INS}
    arrays["L1_router_t"] = np.ascontiguousarray(arrays.pop("L1_ffn_router_w").T)
    arrays.update(constants())
    aps = {n: nc.dram_tensor(f"in_{n}", v.shape, mybir.dt.from_np(v.dtype), kind="ExternalInput").ap() for n, v in arrays.items()}
    out = nc.dram_tensor("out", (BATCH, SEQ, D), F32, kind="ExternalOutput").ap()
    build(nc, aps, out)
    r = run_bass_kernel_spmd(nc, [{f"in_{n}": v for n, v in arrays.items()}], core_ids=[0])
    return r.results[0]["out"]
```
